# Optimizing a Trainium2 kernel written in Bass

```python
import numpy as np
import jax
import jax.numpy as jnp

def _softmax(x, axis=-1):
    return jax.nn.softmax(x, axis=axis)

def _gelu(x):
    return jax.nn.gelu(x, approximate=True)

def _silu(x):
    return jax.nn.silu(x)

def _sigmoid(x):
    return jax.nn.sigmoid(x)

def _layernorm(x, axis=-1, eps=1e-05):
    m = jnp.mean(x, axis=axis, keepdims=True)
    v = jnp.var(x, axis=axis, keepdims=True)
    return (x - m) / jnp.sqrt(v + eps)

def _scatter_add(tgt, idx, src, axis=0):
    return tgt.at[idx].add(src)

def _segment_sum(src, seg, n):
    return jax.ops.segment_sum(src, seg, n)
kernel_name = 'mk_gnn_resnorm_d1_gnn_r8_07de26'

def setup_inputs(seed: int=0):
    np.random.seed(seed)
    _w = jnp.asarray

    def _rec_inputs():
        import jax
        import jax.numpy as jnp
        _gk = jax.random.key(seed)
        x = -0.0005207 + 1.001 * jax.random.normal(jax.random.fold_in(_gk, 1), (12500, 64), jnp.float32)
        src = jax.random.randint(jax.random.fold_in(_gk, 2), (400000,), 0, 12500, jnp.int32)
        dst = jax.random.randint(jax.random.fold_in(_gk, 3), (400000,), 0, 12500, jnp.int32)
        _o = jnp.argsort(dst, stable=True)
        src = src[_o]
        dst = dst[_o]
        return (x, src, dst)
    x, src, dst = _rec_inputs()

    def _L0_gnn_setup():
        import jax, jax.numpy as jnp
        import numpy as np
        N_NODES = 4096
        DEG = 32
        IN_FEAT = 64
        HIDDEN = 64

        def _mab(x, y, in_w, in_b, out_w, out_b, ff_w, ff_b, y_mask=None):
            d = x.shape[-1]
            q = x @ in_w[:, :d] + in_b[:d]
            k = y @ in_w[:, d:2 * d] + in_b[d:2 * d]
            v = y @ in_w[:, 2 * d:] + in_b[2 * d:]
            s = jnp.einsum('bqd,bkd->bqk', q, k) / jnp.asarray(np.sqrt(d), x.dtype)
            if y_mask is not None:
                s = jnp.where(y_mask[:, None, :], s, -jnp.inf)
            a = jax.nn.softmax(s, axis=-1)
            o = jnp.einsum('bqk,bkd->bqd', a, v) @ out_w + out_b
            h = o + x
            return h + jax.nn.relu(h @ ff_w + ff_b)

        def _forward(x, w_lin, b_lin, enc_in_w, enc_in_b, enc_out_w, enc_out_b, enc_ff_w, enc_ff_b, pma_lin_w, pma_lin_b, pma_seed, pma_in_w, pma_in_b, pma_out_w, pma_out_b, pma_ff_w, pma_ff_b, dec_in_w, dec_in_b, dec_out_w, dec_out_b, dec_ff_w, dec_ff_b, edge_src, edge_dst, max_deg):
            n = x.shape[0]
            d = w_lin.shape[1]
            e = edge_src.shape[0]
            h = x @ w_lin + b_lin
            msg = h[edge_src]
            counts = jax.ops.segment_sum(jnp.ones((e,), jnp.int32), edge_dst, num_segments=n)
            starts = jnp.cumsum(counts) - counts
            pos = jnp.arange(e) - starts[edge_dst]
            dense = jnp.zeros((n, max_deg, d), h.dtype).at[edge_dst, pos].set(msg, mode='drop')
            mask = jnp.zeros((n, max_deg), bool).at[edge_dst, pos].set(True, mode='drop')
            xb = _mab(dense, dense, enc_in_w, enc_in_b, enc_out_w, enc_out_b, enc_ff_w, enc_ff_b, mask)
            xp = jax.nn.relu(xb @ pma_lin_w + pma_lin_b)
            seed = jnp.broadcast_to(pma_seed[None], (n, 1, d))
            p = _mab(seed, xp, pma_in_w, pma_in_b, pma_out_w, pma_out_b, pma_ff_w, pma_ff_b, mask)
            dd = _mab(p, p, dec_in_w, dec_in_b, dec_out_w, dec_out_b, dec_ff_w, dec_ff_b)
            out = jnp.nan_to_num(dd).reshape(n, d)
            return jax.nn.relu(out)
        key = jax.random.key(seed)
        ks = jax.random.split(key, 24)
        d = HIDDEN

        def w(k, shape):
            return jax.random.normal(k, shape, jnp.float32) * 0.05
        return {'x': jax.random.normal(ks[0], (N_NODES, IN_FEAT), jnp.float32), 'w_lin': w(ks[1], (IN_FEAT, d)), 'b_lin': w(ks[2], (d,)), 'enc_in_w': w(ks[3], (d, 3 * d)), 'enc_in_b': w(ks[4], (3 * d,)), 'enc_out_w': w(ks[5], (d, d)), 'enc_out_b': w(ks[6], (d,)), 'enc_ff_w': w(ks[7], (d, d)), 'enc_ff_b': w(ks[8], (d,)), 'pma_lin_w': w(ks[9], (d, d)), 'pma_lin_b': w(ks[10], (d,)), 'pma_seed': w(ks[11], (1, d)), 'pma_in_w': w(ks[12], (d, 3 * d)), 'pma_in_b': w(ks[13], (3 * d,)), 'pma_out_w': w(ks[14], (d, d)), 'pma_out_b': w(ks[15], (d,)), 'pma_ff_w': w(ks[16], (d, d)), 'pma_ff_b': w(ks[17], (d,)), 'dec_in_w': w(ks[18], (d, 3 * d)), 'dec_in_b': w(ks[19], (3 * d,)), 'dec_out_w': w(ks[20], (d, d)), 'dec_out_b': w(ks[21], (d,)), 'dec_ff_w': w(ks[22], (d, d)), 'dec_ff_b': w(ks[23], (d,)), 'edge_src': jax.random.randint(jax.random.fold_in(key, 99), (N_NODES * DEG,), 0, N_NODES), 'edge_dst': jnp.repeat(jnp.arange(N_NODES), DEG), 'max_deg': DEG}
    _L0_gnn_all = _L0_gnn_setup()
    _L0_gnn_in = {k: v for k, v in _L0_gnn_all.items() if k in ('w_lin', 'b_lin', 'enc_in_w', 'enc_in_b', 'enc_out_w', 'enc_out_b', 'enc_ff_w', 'enc_ff_b', 'pma_lin_w', 'pma_lin_b', 'pma_seed', 'pma_in_w', 'pma_in_b', 'pma_out_w', 'pma_out_b', 'pma_ff_w', 'pma_ff_b', 'dec_in_w', 'dec_in_b', 'dec_out_w', 'dec_out_b', 'dec_ff_w', 'dec_ff_b')}
    del _L0_gnn_all
    return {'x': x, 'src': src, 'dst': dst, 'L0_gnn_w_lin': _L0_gnn_in['w_lin'], 'L0_gnn_b_lin': _L0_gnn_in['b_lin'], 'L0_gnn_enc_in_w': _L0_gnn_in['enc_in_w'], 'L0_gnn_enc_in_b': _L0_gnn_in['enc_in_b'], 'L0_gnn_enc_out_w': _L0_gnn_in['enc_out_w'], 'L0_gnn_enc_out_b': _L0_gnn_in['enc_out_b'], 'L0_gnn_enc_ff_w': _L0_gnn_in['enc_ff_w'], 'L0_gnn_enc_ff_b': _L0_gnn_in['enc_ff_b'], 'L0_gnn_pma_lin_w': _L0_gnn_in['pma_lin_w'], 'L0_gnn_pma_lin_b': _L0_gnn_in['pma_lin_b'], 'L0_gnn_pma_seed': _L0_gnn_in['pma_seed'], 'L0_gnn_pma_in_w': _L0_gnn_in['pma_in_w'], 'L0_gnn_pma_in_b': _L0_gnn_in['pma_in_b'], 'L0_gnn_pma_out_w': _L0_gnn_in['pma_out_w'], 'L0_gnn_pma_out_b': _L0_gnn_in['pma_out_b'], 'L0_gnn_pma_ff_w': _L0_gnn_in['pma_ff_w'], 'L0_gnn_pma_ff_b': _L0_gnn_in['pma_ff_b'], 'L0_gnn_dec_in_w': _L0_gnn_in['dec_in_w'], 'L0_gnn_dec_in_b': _L0_gnn_in['dec_in_b'], 'L0_gnn_dec_out_w': _L0_gnn_in['dec_out_w'], 'L0_gnn_dec_out_b': _L0_gnn_in['dec_out_b'], 'L0_gnn_dec_ff_w': _L0_gnn_in['dec_ff_w'], 'L0_gnn_dec_ff_b': _L0_gnn_in['dec_ff_b']}

def reference(x, src, dst, L0_gnn_w_lin, L0_gnn_b_lin, L0_gnn_enc_in_w, L0_gnn_enc_in_b, L0_gnn_enc_out_w, L0_gnn_enc_out_b, L0_gnn_enc_ff_w, L0_gnn_enc_ff_b, L0_gnn_pma_lin_w, L0_gnn_pma_lin_b, L0_gnn_pma_seed, L0_gnn_pma_in_w, L0_gnn_pma_in_b, L0_gnn_pma_out_w, L0_gnn_pma_out_b, L0_gnn_pma_ff_w, L0_gnn_pma_ff_b, L0_gnn_dec_in_w, L0_gnn_dec_in_b, L0_gnn_dec_out_w, L0_gnn_dec_out_b, L0_gnn_dec_ff_w, L0_gnn_dec_ff_b):
    import jax
    import jax.numpy as jnp

    def _L0_gnn_ref(x, w_lin, b_lin, enc_in_w, enc_in_b, enc_out_w, enc_out_b, enc_ff_w, enc_ff_b, pma_lin_w, pma_lin_b, pma_seed, pma_in_w, pma_in_b, pma_out_w, pma_out_b, pma_ff_w, pma_ff_b, dec_in_w, dec_in_b, dec_out_w, dec_out_b, dec_ff_w, dec_ff_b, edge_src, edge_dst, max_deg):
        import jax, jax.numpy as jnp
        import numpy as np
        N_NODES = 4096
        DEG = 32
        IN_FEAT = 64
        HIDDEN = 64

        def _mab(x, y, in_w, in_b, out_w, out_b, ff_w, ff_b, y_mask=None):
            d = x.shape[-1]
            q = x @ in_w[:, :d] + in_b[:d]
            k = y @ in_w[:, d:2 * d] + in_b[d:2 * d]
            v = y @ in_w[:, 2 * d:] + in_b[2 * d:]
            s = jnp.einsum('bqd,bkd->bqk', q, k) / jnp.asarray(np.sqrt(d), x.dtype)
            if y_mask is not None:
                s = jnp.where(y_mask[:, None, :], s, -jnp.inf)
            a = jax.nn.softmax(s, axis=-1)
            o = jnp.einsum('bqk,bkd->bqd', a, v) @ out_w + out_b
            h = o + x
            return h + jax.nn.relu(h @ ff_w + ff_b)

        def _forward(x, w_lin, b_lin, enc_in_w, enc_in_b, enc_out_w, enc_out_b, enc_ff_w, enc_ff_b, pma_lin_w, pma_lin_b, pma_seed, pma_in_w, pma_in_b, pma_out_w, pma_out_b, pma_ff_w, pma_ff_b, dec_in_w, dec_in_b, dec_out_w, dec_out_b, dec_ff_w, dec_ff_b, edge_src, edge_dst, max_deg):
            n = x.shape[0]
            d = w_lin.shape[1]
            e = edge_src.shape[0]
            h = x @ w_lin + b_lin
            msg = h[edge_src]
            counts = jax.ops.segment_sum(jnp.ones((e,), jnp.int32), edge_dst, num_segments=n)
            starts = jnp.cumsum(counts) - counts
            pos = jnp.arange(e) - starts[edge_dst]
            dense = jnp.zeros((n, max_deg, d), h.dtype).at[edge_dst, pos].set(msg, mode='drop')
            mask = jnp.zeros((n, max_deg), bool).at[edge_dst, pos].set(True, mode='drop')
            xb = _mab(dense, dense, enc_in_w, enc_in_b, enc_out_w, enc_out_b, enc_ff_w, enc_ff_b, mask)
            xp = jax.nn.relu(xb @ pma_lin_w + pma_lin_b)
            seed = jnp.broadcast_to(pma_seed[None], (n, 1, d))
            p = _mab(seed, xp, pma_in_w, pma_in_b, pma_out_w, pma_out_b, pma_ff_w, pma_ff_b, mask)
            dd = _mab(p, p, dec_in_w, dec_in_b, dec_out_w, dec_out_b, dec_ff_w, dec_ff_b)
            out = jnp.nan_to_num(dd).reshape(n, d)
            return jax.nn.relu(out)
        return _forward(x, w_lin, b_lin, enc_in_w, enc_in_b, enc_out_w, enc_out_b, enc_ff_w, enc_ff_b, pma_lin_w, pma_lin_b, pma_seed, pma_in_w, pma_in_b, pma_out_w, pma_out_b, pma_ff_w, pma_ff_b, dec_in_w, dec_in_b, dec_out_w, dec_out_b, dec_ff_w, dec_ff_b, edge_src, edge_dst, max_deg)
    x = _layernorm(x + _L0_gnn_ref(x, L0_gnn_w_lin, L0_gnn_b_lin, L0_gnn_enc_in_w, L0_gnn_enc_in_b, L0_gnn_enc_out_w, L0_gnn_enc_out_b, L0_gnn_enc_ff_w, L0_gnn_enc_ff_b, L0_gnn_pma_lin_w, L0_gnn_pma_lin_b, L0_gnn_pma_seed, L0_gnn_pma_in_w, L0_gnn_pma_in_b, L0_gnn_pma_out_w, L0_gnn_pma_out_b, L0_gnn_pma_ff_w, L0_gnn_pma_ff_b, L0_gnn_dec_in_w, L0_gnn_dec_in_b, L0_gnn_dec_out_w, L0_gnn_dec_out_b, L0_gnn_dec_ff_w, L0_gnn_dec_ff_b, src, dst, 32), axis=-1)
    return x

_drawn_inputs = setup_inputs


def setup_inputs(seed=0):
    import zlib

    import numpy as np

    out = dict(_drawn_inputs(seed))
    spreads = {}
    factors = {'L0_gnn_w_lin': 8.0,
     'L0_gnn_b_lin': 8.0,
     'L0_gnn_enc_in_w': 8.0,
     'L0_gnn_enc_in_b': 8.0,
     'L0_gnn_enc_out_w': 8.0,
     'L0_gnn_enc_out_b': 8.0,
     'L0_gnn_enc_ff_w': 8.0,
     'L0_gnn_enc_ff_b': 21.806,
     'L0_gnn_pma_lin_w': 8.0,
     'L0_gnn_pma_lin_b': 61.632,
     'L0_gnn_pma_in_w': 5.657,
     'L0_gnn_pma_in_b': 3.52,
     'L0_gnn_pma_out_w': 3.57,
     'L0_gnn_pma_ff_w': 3.447,
     'L0_gnn_dec_in_w': 5.627,
     'L0_gnn_dec_in_b': 29.216,
     'L0_gnn_dec_out_w': 3.209,
     'L0_gnn_dec_ff_w': 3.044,
     'L0_gnn_pma_out_b': 8.0,
     'L0_gnn_pma_ff_b': 8.0,
     'L0_gnn_dec_out_b': 8.0,
     'L0_gnn_dec_ff_b': 8.0}
    for name, (base, spread) in spreads.items():
        noise = np.random.default_rng([zlib.crc32(name.encode()), seed]).standard_normal(out[name].shape)
        drawn = base * np.exp(spread * noise) if base else spread * noise
        out[name] = jnp.asarray(drawn.astype(out[name].dtype))
    for name, factor in factors.items():
        out[name] = (out[name] * factor).astype(out[name].dtype)
    return out
```

```python
from contextlib import ExitStack

import concourse.bass as bass
from concourse import mybir

ALU = mybir.AluOpType
ACT = mybir.ActivationFunctionType
F32 = mybir.dt.float32
I32 = mybir.dt.int32
BF16 = mybir.dt.bfloat16
AX_X = mybir.AxisListType.X

P = 128
D = 64
DEG = 32
QUADS = P // DEG
OCT = 8
PAIRS = OCT // 2
OCTS_PER_IT = P // (QUADS * OCT)
TILES_PER_IT = OCT * OCTS_PER_IT
RING = 8
ROW = 4 * D
MASKED = -3.0e38
FLT_MAX = 3.4028234663852886e38
EPS = 1e-5

SAMPLES = 625
HALF = 7
CHUNK = 7

L_SCORES = 1
L_MASK = 2
L_SOFTMAX = 3
L_NORM = 4
L_ATTEND = 5
L_FF = 6
L_PMA = 7
L_BACK = 8
L_MASK2 = 11
L_SEED = 12
L_SEED_T = 13
L_WEIGHTS = 14
L_POOL = 15
L_DEC1 = 16
L_DEC2 = 17
L_OUT = 18
L_Y = 19


class Step:

    def __init__(self, group, at, octets):
        self.group, self.at, self.looped, self.octets = group, at, not isinstance(group, int), octets

    def octet(self, lag):
        return self.group * 8 + (self.at - lag)

    def batch(self, lag):
        return self.group * 4 + (self.at - lag) // 2

    def iteration(self, lag):
        return self.group * 2 + (self.at - lag) // 4

    def round(self, lag):
        return self.group + (self.at - lag) // RING

    def slot(self, lag, n):
        return (self.at - lag) % n

    def has(self, lag):
        return self.looped or 0 <= self.at - lag < self.octets

    def has_batch(self, lag):
        return (self.at - lag) % 2 == 0 and (self.looped or 0 <= self.at - lag < self.octets)

    def has_iteration(self, lag):
        return (self.at - lag) % 4 == 0 and (self.looped or 0 <= self.at - lag < self.octets)


def wait(eng, sem, count):
    if isinstance(count, int) and count <= 0:
        return
    eng.wait_ge(sem, count)


def wait_apart(eng, sem, count, passed):
    if isinstance(count, int) and count <= 0:
        return
    eng.wait_ge(sem, count)
    if not isinstance(count, int):
        eng.sem_inc(passed, 1)


def gnn_kernel(nc, a, out):
    x, src, dst = a["x"], a["src"], a["dst"]
    w = {k[len("L0_gnn_"):]: v for k, v in a.items() if k.startswith("L0_gnn_")}
    N, E = x.shape[0], src.shape[0]
    ITS = -(-N // P)
    NPAD = ITS * P
    LAST = N - (ITS - 1) * P
    OCTETS = ITS * OCTS_PER_IT
    WINDOW = E // SAMPLES
    CHUNKS = ITS // CHUNK
    BLOCK = E // 125
    assert x.shape[1] == D and SAMPLES * WINDOW == E and ITS % (2 * HALF) == 0 and ITS % (2 * CHUNK) == 0
    assert BLOCK % WINDOW == 0 and 125 * BLOCK == E
    PER_ROW = BLOCK // WINDOW

    LOOP_FROM = L_Y + 1
    GROUPS = (OCTETS - LOOP_FROM) // RING
    LOOP_TO = LOOP_FROM + RING * GROUPS
    END = OCTETS + L_Y

    with ExitStack() as ctx:
        def sb(name, shape, dt=F32):
            return ctx.enter_context(nc.sbuf_tensor(name, shape, dt))

        def sem(name):
            return ctx.enter_context(nc.semaphore(name))

        table = nc.dram_tensor("node_table", (NPAD, ROW), F32).ap()
        dst_rows = nc.dram_tensor("dst_rows", (SAMPLES, WINDOW), F32).ap()
        dst_samples = nc.dram_tensor("dst_samples", (1, SAMPLES), F32).ap()
        src_padded = nc.dram_tensor("src_padded", (E + D, 1), I32).ap()

        gathered = sb("gathered", [P, RING, OCT * ROW])
        probs_diag = sb("probs_diag", [P, 2, 2 * OCT, P])
        qT = sb("qT", [P, 2, 512])
        kT = sb("kT", [P, 2, 512])
        hT = sb("hT", [P, RING, 512])
        h2 = sb("h2", [P, 2, 512])
        xb = sb("xb", [P, 2, 512])
        xp = sb("xp", [P, 2, 512])
        xp_rows = sb("xp_rows", [P, RING, 512])
        empty = sb("empty", [P, 512])
        scores = sb("scores", [P, 512])
        probs = sb("probs", [P, 2, 512])
        top = sb("top", [P, 16])
        total = sb("total", [P, 16])
        share = sb("share", [P, 16])
        idx = sb("idx", [P, RING, OCT], I32)
        idx_all = sb("idx_all", [P, (ITS + 2) * DEG], I32)
        count_slot = sb("count_slot", [P, ITS * DEG], BF16)
        rows = sb("rows", [P, ITS, D])
        count_seed = sb("count_seed", [P, ITS, QUADS])
        empty2 = sb("empty2", [P, P])
        scores2 = sb("scores2", [P, P])
        top2 = sb("top2", [P, QUADS])
        total2 = sb("total2", [P, QUADS])
        share2 = sb("share2", [P, QUADS])
        weights2 = sb("weights2", [P, OCTS_PER_IT, OCT, QUADS])
        pool_part = sb("pool_part", [P, 512])
        pooled = sb("pooled", [P, D])
        pooledT = sb("pooledT", [D, P])
        hid1 = sb("hid1", [D, P])
        pvec = sb("pvec", [D, P])
        hid2 = sb("hid2", [D, P])
        dec = sb("dec", [D, P])
        decr = sb("decr", [D, P])
        stats = sb("stats", [P, ITS, 6])
        nonempty = sb("nonempty", [P, ITS])
        lnv = sb("lnv", [P, 5, ITS])

        ident = sb("ident", [P, P])
        shift = scores[:, P:3 * P].rearrange("p (a b) -> p a b", a=2)
        seed_perm = empty[:, :].rearrange("p (a b) -> p a b", a=QUADS)
        pool_perm = scores[:, 0:P]
        quad_of = sb("quad_of", [P, QUADS])
        tile_of = sb("tile_of", [P, OCT])
        iota_j = sb("iota_j", [P, DEG])
        iota_ji = sb("iota_ji", [P, DEG], I32)
        node_i = sb("node_i", [P, ITS], I32)
        node_f = sb("node_f", [P, ITS])
        eps = sb("eps", [P, 1])
        wtab = sb("wtab", [D + 1, ROW])
        wlin = sb("wlin", [D, D])
        ff_diag = sb("ff_diag", [P, P])
        pma_diag = sb("pma_diag", [P, P])
        seed_u = sb("seed_u", [P, 38])
        mats = {n: sb(n, [D, D]) for n in ("enc_out", "p_out", "p_ff", "d_out", "d_ff", "wvo2", "wvo3")}
        borrowed = probs_diag[:, :, :, :].rearrange("p b t n -> p (b t n)")
        wraw = borrowed[0:D + 1, 0:3 * D]
        p_in = borrowed[0:D, 3 * D:6 * D]
        d_in = borrowed[0:D, 6 * D:9 * D]
        tmpT = borrowed[0:D, 9 * D:10 * D + 1]
        wkT2 = borrowed[0:D, 11 * D:13 * D].rearrange("p (a b) -> p a b", a=2)
        out_b = borrowed[D:D + 1, 15 * D:16 * D]
        wide = borrowed[0:D, 13 * D:15 * D]
        cols = sb("cols", [P, 24])
        COLS = ["b_lin", "ff_b", "pma_b", "seed", "bq2", "bk2", "bv2", "bo2", "bff2", "bv3", "bo3", "bff3",
                "qs", "b1", "b3", "c2"]
        col = {n: i for i, n in enumerate(COLS)}

        def c_(n, rows_=D):
            return cols[0:rows_, col[n]:col[n] + 1]

        junk = probs[:, :, :].rearrange("p s n -> p (s n)")
        count1, row_f, below = (pool_part[:, i * ITS:(i + 1) * ITS] for i in range(3))
        row_i = sb("row_i", [P, ITS + 2 * HALF], I32)
        counts_b = sb("counts_b", [P, ITS], BF16)
        starts = sb("starts", [P, ITS + 1])
        start_i = sb("start_i", [P, ITS + 2 * HALF], I32)
        sample_own = sb("sample_own", [125, PER_ROW])
        counts = sb("counts", [P, ITS])
        win_idx = sb("win_idx", [P, 2, HALF], I32)
        sidx = sb("sidx", [P, 2, HALF], I32)

        flat = gathered[:, :, :].rearrange("p s n -> p (s n)")
        windows = flat[:, 0:2 * HALF * WINDOW].rearrange("p (h t n) -> p h t n", h=2, t=HALF)
        at = 2 * HALF * WINDOW
        dst_i = flat[0:125, at:at + BLOCK].bitcast(I32)
        dst_f = flat[0:125, at + BLOCK:at + 2 * BLOCK]
        hflat = hT[:, :, :].rearrange("p s n -> p (s n)")
        trow = hflat[:, 0:2 * CHUNK * ROW].rearrange("p (b n) -> p b n", b=2)
        xflat = xp_rows[:, :, :].rearrange("p s n -> p (s n)")
        src_all = xflat[:, 0:ITS * DEG].bitcast(I32)
        src_win = xflat[:, ITS * DEG:ITS * DEG + 2 * HALF * DEG].bitcast(I32).rearrange(
            "p (h t n) -> p h t n", h=2, t=HALF)
        xin = qT[:, :, :].rearrange("p s n -> p (s n)")[:, 0:2 * CHUNK * D].rearrange(
            "p (b t n) -> p b t n", b=2, t=CHUNK)
        xinT = kT[:, :, :].rearrange("p s n -> p (s n)")[0:D, 0:CHUNK * P]
        nodeT = h2[:, :, :].rearrange("p s n -> p (s n)")[0:D + 1, 0:CHUNK * P]
        sample_f = xb[:, :, :].rearrange("p s n -> p (s n)")[:, 0:SAMPLES]

        ps = ctx.enter_context(nc.psum_tensor("ps", [P, 8, 512], F32))
        B_QH, B_KX, B_S, B_AV, B_FF, B_POOL, B_SEED = 0, 1, 2, 4, 5, 6, 7
        ps_scores = ps[:, B_S:B_S + 2, :].rearrange("p h n -> p (h n)").rearrange("p (h n) -> p h n", h=2)[:, :, 0:256]
        ps_seed = ps[:, B_SEED, 0:P]
        ps_seedT = ps[:, B_POOL, P:2 * P]
        ps_fin = ps[:, B_POOL, 2 * P:3 * P]
        psf = ps[:, :, :].rearrange("p b n -> p (b n)")
        ps_xT = psf[0:D, 0:CHUNK * P]
        ps_node = psf[0:D, 1024:1024 + CHUNK * P]
        ps_row = psf[:, 2048:2048 + CHUNK * ROW]

        w_in = sem("w_in")
        dst_in = sem("dst_in")
        dst_cast = sem("dst_cast")
        dst_out = sem("dst_out")
        samples_in = sem("samples_in")
        pad_out = sem("pad_out")
        x_in = [sem("x_in0"), sem("x_in1")]
        tab_out = [sem("tab_out0"), sem("tab_out1")]
        x_tail = sem("x_tail")
        rows_in = sem("rows_in")
        out_done = sem("out_done")
        pool_cst = sem("pool_cst")
        pool_zero = sem("pool_zero")
        dve_zero = sem("dve_zero")
        dve_chain = sem("dve_chain")
        prep = sem("prep")
        prep_pe = sem("prep_pe")
        nodes_f = sem("nodes_f")
        t_xT = sem("t_xT")
        t_xTc = sem("t_xTc")
        t_node = sem("t_node")
        t_nodec = sem("t_nodec")
        t_row = sem("t_row")
        t_rowc = sem("t_rowc")
        sampled = sem("sampled")
        win_in = [sem("win_in0"), sem("win_in1")]
        win_idx_ready = sem("win_idx_ready")
        searched = sem("searched")
        swin_in = [sem("swin_in0"), sem("swin_in1")]
        sidx_ready = sem("sidx_ready")
        src_copied = sem("src_copied")
        shifted = sem("shifted")
        permuted = sem("permuted")
        counted = sem("counted")

        g_in = [sem(f"g_in{i}") for i in range(RING)]
        idx_ready = sem("idx_ready")
        q_ps, k_ps, h_ps = sem("q_ps"), sem("k_ps"), sem("h_ps")
        q_sb, k_sb, h_sb = sem("q_sb"), sem("k_sb"), sem("h_sb")
        s_ps = sem("s_ps")
        mask_ok, s_sb, s_top, s_diff = sem("mask_ok"), sem("s_sb"), sem("s_top"), sem("s_diff")
        p_exp, p_sum, p_share, p_norm, p_diag = sem("p_exp"), sem("p_sum"), sem("p_share"), sem("p_norm"), sem("p_diag")
        av_ps, h2_sb, ff_ps, xb_sb, pma_ps, xp_sb = (sem("av_ps"), sem("h2_sb"), sem("ff_ps"), sem("xb_sb"),
                                                     sem("pma_ps"), sem("xp_sb"))
        back_ps, back_sb, seed_ps = sem("back_ps"), sem("back_sb"), sem("seed_ps")
        m2_cmp, m2_ok, s2_sb, s2_top, s2_diff = (sem("m2_cmp"), sem("m2_ok"), sem("s2_sb"), sem("s2_top"),
                                                 sem("s2_diff"))
        p2_exp, p2_sum, p2_share, p2_norm = sem("p2_exp"), sem("p2_sum"), sem("p2_share"), sem("p2_norm")
        seedT_ps, weights2_ok, pool_ps, pool_own, pooled_ok = (sem("seedT_ps"), sem("weights2_ok"), sem("pool_ps"),
                                                               sem("pool_own"), sem("pooled_ok"))
        fin_ps = sem("fin_ps")
        pooledT_ok, hid1_ok, pvec_ok, hid2_ok, dec_ok, decr_ok = (
            sem("pooledT_ok"), sem("hid1_ok"), sem("pvec_ok"), sem("hid2_ok"), sem("dec_ok"), sem("decr_ok"))
        y_ok, stats_ok = sem("y_ok"), sem("stats_ok")
        pe_passed, pool_passed = sem("pe_passed"), sem("pool_passed")
        ln_ok = sem("ln_ok")
        ln_std = sem("ln_std")
        normed = sem("normed")

        block = ctx.enter_context(nc.Block())

        def steps(eng, body):
            for t in range(LOOP_FROM):
                body(Step(0, t, OCTETS))
            with eng.Fori(0, GROUPS) as group:
                for k in range(RING):
                    body(Step(group, LOOP_FROM + k, OCTETS))
            for t in range(LOOP_TO, END + 1):
                body(Step(0, t, OCTETS))

        WEIGHT_LOADS = []

        def vec(name, lo=0, hi=D):
            return w[name][lo:hi].rearrange("(n o) -> n o", o=1)

        def load(dst_ap, src_ap):
            WEIGHT_LOADS.append((dst_ap, src_ap))

        load(wraw[0:D, :], w["enc_in_w"])
        load(wraw[D:D + 1, :], w["enc_in_b"].rearrange("(o n) -> o n", o=1))
        load(out_b, w["enc_out_b"].rearrange("(o n) -> o n", o=1))
        load(wlin[:, :], w["w_lin"])
        load(mats["enc_out"][:, :], w["enc_out_w"])
        load(p_in[:, :], w["pma_in_w"])
        load(d_in[:, :], w["dec_in_w"])
        load(mats["p_out"][:, :], w["pma_out_w"])
        load(mats["p_ff"][:, :], w["pma_ff_w"])
        load(mats["d_out"][:, :], w["dec_out_w"])
        load(mats["d_ff"][:, :], w["dec_ff_w"])
        load(c_("b_lin"), vec("b_lin"))
        load(c_("ff_b"), vec("enc_ff_b"))
        load(cols[D:P, col["ff_b"]:col["ff_b"] + 1], vec("enc_ff_b"))
        load(c_("pma_b"), vec("pma_lin_b"))
        load(cols[D:P, col["pma_b"]:col["pma_b"] + 1], vec("pma_lin_b"))
        load(c_("seed"), w["pma_seed"].rearrange("o n -> n o"))
        load(c_("bq2"), vec("pma_in_b"))
        load(c_("bk2"), vec("pma_in_b", D, 2 * D))
        load(c_("bv2"), vec("pma_in_b", 2 * D, 3 * D))
        load(c_("bo2"), vec("pma_out_b"))
        load(c_("bff2"), vec("pma_ff_b"))
        load(c_("bv3"), vec("dec_in_b", 2 * D, 3 * D))
        load(c_("bo3"), vec("dec_out_b"))
        load(c_("bff3"), vec("dec_ff_b"))
        DIAG_LOADS = [(ff_diag[0:D, 0:D], w["enc_ff_w"]), (ff_diag[D:P, D:P], w["enc_ff_w"]),
                      (pma_diag[0:D, 0:D], w["pma_lin_w"]), (pma_diag[D:P, D:P], w["pma_lin_w"])]
        ALL_WEIGHTS = 16 * (len(WEIGHT_LOADS) + len(DIAG_LOADS))

        @block.sync
        def _(sp):
            sp.dma_start(dst_i, dst.rearrange("(p n) -> p n", p=125)).then_inc(dst_in, 16)
            sp.dma_start(src_padded[0:E, :].rearrange("(p n) o -> p (n o)", p=P), src.rearrange("(p n) -> p n", p=P)
                         ).then_inc(pad_out, 16)
            sp.dma_start(src_padded[E:E + D, :].rearrange("n o -> o n"), src[0:D].rearrange("(o n) -> o n", o=1)
                         ).then_inc(pad_out, 16)
            for d_, s_ in WEIGHT_LOADS:
                sp.dma_start(d_, s_).then_inc(w_in, 16)
            sp.wait_ge(dst_cast, 2)
            sp.dma_start(dst_samples.rearrange("o (p n) -> (o p) n", p=125), sample_own[:, :]
                         ).then_inc(dst_out, 16)
            sp.wait_ge(dst_out, 16)
            sp.dma_start(sample_f, dst_samples.broadcast_to((P, SAMPLES))).then_inc(samples_in, 16)
            sp.dma_start(dst_rows.rearrange("(p n) m -> p (n m)", p=125), dst_f).then_inc(dst_out, 16)
            sp.wait_ge(dve_zero, 1)
            for d_, s_ in DIAG_LOADS:
                sp.dma_start(d_, s_).then_inc(w_in, 16)

            def load_chunk(c, b):
                sp.dma_start(xin[:, b], x[bass.ds(c * (CHUNK * P), CHUNK * P), :].rearrange(
                    "(t p) d -> p t d", p=P)).then_inc(x_in[b], 16)

            def store_chunk(c, b):
                sp.dma_start(table[bass.ds(c * (CHUNK * P), CHUNK * P), :].rearrange("(t p) n -> p t n", p=P),
                             trow[:, b].rearrange("p (t n) -> p t n", t=CHUNK)).then_inc(tab_out[b], 16)

            load_chunk(0, 0)
            load_chunk(1, 1)
            with sp.Fori(0, CHUNKS // 2 - 2) as g:
                for b in range(2):
                    sp.wait_ge(t_rowc, g * 2 + (b + 1))
                    store_chunk(g * 2 + b, b)
                    load_chunk(g * 2 + (b + 2), b)
            sp.wait_ge(t_rowc, CHUNKS - 3)
            store_chunk(CHUNKS - 4, 0)
            load_chunk(CHUNKS - 2, 0)
            sp.wait_ge(t_rowc, CHUNKS - 2)
            store_chunk(CHUNKS - 3, 1)
            base = (CHUNKS - 1) * CHUNK * P
            sp.dma_start(xin[0:LAST, 1, CHUNK - 1], x[N - LAST:N, :]).then_inc(x_tail, 16)
            sp.wait_ge(x_tail, 16)
            sp.dma_start(xin[:, 1, 0:CHUNK - 1], x[base:N - LAST, :].rearrange("(t p) d -> p t d", p=P)
                         ).then_inc(x_in[1], 16)
            for b in range(2):
                sp.wait_ge(t_rowc, CHUNKS - 1 + b)
                store_chunk(CHUNKS - 2 + b, b)
            sp.wait_ge(dve_zero, 2)
            for q in range(QUADS):
                sp.dma_start(rows[q::QUADS, 0:ITS - 1, :],
                             x[0:(ITS - 1) * P, :].rearrange("(m a b) d -> a b m d", a=QUADS, b=DEG)[q]
                             ).then_inc(rows_in, 16)
                n = min(max(LAST - q * DEG, 0), DEG)
                if n:
                    base = (ITS - 1) * P + q * DEG
                    sp.dma_start(rows[q:q + QUADS * (n - 1) + 1:QUADS, ITS - 1, :], x[base:base + n, :]
                                 ).then_inc(rows_in, 16)

            stores = 0
            for g in range(ITS // 14):
                sp.wait_ge(normed, g + 1)
                lo, hi = 14 * g, min(14 * (g + 1), ITS - 1)
                for q in range(QUADS):
                    sp.dma_start(out[lo * P:hi * P, :].rearrange("(m a b) d -> a b m d", a=QUADS, b=DEG)[q],
                                 rows[q::QUADS, lo:hi, :]).then_inc(out_done, 16)
                    stores += 1
                    n = min(max(LAST - q * DEG, 0), DEG)
                    if hi == ITS - 1 and n:
                        base = (ITS - 1) * P + q * DEG
                        sp.dma_start(out[base:base + n, :], rows[q:q + QUADS * (n - 1) + 1:QUADS, ITS - 1, :]
                                     ).then_inc(out_done, 16)
                        stores += 1
            sp.wait_ge(out_done, 16 * stores)

        ROWS_LOADED = 16 * (QUADS + sum(1 for q in range(QUADS) if LAST > q * DEG))

        @block.gpsimd
        def _(pool):
            nc.gpsimd.iota(node_i[:, :], [[P, ITS]], 0, 1).then_inc(pool_cst, 1)
            nc.gpsimd.iota(iota_ji[:, :], [[1, DEG]], 0, 0).then_inc(pool_cst, 1)
            for t in (ident[:, :], shift, seed_perm, pool_perm):
                nc.gpsimd.memset(t, 0.0).then_inc(pool_zero, 1)
            pool.wait_ge(pool_zero, 4)

            def one_where_zero(view, pattern, base, mult=1):
                nc.gpsimd.affine_select(out=view, in_=view, compare_op=ALU.not_equal, fill=1.0, base=base,
                                        pattern=pattern, channel_multiplier=mult).then_inc(pool_cst, 1)

            one_where_zero(ident[:, :], [[-1, P]], 0)
            one_where_zero(shift[:, 0, :], [[-1, P]], -1)
            one_where_zero(shift[:, 1, :], [[1, P]], -(P - 1), P)
            for q in range(QUADS):
                one_where_zero(seed_perm[:, q, :].rearrange("p (c r) -> p c r", c=QUADS)[:, :, 0:OCT],
                               [[-OCT, QUADS], [-1, OCT]], -DEG * q)
                one_where_zero(pool_perm.rearrange("p (b a) -> p a b", a=QUADS)[:, q, :],
                               [[-1, DEG]], -DEG * q)
            def gather_windows(table_ap, size, index, ready, target, landed):
                with pool.Fori(0, ITS // (2 * HALF)) as g:
                    for h in range(2):
                        wait_apart(pool, ready, g * 2 + (h + 1), pool_passed)
                        for t in range(HALF):
                            pool.indirect_dma_start(
                                out=target[:, h, t, 0:size], out_offset=None, in_=table_ap,
                                in_offset=bass.IndirectOffsetOnAxis(ap=index[:, h, t:t + 1], axis=0),
                            ).then_inc(landed[h], 16)

            pool.wait_ge(dst_out, 32)
            gather_windows(dst_rows, WINDOW, win_idx, win_idx_ready, windows, win_in)
            pool.wait_ge(pad_out, 32)
            gather_windows(src_padded, DEG, sidx, sidx_ready, src_win, swin_in)

            pool.wait_ge(idx_ready, RING)
            pool.wait_ge(tab_out[0], 16 * (CHUNKS // 2))
            pool.wait_ge(tab_out[1], 16 * (CHUNKS // 2))

            def step(s):
                if not s.has(0):
                    return
                wait_apart(pool, av_ps, s.octet(RING - 1), pool_passed)
                wait_apart(pool, idx_ready, s.octet(-1), pool_passed)
                for t in range(OCT):
                    pool.indirect_dma_start(
                        out=gathered[:, s.slot(0, RING), t * ROW:(t + 1) * ROW], out_offset=None, in_=table,
                        in_offset=bass.IndirectOffsetOnAxis(ap=idx[:, s.slot(0, RING), t:t + 1], axis=0),
                    ).then_inc(g_in[s.slot(0, RING)], 16)

            steps(pool, step)

        @block.tensor
        def _(pe):
            pe.wait_ge(w_in, ALL_WEIGHTS)
            pe.wait_ge(prep, 1)
            pe.transpose(ps[0:D, 0, 0:D + 1], wraw[:, 2 * D:3 * D], ident[0:D + 1, 0:D + 1]).then_inc(prep_pe, 1)
            pe.wait_ge(prep, 2)
            pe.matmul(ps[0:D + 1, 1, 0:D], tmpT[:, :], mats["enc_out"][:, :], start=True, stop=True
                      ).then_inc(prep_pe, 1)
            pe.transpose(ps[0:D, 2, 0:D], p_in[:, D:2 * D], ident[0:D, 0:D]).then_inc(prep_pe, 1)
            pe.matmul(ps[0:D, 3, 0:1], p_in[:, 0:D], c_("seed"), start=True, stop=True).then_inc(prep_pe, 1)
            pe.wait_ge(prep, 6)
            pe.matmul(ps[:, 4, 0:1], wkT2[:, :, :].rearrange("p a b -> p (a b)"), c_("qs"), start=True, stop=True
                      ).then_inc(prep_pe, 1)
            pe.matmul(ps[:, 5, 0:1], wide[:, :], c_("bk2"), start=True, stop=True).then_inc(prep_pe, 1)
            pe.transpose(ps[0:D, 0, 0:D], p_in[:, 2 * D:3 * D], ident[0:D, 0:D]).then_inc(prep_pe, 1)
            pe.transpose(ps[0:D, 1, 0:D], d_in[:, 2 * D:3 * D], ident[0:D, 0:D]).then_inc(prep_pe, 1)
            pe.matmul(ps[0:D, 2, 0:1], mats["p_out"][:, :], c_("bv2"), start=True, stop=True).then_inc(prep_pe, 1)
            pe.matmul(ps[0:D, 3, 0:1], mats["d_out"][:, :], c_("bv3"), start=True, stop=True).then_inc(prep_pe, 1)
            pe.wait_ge(prep, 7)
            pe.matmul(ps[0:D, 6, 0:D], wide[:, 0:D], mats["p_out"][:, :], start=True, stop=True).then_inc(prep_pe, 1)
            pe.matmul(ps[0:D, 7, 0:D], wide[:, D:2 * D], mats["d_out"][:, :], start=True, stop=True
                      ).then_inc(prep_pe, 1)
            pe.wait_ge(prep, 8)

            with pe.Fori(0, CHUNKS // 2) as g:
                for b in range(2):
                    n = g * 2 + (b + 1)
                    wait_apart(pe, x_in[b], g * 16 + 16, pe_passed)
                    for t in range(CHUNK):
                        mm = pe.transpose(ps_xT[:, t * P:(t + 1) * P], xin[:, b, t, :], ident[:, :])
                    mm.then_inc(t_xT, 1)
                    wait_apart(pe, t_xTc, n, pe_passed)
                    pe.matmul(ps_node[:, 0:512], wlin[:, :], xinT[:, 0:512], start=True, stop=True)
                    pe.matmul(ps_node[:, 512:CHUNK * P], wlin[:, :], xinT[:, 512:CHUNK * P], start=True, stop=True
                              ).then_inc(t_node, 1)
                    wait_apart(pe, t_nodec, n, pe_passed)
                    for t in range(CHUNK):
                        mm = pe.matmul(ps_row[:, t * ROW:(t + 1) * ROW], nodeT[:, t * P:(t + 1) * P], wtab[:, :],
                                       start=True, stop=True)
                    mm.then_inc(t_row, 1)

            pe.wait_ge(sidx_ready, 2)
            pe.wait_ge(t_rowc, CHUNKS)
            pe.matmul(ps[:, 0, 0:ITS], shift[:, 0, :], starts[:, 0:ITS], start=True, stop=False)
            pe.matmul(ps[:, 0, 0:ITS], shift[:, 1, :], starts[:, 1:ITS + 1], start=False, stop=True
                      ).then_inc(shifted, 1)
            pe.wait_ge(counted, 1)
            for q in range(QUADS):
                pe.matmul(ps[:, 1, q * P:q * P + ITS], seed_perm[:, q, :], counts[:, :], start=True, stop=True)
            pe.matmul(ps[:, 2, 0:ITS], pool_perm, counts[:, :], start=True, stop=True).then_inc(permuted, 1)
            pe.wait_ge(idx_ready, RING)

            def turn(s, c, bank):
                for p in range(PAIRS):
                    lo = 2 * p * ROW + c
                    mm = pe.transpose(ps[:, bank, p * P:(p + 1) * P],
                                      gathered[:, s.slot(0, RING), lo:lo + 2 * ROW - 3:4], ident[:, :])
                return mm

            def step(s):
                if s.has(0):
                    wait(pe, h_sb, s.octet(0))
                    pe.wait_ge(g_in[s.slot(0, RING)], s.round(0) * (16 * OCT) + 16 * OCT)
                    turn(s, 0, B_QH).then_inc(q_ps, 1)
                    wait(pe, back_sb, s.octet(L_BACK))
                    turn(s, 1, B_KX).then_inc(k_ps, 1)
                if s.has(L_PMA):
                    wait(pe, xb_sb, s.octet(L_PMA - 1))
                    pe.matmul(ps[:, B_FF, :], pma_diag[:, :], xb[:, s.slot(L_PMA, 2), :], start=True, stop=True
                              ).then_inc(pma_ps, 1)
                if s.has_iteration(L_DEC1):
                    fin_op(s, L_DEC1, pooled_ok, ps_fin[0:D, :], pooled, ident)
                if s.has_iteration(L_DEC2):
                    fin_op(s, L_DEC2, hid1_ok, ps_fin[0:D, :], mats["p_ff"], hid1)
                if s.has_iteration(L_OUT):
                    fin_op(s, L_OUT, hid2_ok, ps_fin[0:D, :], mats["d_ff"], hid2)
                if s.has_iteration(L_WEIGHTS):
                    wait(pe, p2_norm, s.iteration(L_WEIGHTS) + 1)
                    pe.transpose(ps_seedT, scores2[:, :], ident[:, :]).then_inc(seedT_ps, 1)
                if s.has(L_ATTEND):
                    if s.slot(L_ATTEND, 2) == 0:
                        wait(pe, p_diag, s.batch(L_ATTEND) * 4 + 4)
                    wait(pe, h2_sb, s.octet(L_ATTEND))
                    for p in range(PAIRS):
                        for h in range(2):
                            lo = (2 * p + h) * ROW + 3
                            mm = pe.matmul(ps[D * h:D * h + D, B_AV, p * P:(p + 1) * P],
                                           gathered[:, s.slot(L_ATTEND, RING), lo:lo + ROW - 3:4],
                                           probs_diag[:, s.slot(L_ATTEND, 4) // 2,
                                                      OCT * h + PAIRS * s.slot(L_ATTEND, 2) + p, :],
                                           start=True, stop=True)
                    mm.then_inc(av_ps, 1)
                if s.has(L_SCORES):
                    if s.slot(L_SCORES, 2) == 0:
                        wait(pe, s_sb, s.batch(L_SCORES))
                    wait(pe, k_sb, s.octet(L_SCORES - 1))
                if s.has(0):
                    wait(pe, q_sb, s.octet(-1))
                    turn(s, 2, B_QH).then_inc(h_ps, 1)
                if s.has(L_SCORES):
                    par = s.slot(L_SCORES, 2)
                    for p in range(PAIRS):
                        for q in range(QUADS):
                            for h in range(2):
                                lo = p * P + DEG * q
                                hi = D * h
                                mm = pe.matmul(
                                    ps[DEG * q:DEG * q + DEG, B_S + h, (PAIRS * par + p) * DEG:(PAIRS * par + p + 1) * DEG],
                                    qT[hi:hi + D, par, lo:lo + DEG], kT[hi:hi + D, par, lo:lo + DEG],
                                    start=True, stop=True)
                    mm.then_inc(s_ps, 1)
                if s.has_iteration(L_POOL):
                    wait(pe, weights2_ok, s.iteration(L_POOL) + 1)
                    wait(pe, y_ok, s.iteration(L_POOL))
                    wait(pe, back_sb, s.octet(L_POOL - OCTS_PER_IT))
                    for c in range(OCTS_PER_IT):
                        mm = pe.matmul(ps[DEG * c:DEG * c + DEG, B_POOL, :],
                                       weights2[:, c].rearrange("p t a -> p (t a)"),
                                       xp_rows[:, (s.slot(L_POOL, RING) + c) % RING, :], start=True, stop=True)
                    mm.then_inc(pool_ps, 1)
                if s.has(L_FF):
                    wait(pe, xp_sb, s.octet(L_FF))
                    wait(pe, h2_sb, s.octet(L_FF - 1))
                    pe.matmul(ps[:, B_FF, :], ff_diag[:, :], h2[:, s.slot(L_FF, 2), :], start=True, stop=True
                              ).then_inc(ff_ps, 1)
                if s.has_iteration(L_DEC1):
                    fin_op(s, L_DEC1, pooledT_ok, ps_fin[0:D, :], mats["wvo2"], pooledT)
                if s.has_iteration(L_DEC2):
                    fin_op(s, L_DEC2, pvec_ok, ps_fin[0:D, :], mats["wvo3"], pvec)
                if s.has_iteration(L_OUT):
                    if s.has_iteration(L_WEIGHTS):
                        wait(pe, weights2_ok, s.iteration(L_WEIGHTS) + 1)
                    fin_op(s, L_OUT, decr_ok, ps_fin[:, 0:D], decr, ident)
                if s.has(L_BACK):
                    if s.has(0):
                        wait(pe, k_sb, s.octet(-1))
                    else:
                        wait(pe, back_sb, s.octet(L_BACK))
                    wait(pe, xp_sb, s.octet(L_BACK - 1))
                    for p in range(PAIRS):
                        mm = pe.transpose(ps[:, B_KX, p * P:(p + 1) * P],
                                          xp[:, s.slot(L_BACK, 2), p * P:(p + 1) * P], ident[:, :])
                    mm.then_inc(back_ps, 1)
                    c = s.slot(L_BACK, OCTS_PER_IT)
                    if c == 0:
                        wait(pe, s2_sb, s.iteration(L_BACK))
                    for p in range(PAIRS):
                        mm = pe.matmul(ps_seed[DEG * c:DEG * c + DEG, :], seed_u[:, 6 - 2 * p:38 - 2 * p],
                                       xp[:, s.slot(L_BACK, 2), p * P:(p + 1) * P],
                                       start=(p == 0), stop=(p == PAIRS - 1))
                    mm.then_inc(seed_ps, 1)
            def fin_op(s, lag, ready, out_, lhs, rhs):
                wait_apart(pe, ready, s.iteration(lag) + 1, pe_passed)
                if rhs is ident:
                    mm = pe.transpose(out_, lhs[:, :], rhs[0:lhs.shape[0], 0:lhs.shape[0]])
                else:
                    mm = pe.matmul(out_, lhs[:, :], rhs[:, :], start=True, stop=True)
                mm.then_inc(fin_ps, 1)

            steps(pe, step)

        @block.scalar
        def _(act):
            def copy(o, i):
                return nc.scalar.activation(o, i, ACT.Copy)

            act.wait_ge(dst_in, 16)
            copy(sample_own[:, :], dst_i[:, 0:BLOCK:WINDOW]).then_inc(dst_cast, 1)
            copy(dst_f, dst_i).then_inc(dst_cast, 1)
            act.wait_ge(w_in, ALL_WEIGHTS)
            act.wait_ge(dve_zero, 1)

            def table_chunk(g, b):
                n = g * 2 + (b + 1)
                act.wait_ge(t_xT, n)
                copy(xinT, ps_xT).then_inc(t_xTc, 1)
                act.wait_ge(t_node, n)
                nc.scalar.activation(nodeT[0:D, :], ps_node, ACT.Identity, bias=c_("b_lin")).then_inc(t_nodec, 1)
                act.wait_ge(t_row, n)
                wait(act, tab_out[b], g * 16)
                copy(trow[:, b, :], ps_row).then_inc(t_rowc, 1)

            table_chunk(0, 0)
            table_chunk(0, 1)
            with act.Fori(1, CHUNKS // 2) as g:
                table_chunk(g, 0)
                table_chunk(g, 1)

            def step(s):
                if s.has(0):
                    act.wait_ge(q_ps, s.octet(-1))
                    wait(act, s_ps, s.octet(1))
                    copy(qT[:, s.slot(0, 2), :], ps[:, B_QH, :]).then_inc(q_sb, 1)
                    act.wait_ge(k_ps, s.octet(-1))
                    copy(kT[:, s.slot(0, 2), :], ps[:, B_KX, :]).then_inc(k_sb, 1)
                if s.has_iteration(L_DEC2):
                    wait(act, fin_ps, s.iteration(L_DEC2) * 6 + 2)
                    nc.scalar.activation(hid1[:, :], ps_fin[0:D, :], ACT.Identity, bias=c_("b1")).then_inc(hid1_ok, 1)
                if s.has_iteration(L_OUT):
                    wait(act, fin_ps, s.iteration(L_OUT) * 6 + 4)
                    nc.scalar.activation(hid2[:, :], ps_fin[0:D, :], ACT.Identity, bias=c_("b3")).then_inc(hid2_ok, 1)
                if s.has_iteration(L_SEED_T):
                    wait(act, s2_diff, s.iteration(L_SEED_T) + 1)
                    nc.scalar.activation(scores2[:, :], scores2[:, :], ACT.Exp).then_inc(p2_exp, 1)
                if s.has(L_PMA):
                    act.wait_ge(pma_ps, s.octet(L_PMA - 1))
                    wait(act, seed_ps, s.octet(L_PMA + 1))
                    nc.scalar.activation(xp[:, s.slot(L_PMA, 2), :], ps[:, B_FF, :], ACT.Relu,
                                         bias=c_("pma_b", P)).then_inc(xp_sb, 1)
                if s.has(0):
                    act.wait_ge(h_ps, s.octet(-1))
                    wait(act, h2_sb, s.octet(RING - 1))
                    copy(hT[:, s.slot(0, RING), :], ps[:, B_QH, :]).then_inc(h_sb, 1)
                if s.has_batch(L_SOFTMAX):
                    wait(act, s_diff, s.batch(L_SOFTMAX) + 1)
                    wait(act, p_diag, s.batch(L_SOFTMAX + 2) * 4)
                    nc.scalar.activation(probs[:, s.slot(L_SOFTMAX, 4) // 2, :], scores[:, :], ACT.Exp
                                         ).then_inc(p_exp, 1)
                if s.has_iteration(L_DEC1):
                    wait(act, fin_ps, s.iteration(L_DEC1) * 6 + 1)
                    copy(pooledT[:, :], ps_fin[0:D, :]).then_inc(pooledT_ok, 1)
                if s.has(L_BACK):
                    act.wait_ge(back_ps, s.octet(L_BACK - 1))
                    wait(act, pool_ps, s.iteration(L_BACK) - 1)
                    copy(xp_rows[:, s.slot(L_BACK, RING), :], ps[:, B_KX, :]).then_inc(back_sb, 1)

            steps(act, step)
            act.wait_ge(ln_ok, 5)
            nc.scalar.activation(lnv[:, 3, :], lnv[:, 2, :], ACT.Sqrt, bias=eps[:, 0:1], scale=1.0).then_inc(ln_std, 1)

        @block.vector
        def _(dve):
            V = nc.vector
            chained = [0]

            def link(ins):
                chained[0] += 1
                ins.then_inc(dve_chain, 1)
                dve.wait_ge(dve_chain, chained[0])

            V.memset(ff_diag[:, :], 0.0)
            V.memset(pma_diag[:, :], 0.0)
            V.memset(wtab[:, :], 0.0)
            link(V.memset(nodeT[D:D + 1, :], 1.0))
            V.memset(xin[:, :, :, :], 0.0).then_inc(dve_zero, 1)
            V.memset(seed_u[:, :], 0.0)
            V.memset(row_i[:, :], 0)
            V.memset(start_i[:, :], 0)
            V.memset(idx_all[:, ITS * DEG:], 0)
            V.memset(starts[:, ITS:ITS + 1], float(E))
            V.memset(eps[:, :], EPS)
            V.memset(rows[:, ITS - 1, :], 0.0).then_inc(dve_zero, 1)
            dve.wait_ge(pool_cst, 2)
            V.tensor_copy(iota_j[:, :], iota_ji[:, :])
            link(V.tensor_copy(node_f[:, :], node_i[:, :]))

            dve.wait_ge(samples_in, 16)
            with dve.Fori(0, ITS) as m:
                V.tensor_scalar(junk[:, 0:SAMPLES], sample_f, node_f[:, bass.ds(m, 1)], None, ALU.is_lt, ALU.add,
                                accum_out=count1[:, bass.ds(m, 1)]).then_inc(sampled, 1)
                dve.wait_ge(sampled, m + 1)
            link(V.tensor_scalar(row_f[:, :], count1[:, :], -1.0, 0.0, ALU.add, ALU.max))
            link(V.tensor_copy(row_i[:, 0:ITS], row_f[:, :]))
            V.tensor_copy(win_idx[:, :, :], row_i[:, 0:2 * HALF].rearrange("p (h t) -> p h t", h=2)
                          ).then_inc(win_idx_ready, 2)

            marked = [0]

            def mark(ins):
                marked[0] += 1
                ins.then_inc(prep, 1)
                dve.wait_ge(prep, marked[0])

            dve.wait_ge(w_in, ALL_WEIGHTS)
            dve.wait_ge(pool_cst, 2 + 3 + 2 * QUADS)
            V.tensor_reduce(quad_of[:, :], ident[:, :].rearrange("p (a j) -> p a j", j=DEG), AX_X, ALU.add)
            V.tensor_reduce(tile_of[:, :], ident[:, :].rearrange("p (c t a) -> p t c a", c=QUADS, t=OCT),
                            mybir.AxisListType.XY, ALU.add)
            V.tensor_copy(wtab[D:D + 1, 2:ROW:4], out_b)
            mark(V.tensor_copy(wtab[0:D, 2:ROW:4], ident[0:D, 0:D]))
            dve.wait_ge(prep_pe, 1)
            mark(V.tensor_copy(tmpT[:, :], ps[0:D, 0, 0:D + 1]))
            V.tensor_scalar(wtab[:, 0:ROW:4], wraw[:, 0:D], D ** -0.5, None, ALU.mult)
            V.tensor_copy(wtab[:, 1:ROW:4], wraw[:, D:2 * D])
            dve.wait_ge(prep_pe, 2)
            mark(V.tensor_copy(wtab[:, 3:ROW:4], ps[0:D + 1, 1, 0:D]))
            dve.wait_ge(prep_pe, 4)
            V.tensor_copy(wkT2[:, 0, :], ps[0:D, 2, 0:D])
            mark(V.tensor_copy(wkT2[:, 1, :], ps[0:D, 2, 0:D]))
            mark(V.tensor_scalar(c_("qs"), ps[0:D, 3, 0:1], c_("bq2"), D ** -0.5,
                                 ALU.add, ALU.mult))
            mark(V.tensor_copy(wide[:, :], c_("qs").broadcast_to((D, P))))
            dve.wait_ge(prep_pe, 10)
            V.tensor_copy(seed_u[0:D, 6:7], ps[0:D, 4, 0:1])
            V.tensor_copy(seed_u[D:P, 7:8], ps[D:P, 4, 0:1])
            V.tensor_copy(c_("c2", P), ps[:, 5, 0:1])
            V.tensor_tensor(c_("b3"), ps[0:D, 3, 0:1], c_("bo3"), ALU.add)
            link(V.tensor_tensor(c_("b1"), ps[0:D, 2, 0:1], c_("bo2"), ALU.add))
            link(V.tensor_tensor(c_("b1"), c_("b1"), c_("seed"), ALU.add))
            V.tensor_copy(wide[:, 0:D], ps[0:D, 0, 0:D])
            mark(V.tensor_copy(wide[:, D:2 * D], ps[0:D, 1, 0:D]))
            for t, n in ((ff_diag, P), (mats["p_ff"], D), (mats["d_ff"], D)):
                V.tensor_tensor(t[:, :], t[:, :], ident[0:n, 0:n], ALU.add)
            dve.wait_ge(prep_pe, 12)
            V.tensor_copy(mats["wvo2"][:, :], ps[0:D, 6, 0:D])
            mark(V.tensor_tensor(mats["wvo3"][:, :], ps[0:D, 7, 0:D], ident[0:D, 0:D], ALU.add))

            link(V.memset(borrowed, 0.0))

            with dve.Fori(0, ITS // (2 * HALF)) as g:
                for h in range(2):
                    dve.wait_ge(win_in[h], g * (16 * HALF) + 16 * HALF)
                    for t in range(HALF):
                        m = g * (2 * HALF) + (h * HALF + t)
                        V.tensor_scalar(junk[:, 0:WINDOW], windows[:, h, t, :], node_f[:, bass.ds(m, 1)], None,
                                        ALU.is_lt, ALU.add, accum_out=below[:, bass.ds(m, 1)]).then_inc(searched, 1)
                        dve.wait_ge(searched, m + 1)
                    V.tensor_copy(win_idx[:, h, :], row_i[:, bass.ds(g * (2 * HALF) + (h + 2) * HALF, HALF)]
                                  ).then_inc(win_idx_ready, 1)
            link(V.scalar_tensor_tensor(starts[:, 0:ITS], row_f[:, :], float(WINDOW), below[:, :], ALU.mult, ALU.add))
            link(V.tensor_copy(start_i[:, 0:ITS], starts[:, 0:ITS]))
            V.tensor_copy(sidx[:, :, :], start_i[:, 0:2 * HALF].rearrange("p (h t) -> p h t", h=2)
                          ).then_inc(sidx_ready, 2)
            dve.wait_ge(shifted, 1)
            V.tensor_tensor(counts[:, :], ps[:, 0, 0:ITS], starts[:, 0:ITS], ALU.subtract).then_inc(counted, 1)
            dve.wait_ge(counted, 1)
            link(V.tensor_scalar(counts_b[:, :], counts[:, :], float(DEG), None, ALU.min))
            V.transpose(count_slot[:, :].rearrange("p (m b) -> p m b", b=DEG),
                        counts_b[:, :].unsqueeze(2).broadcast_to((P, ITS, DEG)))
            dve.wait_ge(permuted, 1)
            for q in range(QUADS):
                V.tensor_copy(count_seed[:, :, q], ps[:, 1, q * P:q * P + ITS])
            link(V.tensor_scalar(nonempty[:, :], ps[:, 2, 0:ITS], 0.0, None, ALU.is_gt))
            with dve.Fori(0, ITS // (2 * HALF)) as g:
                for h in range(2):
                    dve.wait_ge(swin_in[h], g * (16 * HALF) + 16 * HALF)
                    V.tensor_copy(src_all[:, bass.ds(g * (2 * HALF * DEG) + h * HALF * DEG, HALF * DEG)],
                                  src_win[:, h].rearrange("p t n -> p (t n)")).then_inc(src_copied, 1)
                    V.tensor_copy(sidx[:, h, :], start_i[:, bass.ds(g * (2 * HALF) + (h + 2) * HALF, HALF)]
                                  ).then_inc(sidx_ready, 1)
            dve.wait_ge(src_copied, ITS // HALF)
            link(V.transpose(idx_all[:, 0:ITS * DEG], src_all))
            V.tensor_copy(idx[:, :, :].rearrange("p s t -> p (s t)"), idx_all[:, 0:RING * OCT]
                          ).then_inc(idx_ready, RING)

            def by_slot(ap):
                return ap.rearrange("p (t j) -> p t j", j=DEG)

            iota_slots = iota_j[:, :].unsqueeze(1).broadcast_to((P, 2, DEG))

            def step(s):
                if s.has_batch(L_SOFTMAX):
                    n = s.batch(L_SOFTMAX)
                    dve.wait_ge(s_ps, s.octet(L_SOFTMAX - 2))
                    dve.wait_ge(mask_ok, n + 1)
                    wait(dve, p_exp, n)
                    V.scalar_tensor_tensor(scores[:, :].rearrange("p (h n) -> p h n", h=2),
                                           empty[:, :].rearrange("p (h n) -> p h n", h=2), MASKED, ps_scores,
                                           ALU.mult, ALU.add).then_inc(s_sb, 1)
                if s.has_iteration(L_Y):
                    y_rows(s)
                if s.has_iteration(L_SEED):
                    m = s.iteration(L_SEED)
                    dve.wait_ge(m2_ok, m + 1)
                    dve.wait_ge(seed_ps, s.octet(L_SEED - 4))
                    wait(dve, seedT_ps, m)
                    V.scalar_tensor_tensor(scores2[:, :], ps_seed, c_("c2", P), empty2[:, :], ALU.add, ALU.add
                                           ).then_inc(s2_sb, 1)
                if s.has_batch(L_SOFTMAX):
                    n = s.batch(L_SOFTMAX)
                    dve.wait_ge(s_sb, n + 1)
                    V.tensor_reduce(top[:, :], by_slot(scores[:, :]), AX_X, ALU.max).then_inc(s_top, 1)
                if s.has_batch(L_NORM):
                    pr = probs[:, s.slot(L_NORM, 4) // 2, :]
                    n = s.batch(L_NORM)
                    dve.wait_ge(p_exp, n + 1)
                    V.tensor_reduce(total[:, :], by_slot(pr), AX_X, ALU.add).then_inc(p_sum, 1)
                if s.has(L_ATTEND):
                    wait(dve, av_ps, s.octet(L_ATTEND - 1))
                    wait(dve, h_sb, s.octet(L_ATTEND - 1))
                    wait(dve, ff_ps, s.octet(L_ATTEND + 1))
                    V.tensor_tensor(h2[:, s.slot(L_ATTEND, 2), :], ps[:, B_AV, :],
                                    hT[:, s.slot(L_ATTEND, RING), :], ALU.add).then_inc(h2_sb, 1)
                if s.has_batch(L_SOFTMAX):
                    dve.wait_ge(s_top, n + 1)
                    V.tensor_tensor(by_slot(scores[:, :]), by_slot(scores[:, :]),
                                    top[:, :].unsqueeze(2).broadcast_to((P, 16, DEG)), ALU.subtract
                                    ).then_inc(s_diff, 1)
                if s.has_batch(L_NORM):
                    dve.wait_ge(p_sum, n + 1)
                    V.reciprocal(share[:, :], total[:, :]).then_inc(p_share, 1)
                if s.has_iteration(L_DEC2):
                    m = s.iteration(L_DEC2)
                    wait(dve, fin_ps, m * 6 + 3)
                    V.scalar_tensor_tensor(pvec[:, :], ps_fin[0:D, :], c_("bff2"), hid1[:, :], ALU.add, ALU.max
                                           ).then_inc(pvec_ok, 1)
                if s.has_iteration(L_OUT):
                    out_rows(s)
                if s.has_iteration(L_WEIGHTS):
                    wait(dve, seedT_ps, s.iteration(L_WEIGHTS) + 1)
                    wait(dve, pool_ps, s.iteration(L_WEIGHTS))
                    V.tensor_tensor(
                        weights2[:, :, :, :],
                        ps_seedT.rearrange("p (c t) -> p c t", c=OCTS_PER_IT)[:, :, 0:OCT].unsqueeze(3).broadcast_to(
                            (P, OCTS_PER_IT, OCT, QUADS)),
                        quad_of[:, :].unsqueeze(1).unsqueeze(1).broadcast_to((P, OCTS_PER_IT, OCT, QUADS)),
                        ALU.mult).then_inc(weights2_ok, 1)
                if s.has_batch(L_NORM):
                    dve.wait_ge(p_share, n + 1)
                    V.tensor_tensor(by_slot(pr), by_slot(pr), share[:, :].unsqueeze(2).broadcast_to((P, 16, DEG)),
                                    ALU.mult).then_inc(p_norm, 1)
                if s.has(L_FF):
                    wait(dve, ff_ps, s.octet(L_FF - 1))
                    wait(dve, pma_ps, s.octet(L_FF + 1))
                    V.scalar_tensor_tensor(xb[:, s.slot(L_FF, 2), :], ps[:, B_FF, :], c_("ff_b", P),
                                           h2[:, s.slot(L_FF, 2), :], ALU.add, ALU.max).then_inc(xb_sb, 1)
                if s.has_batch(L_NORM):
                    dve.wait_ge(p_norm, n + 1)
                    wait(dve, av_ps, s.octet(L_NORM + 2))
                    for q in range(QUADS):
                        lo = DEG * q
                        V.transpose(probs_diag[lo:lo + DEG, s.slot(L_NORM, 4) // 2, :, lo:lo + DEG],
                                    pr[lo:lo + DEG, :].rearrange("p (t j) -> p t j", j=DEG)).then_inc(p_diag, 1)
                if s.has_iteration(L_MASK2):
                    m = s.iteration(L_MASK2)
                    wait(dve, s2_sb, m)
                    V.tensor_tensor(empty2[:, :].rearrange("p (a j) -> p a j", j=DEG),
                                    iota_j[:, :].unsqueeze(1).broadcast_to((P, QUADS, DEG)),
                                    count_seed[:, bass.ds(m, 1), :].rearrange("p m a -> p (m a)").unsqueeze(2)
                                    .broadcast_to((P, QUADS, DEG)), ALU.is_ge).then_inc(m2_cmp, 1)
                    dve.wait_ge(m2_cmp, m + 1)
                    V.tensor_scalar(empty2[:, :], empty2[:, :], MASKED, None, ALU.mult).then_inc(m2_ok, 1)
                if s.has_iteration(L_SEED):
                    m = s.iteration(L_SEED)
                    dve.wait_ge(s2_sb, m + 1)
                    V.tensor_reduce(top2[:, :], by_slot(scores2[:, :]), AX_X, ALU.max).then_inc(s2_top, 1)
                    dve.wait_ge(s2_top, m + 1)
                    V.tensor_tensor(by_slot(scores2[:, :]), by_slot(scores2[:, :]),
                                    top2[:, :].unsqueeze(2).broadcast_to((P, QUADS, DEG)), ALU.subtract
                                    ).then_inc(s2_diff, 1)
                if s.has_iteration(L_SEED_T):
                    m = s.iteration(L_SEED_T)
                    dve.wait_ge(p2_exp, m + 1)
                    V.tensor_reduce(total2[:, :], by_slot(scores2[:, :]), AX_X, ALU.add).then_inc(p2_sum, 1)
                    dve.wait_ge(p2_sum, m + 1)
                    V.reciprocal(share2[:, :], total2[:, :]).then_inc(p2_share, 1)
                    dve.wait_ge(p2_share, m + 1)
                    V.tensor_tensor(by_slot(scores2[:, :]), by_slot(scores2[:, :]),
                                    share2[:, :].unsqueeze(2).broadcast_to((P, QUADS, DEG)), ALU.mult
                                    ).then_inc(p2_norm, 1)
                if s.has_iteration(L_POOL):
                    m = s.iteration(L_POOL)
                    dve.wait_ge(pool_ps, m + 1)
                    V.tensor_tensor(pool_part[:, :].rearrange("p (t d) -> p t d", d=D),
                                    ps[:, B_POOL, :].rearrange("p (t d) -> p t d", d=D),
                                    tile_of[:, :].unsqueeze(2).broadcast_to((P, OCT, D)), ALU.mult
                                    ).then_inc(pool_own, 1)
                    dve.wait_ge(pool_own, m + 1)
                    wait(dve, fin_ps, m * 6 - 5 if s.looped or m > 0 else 0)
                    V.tensor_reduce(pooled[:, :], pool_part[:, :].rearrange("p (t d) -> p d t", d=D), AX_X, ALU.add
                                    ).then_inc(pooled_ok, 1)
                if s.has(0):
                    if s.looped or 1 <= s.at <= OCTETS - RING:
                        dve.wait_ge(g_in[s.slot(1, RING)], s.round(1) * (16 * OCT) + 16 * OCT)
                        V.tensor_copy(idx[:, s.slot(1, RING), :], idx_all[:, bass.ds(s.octet(1 - RING) * OCT, OCT)]
                                      ).then_inc(idx_ready, 1)

                if s.has_batch(L_MASK):
                    n = s.batch(L_MASK)
                    V.tensor_tensor(
                        empty[:, :].rearrange("p (h t j) -> p h t j", h=2, j=DEG),
                        iota_j[:, :].unsqueeze(1).unsqueeze(1).broadcast_to((P, 2, OCT, DEG)),
                        count_slot[:, bass.ds(n * 16, 16)].rearrange("p (t h) -> p h t", h=2).unsqueeze(3).broadcast_to(
                            (P, 2, OCT, DEG)), ALU.is_ge).then_inc(mask_ok, 1)

            def out_rows(s):
                m = s.iteration(L_OUT)
                if s.has_iteration(L_WEIGHTS):
                    dve.wait_ge(seedT_ps, s.iteration(L_WEIGHTS) + 1)
                dve.wait_ge(fin_ps, m * 6 + 5)
                V.scalar_tensor_tensor(dec[:, :], ps_fin[0:D, :], c_("bff3"), hid2[:, :], ALU.add, ALU.max
                                       ).then_inc(dec_ok, 1)
                dve.wait_ge(dec_ok, m + 1)
                V.tensor_scalar(decr[:, :], dec[:, :], 0.0, FLT_MAX, ALU.max, ALU.min).then_inc(decr_ok, 1)

            def y_rows(s):
                m = s.iteration(L_Y)
                dve.wait_ge(fin_ps, m * 6 + 6)
                row = rows[:, bass.ds(m, 1), :].rearrange("p m d -> p (m d)")
                V.scalar_tensor_tensor(row, ps_fin[:, 0:D], nonempty[:, bass.ds(m, 1)], row, ALU.mult, ALU.add
                                       ).then_inc(y_ok, 1)
                dve.wait_ge(y_ok, m + 1)
                V.bn_stats(stats[:, bass.ds(m, 1), :].rearrange("p m n -> p (m n)"), row).then_inc(stats_ok, 1)

            dve.wait_ge(rows_in, ROWS_LOADED)
            steps(dve, step)

            dve.wait_ge(stats_ok, ITS)
            mean, half, var, std, inv = (lnv[:, i, :] for i in range(5))
            V.tensor_tensor(mean, stats[:, :, 1], stats[:, :, 4], ALU.add).then_inc(ln_ok, 1)
            V.tensor_tensor(half, stats[:, :, 1], stats[:, :, 4], ALU.subtract).then_inc(ln_ok, 1)
            V.tensor_tensor(var, stats[:, :, 2], stats[:, :, 5], ALU.add).then_inc(ln_ok, 1)
            dve.wait_ge(ln_ok, 3)
            V.scalar_tensor_tensor(half, half, D / 4.0, half, ALU.mult, ALU.mult).then_inc(ln_ok, 1)
            V.tensor_scalar(mean, mean, 0.5, None, ALU.mult)
            dve.wait_ge(ln_ok, 4)
            link(V.tensor_tensor(var, var, half, ALU.add))
            V.tensor_scalar(var, var, 1.0 / D, None, ALU.mult).then_inc(ln_ok, 1)
            dve.wait_ge(ln_std, 1)
            link(V.reciprocal(inv, std))
            with dve.Fori(0, ITS // 14) as g:
                for k in range(14):
                    m = g * 14 + k
                    row = rows[:, bass.ds(m, 1), :].rearrange("p m d -> p (m d)")
                    ins = V.tensor_scalar(row, row, lnv[:, 0, bass.ds(m, 1)], lnv[:, 4, bass.ds(m, 1)],
                                          ALU.subtract, ALU.mult)
                ins.then_inc(normed, 1)


_OUT = (12500, 64)


def kernel(**inputs):
    import numpy as np
    import concourse.bacc as bacc
    from concourse.bass_utils import run_bass_kernel_spmd

    nc = bacc.Bacc("TRN2", target_bir_lowering=False, num_devices=1)
    arrays, args = {}, {}
    for name, value in inputs.items():
        arr = np.ascontiguousarray(value)
        arrays[f"in_{name}"] = arr
        args[name] = nc.dram_tensor(f"in_{name}", arr.shape, mybir.dt.from_np(arr.dtype), kind="ExternalInput").ap()
    out = nc.dram_tensor("out_rows", _OUT, F32, kind="ExternalOutput").ap()
    gnn_kernel(nc, args, out)
    r = run_bass_kernel_spmd(nc, [arrays], core_ids=[0])
    return r.results[0]["out_rows"]
```

```python
from contextlib import ExitStack

import concourse.bass as bass
from concourse import mybir

ALU = mybir.AluOpType
ACT = mybir.ActivationFunctionType
F32 = mybir.dt.float32
I32 = mybir.dt.int32
BF16 = mybir.dt.bfloat16
AX_X = mybir.AxisListType.X

P = 128
D = 64
DEG = 32
QUADS = P // DEG
OCT = 8
PAIRS = OCT // 2
OCTS_PER_IT = P // (QUADS * OCT)
TILES_PER_IT = OCT * OCTS_PER_IT
RING = 8
ROW = 2 * D
MASKED = -3.0e38
FLT_MAX = 3.4028234663852886e38
EPS = 1e-5

SAMPLES = 625
HALF = 7
CHUNK = 7

L_SCORES = 1
L_MASK = 2
L_SOFTMAX = 3
L_NORM = 4
L_ATTEND = 5
L_H2 = 6
L_FF = 6
L_PMA = 7
L_BACK = 8
L_MASK2 = 11
L_SEED = 12
L_SEED_T = 13
L_WEIGHTS = 14
L_POOL = 15
L_DEC1 = 16
L_DEC2 = 17
L_OUT = 18
L_Y = 19


class Step:

    def __init__(self, group, at, octets):
        self.group, self.at, self.looped, self.octets = group, at, not isinstance(group, int), octets

    def octet(self, lag):
        return self.group * 8 + (self.at - lag)

    def batch(self, lag):
        return self.group * 4 + (self.at - lag) // 2

    def iteration(self, lag):
        return self.group * 2 + (self.at - lag) // 4

    def round(self, lag):
        return self.group + (self.at - lag) // RING

    def slot(self, lag, n):
        return (self.at - lag) % n

    def has(self, lag):
        return self.looped or 0 <= self.at - lag < self.octets

    def has_batch(self, lag):
        return (self.at - lag) % 2 == 0 and (self.looped or 0 <= self.at - lag < self.octets)

    def has_iteration(self, lag):
        return (self.at - lag) % 4 == 0 and (self.looped or 0 <= self.at - lag < self.octets)


def wait(eng, sem, count):
    if isinstance(count, int) and count <= 0:
        return
    eng.wait_ge(sem, count)


def wait_apart(eng, sem, count, passed):
    if isinstance(count, int) and count <= 0:
        return
    eng.wait_ge(sem, count)
    if not isinstance(count, int):
        eng.sem_inc(passed, 1)


def gnn_kernel(nc, a, out):
    x, src, dst = a["x"], a["src"], a["dst"]
    w = {k[len("L0_gnn_"):]: v for k, v in a.items() if k.startswith("L0_gnn_")}
    N, E = x.shape[0], src.shape[0]
    ITS = -(-N // P)
    NPAD = ITS * P
    LAST = N - (ITS - 1) * P
    OCTETS = ITS * OCTS_PER_IT
    WINDOW = E // SAMPLES
    CHUNKS = ITS // CHUNK
    BLOCK = E // 125
    assert x.shape[1] == D and SAMPLES * WINDOW == E and ITS % (2 * HALF) == 0 and ITS % (2 * CHUNK) == 0
    assert BLOCK % WINDOW == 0 and 125 * BLOCK == E
    PER_ROW = BLOCK // WINDOW
    SEARCHES = ITS // HALF

    LOOP_FROM = L_Y + 1
    GROUPS = (OCTETS - LOOP_FROM) // RING
    LOOP_TO = LOOP_FROM + RING * GROUPS
    END = OCTETS + L_Y

    with ExitStack() as ctx:
        def sb(name, shape, dt=F32):
            return ctx.enter_context(nc.sbuf_tensor(name, shape, dt))

        def sem(name):
            return ctx.enter_context(nc.semaphore(name))

        table = nc.dram_tensor("node_table", (NPAD, ROW), F32).ap()
        dst_rows = nc.dram_tensor("dst_rows", (SAMPLES, WINDOW), F32).ap()
        dst_samples = nc.dram_tensor("dst_samples", (1, SAMPLES), F32).ap()
        src_padded = nc.dram_tensor("src_padded", (E + D, 1), I32).ap()

        gathered_all = sb("gathered", [P, max(RING * OCT * ROW, 2 * HALF * WINDOW)])
        gathered = gathered_all[:, 0:RING * OCT * ROW].rearrange("p (s n) -> p s n", s=RING)
        probs_diag = sb("probs_diag", [P, 2, 2 * OCT, P])
        qT = sb("qT", [P, 2, 512])
        avT = sb("avT", [P, 2, 512])
        hT = sb("hT", [P, RING, 512])
        h2 = sb("h2", [P, 2, 512])
        xb = sb("xb", [P, 2, 512])
        xp = sb("xp", [P, 2, 512])
        xp_rows = sb("xp_rows", [P, RING, 512])
        empty = sb("empty", [P, 512])
        scores = sb("scores", [P, 512])
        probs = sb("probs", [P, 2, 512])
        top = sb("top", [P, 16])
        total = sb("total", [P, 16])
        share = sb("share", [P, 16])
        idx = sb("idx", [P, RING, OCT], I32)
        idx_all = sb("idx_all", [P, (ITS + 2) * DEG], I32)
        count_slot = sb("count_slot", [P, ITS * DEG], BF16)
        rows = sb("rows", [P, ITS, D])
        count_seed = sb("count_seed", [P, ITS, QUADS])
        empty2 = sb("empty2", [P, P])
        scores2 = sb("scores2", [P, P])
        top2 = sb("top2", [P, QUADS])
        total2 = sb("total2", [P, QUADS])
        share2 = sb("share2", [P, QUADS])
        weights2 = sb("weights2", [P, OCTS_PER_IT, OCT, QUADS])
        pool_part = sb("pool_part", [P, 512])
        pooled = sb("pooled", [P, D])
        pooledT = sb("pooledT", [D, P])
        hid1 = sb("hid1", [D, P])
        pvec = sb("pvec", [D, P])
        hid2 = sb("hid2", [D, P])
        dec = sb("dec", [D, P])
        decr = sb("decr", [D, P])
        stats = sb("stats", [P, ITS, 6])
        nonempty = sb("nonempty", [P, ITS])
        lnv = sb("lnv", [P, 5, ITS])

        ident = sb("ident", [P, P])
        shift = scores[:, P:3 * P].rearrange("p (a b) -> p a b", a=2)
        seed_perm = empty[:, :].rearrange("p (a b) -> p a b", a=QUADS)
        pool_perm = scores[:, 0:P]
        quad_of = sb("quad_of", [P, QUADS])
        tile_of = sb("tile_of", [P, OCT])
        iota_j = sb("iota_j", [P, DEG])
        iota_ji = sb("iota_ji", [P, DEG], I32)
        node_i = sb("node_i", [P, ITS], I32)
        node_f = sb("node_f", [P, ITS])
        eps = sb("eps", [P, 1])
        wtab = sb("wtab", [D + 1, ROW])
        wlin = sb("wlin", [D, D])
        ff_diag = sb("ff_diag", [P, P])
        pma_diag = sb("pma_diag", [P, P])
        vo_diag = sb("vo_diag", [P, P])
        seed_u = sb("seed_u", [P, 38])
        mats = {n: sb(n, [D, D]) for n in ("enc_out", "p_out", "p_ff", "d_out", "d_ff", "wvo2", "wvo3")}
        borrowed = probs_diag[:, :, :, :].rearrange("p b t n -> p (b t n)")
        wraw = borrowed[0:D + 1, 0:3 * D]
        p_in = borrowed[0:D, 3 * D:6 * D]
        d_in = borrowed[0:D, 6 * D:9 * D]
        wqT = borrowed[0:D, 9 * D:10 * D + 1]
        wkT = borrowed[0:D, 11 * D:12 * D]
        wvT2, wo2, wkT2, wide, wv23 = (
            borrowed[0:D, i * D:(i + 2) * D].rearrange("p (a b) -> p a b", a=2) for i in range(12, 22, 2))
        cols = sb("cols", [P, 24])
        COLS = ["b_lin", "ff_b", "pma_b", "seed", "bq2", "bk2", "bv2", "bo2", "bff2", "bv3", "bo3", "bff3",
                "qs", "b1", "b3", "c2", "bv1", "bo1"]
        col = {n: i for i, n in enumerate(COLS)}

        def c_(n, rows_=D):
            return cols[0:rows_, col[n]:col[n] + 1]

        count1 = sb("count1", [P, 2, HALF])
        row_f = sb("row_f", [P, 2, HALF])
        below = sb("below", [P, 2, HALF])
        start_f = sb("start_f", [P, 2, HALF])
        counts_b = sb("counts_b", [P, ITS], BF16)
        starts = sb("starts", [P, ITS + 1])
        sample_own = sb("sample_own", [125, PER_ROW])
        counts = sb("counts", [P, ITS])
        win_idx = sb("win_idx", [P, 2, HALF], I32)
        sidx = sb("sidx", [P, 2, HALF], I32)

        windows = gathered_all[:, 0:2 * HALF * WINDOW].rearrange("p (h n) -> p h n", h=2)
        hflat = hT[:, :, :].rearrange("p s n -> p (s n)")
        trow = hflat[:, 0:2 * CHUNK * ROW].rearrange("p (b n) -> p b n", b=2)
        xflat = xp_rows[:, :, :].rearrange("p s n -> p (s n)")
        dst_f = xflat[0:125, 0:BLOCK]
        dst_i = dst_f.bitcast(I32)
        src_win = xflat[:, BLOCK:BLOCK + 2 * HALF * DEG].bitcast(I32).rearrange("p (h n) -> p h n", h=2)
        src_slots = xflat[:, BLOCK + 2 * HALF * DEG:BLOCK + 4 * HALF * DEG].bitcast(I32).rearrange(
            "p (h n) -> p h n", h=2)
        spare = 2 * CHUNK * ROW
        flags2 = [hflat[:, spare + i * WINDOW:spare + (i + 1) * WINDOW] for i in range(2)]
        flags1 = [hflat[:, spare + 2 * WINDOW:spare + 2 * WINDOW + SAMPLES],
                  probs[:, :, :].rearrange("p s n -> p (s n)")[:, 0:SAMPLES]]
        xin = qT[:, :, :].rearrange("p s n -> p (s n)")[:, 0:2 * CHUNK * D].rearrange(
            "p (b t n) -> p b t n", b=2, t=CHUNK)
        xinT = avT[:, :, :].rearrange("p s n -> p (s n)")[0:D, 0:CHUNK * P]
        nodeT = h2[:, :, :].rearrange("p s n -> p (s n)")[0:D + 1, 0:CHUNK * P]
        sample_f = xb[:, :, :].rearrange("p s n -> p (s n)")[:, 0:SAMPLES]

        ps = ctx.enter_context(nc.psum_tensor("ps", [P, 8, 512], F32))
        B_Q, B_HX, B_S, B_AV, B_FF, B_POOL, B_SEED = 0, 1, 2, 4, 5, 6, 7
        ps_scores = ps[:, B_S:B_S + 2, :].rearrange("p h n -> p (h n)").rearrange("p (h n) -> p h n", h=2)[:, :, 0:256]
        ps_seed = ps[:, B_SEED, 0:P]
        ps_seedT = ps[:, B_POOL, P:2 * P]
        ps_fin = ps[:, B_POOL, 2 * P:3 * P]
        psf = ps[:, :, :].rearrange("p b n -> p (b n)")
        ps_xT = psf[0:D, 0:CHUNK * P]
        ps_node = psf[0:D, 1024:1024 + CHUNK * P]
        ps_row = psf[:, 2048:2048 + CHUNK * ROW]

        w_in = sem("w_in")
        dst_in = sem("dst_in")
        dst_cast = sem("dst_cast")
        dst_out = sem("dst_out")
        samples_in = sem("samples_in")
        pad_out = sem("pad_out")
        x_in = [sem("x_in0"), sem("x_in1")]
        tab_out = [sem("tab_out0"), sem("tab_out1")]
        x_tail = sem("x_tail")
        rows_in = sem("rows_in")
        out_done = sem("out_done")
        pool_cst = sem("pool_cst")
        pool_zero = sem("pool_zero")
        dve_zero = sem("dve_zero")
        dve_chain = sem("dve_chain")
        prep = sem("prep")
        prep_pe = sem("prep_pe")
        nodes_f = sem("nodes_f")
        t_xT = sem("t_xT")
        t_xTc = sem("t_xTc")
        t_node = sem("t_node")
        t_nodec = sem("t_nodec")
        t_row = sem("t_row")
        t_rowc = sem("t_rowc")
        sampled = sem("sampled")
        win_in = [sem("win_in0"), sem("win_in1")]
        win_idx_ready = sem("win_idx_ready")
        searched = sem("searched")
        swin_in = [sem("swin_in0"), sem("swin_in1")]
        sidx_ready = sem("sidx_ready")
        row_ok = sem("row_ok")
        start_ok = sem("start_ok")
        src_turned = sem("src_turned")
        start_kept, src_kept = sem("start_kept"), sem("src_kept")
        counts_read = sem("counts_read")
        shifted = sem("shifted")
        permuted = sem("permuted")
        counted = sem("counted")

        g_in = [sem(f"g_in{i}") for i in range(RING)]
        idx_ready = sem("idx_ready")
        q_ps, h_ps, q_sb, h_sb = sem("q_ps"), sem("h_ps"), sem("q_sb"), sem("h_sb")
        s_ps = sem("s_ps")
        mask_ok, s_sb, s_top, s_diff = sem("mask_ok"), sem("s_sb"), sem("s_top"), sem("s_diff")
        p_exp, p_sum, p_share, p_norm, p_diag = sem("p_exp"), sem("p_sum"), sem("p_share"), sem("p_norm"), sem("p_diag")
        av_sb, vo_ps = sem("av_sb"), sem("vo_ps")
        av_ps, h2_sb, ff_ps, xb_sb, pma_ps, xp_sb = (sem("av_ps"), sem("h2_sb"), sem("ff_ps"), sem("xb_sb"),
                                                     sem("pma_ps"), sem("xp_sb"))
        back_ps, back_sb, seed_ps = sem("back_ps"), sem("back_sb"), sem("seed_ps")
        m2_cmp, m2_ok, s2_sb, s2_top, s2_diff = (sem("m2_cmp"), sem("m2_ok"), sem("s2_sb"), sem("s2_top"),
                                                 sem("s2_diff"))
        p2_exp, p2_sum, p2_share, p2_norm = sem("p2_exp"), sem("p2_sum"), sem("p2_share"), sem("p2_norm")
        seedT_ps, weights2_ok, pool_ps, pool_own, pooled_ok = (sem("seedT_ps"), sem("weights2_ok"), sem("pool_ps"),
                                                               sem("pool_own"), sem("pooled_ok"))
        fin_ps = sem("fin_ps")
        pooledT_ok, hid1_ok, pvec_ok, hid2_ok, dec_ok, decr_ok = (
            sem("pooledT_ok"), sem("hid1_ok"), sem("pvec_ok"), sem("hid2_ok"), sem("dec_ok"), sem("decr_ok"))
        y_ok, stats_ok = sem("y_ok"), sem("stats_ok")
        pe_passed, pool_passed, dve_passed = sem("pe_passed"), sem("pool_passed"), sem("dve_passed")
        ln_ok = sem("ln_ok")
        ln_std = sem("ln_std")
        normed = sem("normed")

        block = ctx.enter_context(nc.Block())

        def steps(eng, body):
            for t in range(LOOP_FROM):
                body(Step(0, t, OCTETS))
            with eng.Fori(0, GROUPS) as group:
                for k in range(RING):
                    body(Step(group, LOOP_FROM + k, OCTETS))
            for t in range(LOOP_TO, END + 1):
                body(Step(0, t, OCTETS))

        WEIGHT_LOADS = []

        def vec(name, lo=0, hi=D):
            return w[name][lo:hi].rearrange("(n o) -> n o", o=1)

        def load(dst_ap, src_ap):
            WEIGHT_LOADS.append((dst_ap, src_ap))

        load(wraw[0:D, :], w["enc_in_w"])
        load(wraw[D:D + 1, :], w["enc_in_b"].rearrange("(o n) -> o n", o=1))
        load(wlin[:, :], w["w_lin"])
        load(mats["enc_out"][:, :], w["enc_out_w"])
        load(p_in[:, :], w["pma_in_w"])
        load(d_in[:, :], w["dec_in_w"])
        load(mats["p_out"][:, :], w["pma_out_w"])
        load(mats["p_ff"][:, :], w["pma_ff_w"])
        load(mats["d_out"][:, :], w["dec_out_w"])
        load(mats["d_ff"][:, :], w["dec_ff_w"])
        load(c_("b_lin"), vec("b_lin"))
        load(c_("bv1"), vec("enc_in_b", 2 * D, 3 * D))
        load(c_("bo1"), vec("enc_out_b"))
        load(cols[D:P, col["bo1"]:col["bo1"] + 1], vec("enc_out_b"))
        load(c_("ff_b"), vec("enc_ff_b"))
        load(cols[D:P, col["ff_b"]:col["ff_b"] + 1], vec("enc_ff_b"))
        load(c_("pma_b"), vec("pma_lin_b"))
        load(cols[D:P, col["pma_b"]:col["pma_b"] + 1], vec("pma_lin_b"))
        load(c_("seed"), w["pma_seed"].rearrange("o n -> n o"))
        load(c_("bq2"), vec("pma_in_b"))
        load(c_("bk2"), vec("pma_in_b", D, 2 * D))
        load(c_("bv2"), vec("pma_in_b", 2 * D, 3 * D))
        load(c_("bo2"), vec("pma_out_b"))
        load(c_("bff2"), vec("pma_ff_b"))
        load(c_("bv3"), vec("dec_in_b", 2 * D, 3 * D))
        load(c_("bo3"), vec("dec_out_b"))
        load(c_("bff3"), vec("dec_ff_b"))
        DIAG_LOADS = [(ff_diag[0:D, 0:D], w["enc_ff_w"]), (ff_diag[D:P, D:P], w["enc_ff_w"]),
                      (pma_diag[0:D, 0:D], w["pma_lin_w"]), (pma_diag[D:P, D:P], w["pma_lin_w"])]
        ALL_WEIGHTS = 16 * (len(WEIGHT_LOADS) + len(DIAG_LOADS))

        @block.sync
        def _(sp):
            sp.dma_start(dst_i, dst.rearrange("(p n) -> p n", p=125)).then_inc(dst_in, 16)
            sp.dma_start(src_padded[0:E, :].rearrange("(p n) o -> p (n o)", p=P), src.rearrange("(p n) -> p n", p=P)
                         ).then_inc(pad_out, 16)
            sp.dma_start(src_padded[E:E + D, :].rearrange("n o -> o n"), src[0:D].rearrange("(o n) -> o n", o=1)
                         ).then_inc(pad_out, 16)
            early = 6
            for d_, s_ in WEIGHT_LOADS[:early]:
                sp.dma_start(d_, s_).then_inc(w_in, 16)
            sp.wait_ge(dst_cast, 1)
            sp.dma_start(dst_samples.rearrange("o (p n) -> (o p) n", p=125), sample_own[:, :]
                         ).then_inc(dst_out, 16)
            sp.wait_ge(dst_out, 16)
            sp.dma_start(sample_f, dst_samples.broadcast_to((P, SAMPLES))).then_inc(samples_in, 16)
            sp.wait_ge(dst_cast, 2)
            sp.dma_start(dst_rows.rearrange("(p n) m -> p (n m)", p=125), dst_f).then_inc(dst_out, 16)
            for d_, s_ in WEIGHT_LOADS[early:]:
                sp.dma_start(d_, s_).then_inc(w_in, 16)
            sp.wait_ge(dve_zero, 1)
            for d_, s_ in DIAG_LOADS:
                sp.dma_start(d_, s_).then_inc(w_in, 16)

            def load_chunk(c, b):
                sp.dma_start(xin[:, b], x[bass.ds(c * (CHUNK * P), CHUNK * P), :].rearrange(
                    "(t p) d -> p t d", p=P)).then_inc(x_in[b], 16)

            def store_chunk(c, b):
                sp.dma_start(table[bass.ds(c * (CHUNK * P), CHUNK * P), :].rearrange("(t p) n -> p t n", p=P),
                             trow[:, b].rearrange("p (t n) -> p t n", t=CHUNK)).then_inc(tab_out[b], 16)

            load_chunk(0, 0)
            load_chunk(1, 1)
            with sp.Fori(0, CHUNKS // 2 - 2) as g:
                for b in range(2):
                    sp.wait_ge(t_rowc, g * 2 + (b + 1))
                    store_chunk(g * 2 + b, b)
                    load_chunk(g * 2 + (b + 2), b)
            sp.wait_ge(t_rowc, CHUNKS - 3)
            store_chunk(CHUNKS - 4, 0)
            load_chunk(CHUNKS - 2, 0)
            sp.wait_ge(t_rowc, CHUNKS - 2)
            store_chunk(CHUNKS - 3, 1)
            base = (CHUNKS - 1) * CHUNK * P
            sp.dma_start(xin[0:LAST, 1, CHUNK - 1], x[N - LAST:N, :]).then_inc(x_tail, 16)
            sp.wait_ge(x_tail, 16)
            sp.dma_start(xin[:, 1, 0:CHUNK - 1], x[base:N - LAST, :].rearrange("(t p) d -> p t d", p=P)
                         ).then_inc(x_in[1], 16)
            for b in range(2):
                sp.wait_ge(t_rowc, CHUNKS - 1 + b)
                store_chunk(CHUNKS - 2 + b, b)
            sp.wait_ge(dve_zero, 2)
            for q in range(QUADS):
                sp.dma_start(rows[q::QUADS, 0:ITS - 1, :],
                             x[0:(ITS - 1) * P, :].rearrange("(m a b) d -> a b m d", a=QUADS, b=DEG)[q]
                             ).then_inc(rows_in, 16)
                n = min(max(LAST - q * DEG, 0), DEG)
                if n:
                    base = (ITS - 1) * P + q * DEG
                    sp.dma_start(rows[q:q + QUADS * (n - 1) + 1:QUADS, ITS - 1, :], x[base:base + n, :]
                                 ).then_inc(rows_in, 16)

            stores = 0
            for g in range(ITS // 14):
                sp.wait_ge(normed, g + 1)
                lo, hi = 14 * g, min(14 * (g + 1), ITS - 1)
                for q in range(QUADS):
                    sp.dma_start(out[lo * P:hi * P, :].rearrange("(m a b) d -> a b m d", a=QUADS, b=DEG)[q],
                                 rows[q::QUADS, lo:hi, :]).then_inc(out_done, 16)
                    stores += 1
                    n = min(max(LAST - q * DEG, 0), DEG)
                    if hi == ITS - 1 and n:
                        base = (ITS - 1) * P + q * DEG
                        sp.dma_start(out[base:base + n, :], rows[q:q + QUADS * (n - 1) + 1:QUADS, ITS - 1, :]
                                     ).then_inc(out_done, 16)
                        stores += 1
            sp.wait_ge(out_done, 16 * stores)

        ROWS_LOADED = 16 * (QUADS + sum(1 for q in range(QUADS) if LAST > q * DEG))

        @block.gpsimd
        def _(pool):
            nc.gpsimd.iota(node_i[:, :], [[P, ITS]], 0, 1).then_inc(pool_cst, 1)
            nc.gpsimd.iota(iota_ji[:, :], [[1, DEG]], 0, 0).then_inc(pool_cst, 1)
            for t in (ident[:, :], shift, seed_perm, pool_perm):
                nc.gpsimd.memset(t, 0.0).then_inc(pool_zero, 1)
            pool.wait_ge(pool_zero, 4)

            def one_where_zero(view, pattern, base, mult=1):
                nc.gpsimd.affine_select(out=view, in_=view, compare_op=ALU.not_equal, fill=1.0, base=base,
                                        pattern=pattern, channel_multiplier=mult).then_inc(pool_cst, 1)

            one_where_zero(ident[:, :], [[-1, P]], 0)
            one_where_zero(shift[:, 0, :], [[-1, P]], -1)
            one_where_zero(shift[:, 1, :], [[1, P]], -(P - 1), P)
            for q in range(QUADS):
                one_where_zero(seed_perm[:, q, :].rearrange("p (c r) -> p c r", c=QUADS)[:, :, 0:OCT],
                               [[-OCT, QUADS], [-1, OCT]], -DEG * q)
                one_where_zero(pool_perm.rearrange("p (b a) -> p a b", a=QUADS)[:, q, :],
                               [[-1, DEG]], -DEG * q)

            def gather_windows(table_ap, size, index, target, h, landed):
                for t in range(HALF):
                    pool.indirect_dma_start(
                        out=target[:, h, t * size:(t + 1) * size], out_offset=None, in_=table_ap,
                        in_offset=bass.IndirectOffsetOnAxis(ap=index[:, h, t:t + 1], axis=0),
                    ).then_inc(landed[h], 16)

            pool.wait_ge(dst_out, 32)
            for h in range(2):
                pool.wait_ge(win_idx_ready, h + 1)
                gather_windows(dst_rows, WINDOW, win_idx, windows, h, win_in)
            pool.wait_ge(pad_out, 32)
            with pool.Fori(0, SEARCHES // 2 - 1) as g:
                for h in range(2):
                    wait_apart(pool, sidx_ready, g * 2 + (h + 1), pool_passed)
                    gather_windows(src_padded, DEG, sidx, src_win, h, swin_in)
                    wait_apart(pool, win_idx_ready, g * 2 + (h + 3), pool_passed)
                    gather_windows(dst_rows, WINDOW, win_idx, windows, h, win_in)
            for h in range(2):
                pool.wait_ge(sidx_ready, SEARCHES - 1 + h)
                gather_windows(src_padded, DEG, sidx, src_win, h, swin_in)

            pool.wait_ge(idx_ready, RING)
            pool.wait_ge(tab_out[0], 16 * (CHUNKS // 2))
            pool.wait_ge(tab_out[1], 16 * (CHUNKS // 2))

            def step(s):
                if not s.has(0):
                    return
                wait_apart(pool, av_ps, s.octet(RING - 1), pool_passed)
                wait_apart(pool, idx_ready, s.octet(-1), pool_passed)
                for t in range(OCT):
                    pool.indirect_dma_start(
                        out=gathered[:, s.slot(0, RING), t * ROW:(t + 1) * ROW], out_offset=None, in_=table,
                        in_offset=bass.IndirectOffsetOnAxis(ap=idx[:, s.slot(0, RING), t:t + 1], axis=0),
                    ).then_inc(g_in[s.slot(0, RING)], 16)

            steps(pool, step)

        @block.tensor
        def _(pe):
            pe.wait_ge(w_in, ALL_WEIGHTS)
            pe.wait_ge(prep, 1)
            pe.transpose(ps[0:D, 0, 0:D + 1], wraw[:, 0:D], ident[0:D + 1, 0:D + 1]).then_inc(prep_pe, 1)
            pe.transpose(ps[0:D, 1, 0:D], wraw[0:D, D:2 * D], ident[0:D, 0:D]).then_inc(prep_pe, 1)
            pe.transpose(ps[0:D, 2, 0:D], wraw[0:D, 2 * D:3 * D], ident[0:D, 0:D]).then_inc(prep_pe, 1)
            pe.transpose(ps[0:D, 3, 0:D], p_in[:, D:2 * D], ident[0:D, 0:D]).then_inc(prep_pe, 1)
            pe.matmul(ps[0:D, 4, 0:1], p_in[:, 0:D], c_("seed"), start=True, stop=True).then_inc(prep_pe, 1)
            pe.transpose(ps[0:D, 5, 0:D], p_in[:, 2 * D:3 * D], ident[0:D, 0:D]).then_inc(prep_pe, 1)
            pe.transpose(ps[0:D, 6, 0:D], d_in[:, 2 * D:3 * D], ident[0:D, 0:D]).then_inc(prep_pe, 1)
            pe.wait_ge(prep, 2)

            def both(t):
                return t.rearrange("p a b -> p (a b)")

            pe.matmul(ps[0:D + 1, 0, 0:D], wqT, wkT, start=True, stop=True).then_inc(prep_pe, 1)
            pe.matmul(ps[:, 1, 0:D], both(wvT2), mats["enc_out"][:, :], start=True, stop=True).then_inc(prep_pe, 1)
            pe.matmul(ps[:, 2, 0:1], both(wo2), c_("bv1"), start=True, stop=True).then_inc(prep_pe, 1)
            pe.matmul(ps[:, 3, 0:1], both(wkT2), c_("qs"), start=True, stop=True).then_inc(prep_pe, 1)
            pe.matmul(ps[:, 4, 0:1], both(wide), c_("bk2"), start=True, stop=True).then_inc(prep_pe, 1)
            pe.matmul(ps[0:D, 5, 0:1], mats["p_out"][:, :], c_("bv2"), start=True, stop=True).then_inc(prep_pe, 1)
            pe.matmul(ps[0:D, 6, 0:1], mats["d_out"][:, :], c_("bv3"), start=True, stop=True).then_inc(prep_pe, 1)
            pe.matmul(ps[0:D, 7, 0:D], wv23[:, 0, :], mats["p_out"][:, :], start=True, stop=True).then_inc(prep_pe, 1)
            pe.matmul(ps[0:D, 7, D:2 * D], wv23[:, 1, :], mats["d_out"][:, :], start=True, stop=True
                      ).then_inc(prep_pe, 1)
            pe.wait_ge(prep, 3)

            with pe.Fori(0, CHUNKS // 2) as g:
                for b in range(2):
                    n = g * 2 + (b + 1)
                    wait_apart(pe, x_in[b], g * 16 + 16, pe_passed)
                    for t in range(CHUNK):
                        mm = pe.transpose(ps_xT[:, t * P:(t + 1) * P], xin[:, b, t, :], ident[:, :])
                    mm.then_inc(t_xT, 1)
                    wait_apart(pe, t_xTc, n, pe_passed)
                    pe.matmul(ps_node[:, 0:512], wlin[:, :], xinT[:, 0:512], start=True, stop=True)
                    pe.matmul(ps_node[:, 512:CHUNK * P], wlin[:, :], xinT[:, 512:CHUNK * P], start=True, stop=True
                              ).then_inc(t_node, 1)
                    wait_apart(pe, t_nodec, n, pe_passed)
                    for t in range(CHUNK):
                        mm = pe.matmul(ps_row[:, t * ROW:(t + 1) * ROW], nodeT[:, t * P:(t + 1) * P], wtab[:, :],
                                       start=True, stop=True)
                    mm.then_inc(t_row, 1)

            pe.wait_ge(start_kept, SEARCHES)
            pe.wait_ge(t_rowc, CHUNKS)
            pe.matmul(ps[:, 0, 0:ITS], shift[:, 0, :], starts[:, 0:ITS], start=True, stop=False)
            pe.matmul(ps[:, 0, 0:ITS], shift[:, 1, :], starts[:, 1:ITS + 1], start=False, stop=True
                      ).then_inc(shifted, 1)
            pe.wait_ge(counted, 1)
            for q in range(QUADS):
                pe.matmul(ps[:, 1, q * P:q * P + ITS], seed_perm[:, q, :], counts[:, :], start=True, stop=True)
            pe.matmul(ps[:, 2, 0:ITS], pool_perm, counts[:, :], start=True, stop=True).then_inc(permuted, 1)
            pe.wait_ge(counts_read, 1)

            def turn(s, c, bank):
                for p in range(PAIRS):
                    lo = 2 * p * ROW + c
                    mm = pe.transpose(ps[:, bank, p * P:(p + 1) * P],
                                      gathered[:, s.slot(0, RING), lo:lo + 2 * ROW - 1:2], ident[:, :])
                return mm

            def step(s):
                if s.has(0):
                    wait(pe, q_sb, s.octet(0))
                    pe.wait_ge(g_in[s.slot(0, RING)], s.round(0) * (16 * OCT) + 16 * OCT)
                    turn(s, 0, B_Q).then_inc(q_ps, 1)
                    if s.has(L_BACK + 1):
                        wait(pe, back_sb, s.octet(L_BACK))
                    else:
                        wait(pe, h_sb, s.octet(0))
                    turn(s, 1, B_HX).then_inc(h_ps, 1)
                if s.has(L_PMA):
                    wait(pe, xb_sb, s.octet(L_PMA - 1))
                    pe.matmul(ps[:, B_FF, :], pma_diag[:, :], xb[:, s.slot(L_PMA, 2), :], start=True, stop=True
                              ).then_inc(pma_ps, 1)
                if s.has_iteration(L_DEC1):
                    fin_op(s, L_DEC1, pooled_ok, ps_fin[0:D, :], pooled, ident)
                if s.has_iteration(L_DEC2):
                    fin_op(s, L_DEC2, hid1_ok, ps_fin[0:D, :], mats["p_ff"], hid1)
                if s.has_iteration(L_OUT):
                    fin_op(s, L_OUT, hid2_ok, ps_fin[0:D, :], mats["d_ff"], hid2)
                if s.has_iteration(L_WEIGHTS):
                    wait(pe, p2_norm, s.iteration(L_WEIGHTS) + 1)
                    pe.transpose(ps_seedT, scores2[:, :], ident[:, :]).then_inc(seedT_ps, 1)
                if s.has(L_ATTEND):
                    if s.slot(L_ATTEND, 2) == 0:
                        wait(pe, p_diag, s.batch(L_ATTEND) * 4 + 4)
                    wait(pe, h2_sb, s.octet(L_ATTEND))
                    for p in range(PAIRS):
                        for h in range(2):
                            lo = (2 * p + h) * ROW + 1
                            mm = pe.matmul(ps[D * h:D * h + D, B_AV, p * P:(p + 1) * P],
                                           gathered[:, s.slot(L_ATTEND, RING), lo:lo + ROW - 1:2],
                                           probs_diag[:, s.slot(L_ATTEND, 4) // 2,
                                                      OCT * h + PAIRS * s.slot(L_ATTEND, 2) + p, :],
                                           start=True, stop=True)
                    mm.then_inc(av_ps, 1)
                if s.has(L_SCORES):
                    if s.slot(L_SCORES, 2) == 0:
                        wait(pe, s_sb, s.batch(L_SCORES))
                    wait(pe, q_sb, s.octet(L_SCORES - 1))
                    wait_apart(pe, h_sb, s.octet(L_SCORES - 1), pe_passed)
                    par = s.slot(L_SCORES, 2)
                    for p in range(PAIRS):
                        for q in range(QUADS):
                            for h in range(2):
                                lo = p * P + DEG * q
                                hi = D * h
                                mm = pe.matmul(
                                    ps[DEG * q:DEG * q + DEG, B_S + h, (PAIRS * par + p) * DEG:(PAIRS * par + p + 1) * DEG],
                                    qT[hi:hi + D, par, lo:lo + DEG],
                                    hT[hi:hi + D, s.slot(L_SCORES, RING), lo:lo + DEG],
                                    start=True, stop=True)
                    mm.then_inc(s_ps, 1)
                if s.has_iteration(L_POOL):
                    wait(pe, weights2_ok, s.iteration(L_POOL) + 1)
                    wait(pe, y_ok, s.iteration(L_POOL))
                    wait(pe, back_sb, s.octet(L_POOL - OCTS_PER_IT))
                    for c in range(OCTS_PER_IT):
                        mm = pe.matmul(ps[DEG * c:DEG * c + DEG, B_POOL, :],
                                       weights2[:, c].rearrange("p t a -> p (t a)"),
                                       xp_rows[:, (s.slot(L_POOL, RING) + c) % RING, :], start=True, stop=True)
                    mm.then_inc(pool_ps, 1)
                if s.has(L_FF):
                    wait(pe, xp_sb, s.octet(L_FF))
                    wait(pe, h2_sb, s.octet(L_FF - 1))
                    pe.matmul(ps[:, B_FF, :], ff_diag[:, :], h2[:, s.slot(L_FF, 2), :], start=True, stop=True
                              ).then_inc(ff_ps, 1)
                if s.has(L_ATTEND):
                    wait(pe, av_sb, s.octet(L_ATTEND - 1))
                    pe.matmul(ps[:, B_AV, :], vo_diag[:, :], avT[:, s.slot(L_ATTEND, 2), :], start=True, stop=True
                              ).then_inc(vo_ps, 1)
                if s.has_iteration(L_DEC1):
                    fin_op(s, L_DEC1, pooledT_ok, ps_fin[0:D, :], mats["wvo2"], pooledT)
                if s.has_iteration(L_DEC2):
                    fin_op(s, L_DEC2, pvec_ok, ps_fin[0:D, :], mats["wvo3"], pvec)
                if s.has_iteration(L_OUT):
                    if s.has_iteration(L_WEIGHTS):
                        wait(pe, weights2_ok, s.iteration(L_WEIGHTS) + 1)
                    fin_op(s, L_OUT, decr_ok, ps_fin[:, 0:D], decr, ident)
                if s.has(L_BACK):
                    if s.has(0):
                        wait(pe, h_sb, s.octet(-1))
                    else:
                        wait(pe, back_sb, s.octet(L_BACK))
                    wait(pe, xp_sb, s.octet(L_BACK - 1))
                    for p in range(PAIRS):
                        mm = pe.transpose(ps[:, B_HX, p * P:(p + 1) * P],
                                          xp[:, s.slot(L_BACK, 2), p * P:(p + 1) * P], ident[:, :])
                    mm.then_inc(back_ps, 1)
                    c = s.slot(L_BACK, OCTS_PER_IT)
                    if c == 0:
                        wait(pe, s2_sb, s.iteration(L_BACK))
                    for p in range(PAIRS):
                        mm = pe.matmul(ps_seed[DEG * c:DEG * c + DEG, :], seed_u[:, 6 - 2 * p:38 - 2 * p],
                                       xp[:, s.slot(L_BACK, 2), p * P:(p + 1) * P],
                                       start=(p == 0), stop=(p == PAIRS - 1))
                    mm.then_inc(seed_ps, 1)
            def fin_op(s, lag, ready, out_, lhs, rhs):
                wait_apart(pe, ready, s.iteration(lag) + 1, pe_passed)
                if rhs is ident:
                    mm = pe.transpose(out_, lhs[:, :], rhs[0:lhs.shape[0], 0:lhs.shape[0]])
                else:
                    mm = pe.matmul(out_, lhs[:, :], rhs[:, :], start=True, stop=True)
                mm.then_inc(fin_ps, 1)

            steps(pe, step)

        @block.scalar
        def _(act):
            def copy(o, i):
                return nc.scalar.activation(o, i, ACT.Copy)

            act.wait_ge(dst_in, 16)
            copy(sample_own[:, :], dst_i[:, 0:BLOCK:WINDOW]).then_inc(dst_cast, 1)
            act.wait_ge(dst_cast, 1)
            copy(dst_f, dst_i).then_inc(dst_cast, 1)
            act.wait_ge(w_in, ALL_WEIGHTS)
            act.wait_ge(dve_zero, 1)

            def table_chunk(g, b):
                n = g * 2 + (b + 1)
                act.wait_ge(t_xT, n)
                copy(xinT, ps_xT).then_inc(t_xTc, 1)
                act.wait_ge(t_node, n)
                nc.scalar.activation(nodeT[0:D, :], ps_node, ACT.Identity, bias=c_("b_lin")).then_inc(t_nodec, 1)
                act.wait_ge(t_row, n)
                wait(act, tab_out[b], g * 16)
                copy(trow[:, b, :], ps_row).then_inc(t_rowc, 1)

            table_chunk(0, 0)
            table_chunk(0, 1)
            with act.Fori(1, CHUNKS // 2) as g:
                table_chunk(g, 0)
                table_chunk(g, 1)

            def step(s):
                if s.has(0):
                    act.wait_ge(q_ps, s.octet(-1))
                    wait(act, s_ps, s.octet(1))
                    copy(qT[:, s.slot(0, 2), :], ps[:, B_Q, :]).then_inc(q_sb, 1)
                    act.wait_ge(h_ps, s.octet(-1))
                    wait(act, h2_sb, s.octet(RING - 1))
                    copy(hT[:, s.slot(0, RING), :], ps[:, B_HX, :]).then_inc(h_sb, 1)
                if s.has_iteration(L_DEC2):
                    wait(act, fin_ps, s.iteration(L_DEC2) * 6 + 2)
                    nc.scalar.activation(hid1[:, :], ps_fin[0:D, :], ACT.Identity, bias=c_("b1")).then_inc(hid1_ok, 1)
                if s.has_iteration(L_OUT):
                    wait(act, fin_ps, s.iteration(L_OUT) * 6 + 4)
                    nc.scalar.activation(hid2[:, :], ps_fin[0:D, :], ACT.Identity, bias=c_("b3")).then_inc(hid2_ok, 1)
                if s.has_iteration(L_SEED_T):
                    wait(act, s2_diff, s.iteration(L_SEED_T) + 1)
                    nc.scalar.activation(scores2[:, :], scores2[:, :], ACT.Exp).then_inc(p2_exp, 1)
                if s.has(L_PMA):
                    act.wait_ge(pma_ps, s.octet(L_PMA - 1))
                    wait(act, seed_ps, s.octet(L_PMA + 1))
                    nc.scalar.activation(xp[:, s.slot(L_PMA, 2), :], ps[:, B_FF, :], ACT.Relu,
                                         bias=c_("pma_b", P)).then_inc(xp_sb, 1)
                if s.has(L_ATTEND):
                    act.wait_ge(av_ps, s.octet(L_ATTEND - 1))
                    wait(act, vo_ps, s.octet(L_ATTEND + 1))
                    copy(avT[:, s.slot(L_ATTEND, 2), :], ps[:, B_AV, :]).then_inc(av_sb, 1)
                if s.has_batch(L_SOFTMAX):
                    wait(act, s_diff, s.batch(L_SOFTMAX) + 1)
                    wait(act, p_diag, s.batch(L_SOFTMAX + 2) * 4)
                    nc.scalar.activation(probs[:, s.slot(L_SOFTMAX, 4) // 2, :], scores[:, :], ACT.Exp
                                         ).then_inc(p_exp, 1)
                if s.has_iteration(L_DEC1):
                    wait(act, fin_ps, s.iteration(L_DEC1) * 6 + 1)
                    copy(pooledT[:, :], ps_fin[0:D, :]).then_inc(pooledT_ok, 1)
                if s.has(L_BACK):
                    act.wait_ge(back_ps, s.octet(L_BACK - 1))
                    wait(act, pool_ps, s.iteration(L_BACK) - 1)
                    copy(xp_rows[:, s.slot(L_BACK, RING), :], ps[:, B_HX, :]).then_inc(back_sb, 1)

            steps(act, step)
            act.wait_ge(ln_ok, 5)
            nc.scalar.activation(lnv[:, 3, :], lnv[:, 2, :], ACT.Sqrt, bias=eps[:, 0:1], scale=1.0).then_inc(ln_std, 1)

        @block.vector
        def _(dve):
            V = nc.vector
            chained = [0]

            def link(ins):
                chained[0] += 1
                ins.then_inc(dve_chain, 1)
                dve.wait_ge(dve_chain, chained[0])

            V.memset(ff_diag[:, :], 0.0)
            V.memset(pma_diag[:, :], 0.0)
            V.memset(vo_diag[:, :], 0.0)
            V.memset(wtab[:, :], 0.0)
            link(V.memset(nodeT[D:D + 1, :], 1.0))
            V.memset(xin[:, :, :, :], 0.0).then_inc(dve_zero, 1)
            V.memset(seed_u[:, :], 0.0)
            V.memset(idx_all[:, ITS * DEG:], 0)
            V.memset(starts[:, ITS:ITS + 1], float(E))
            V.memset(eps[:, :], EPS)
            V.memset(rows[:, ITS - 1, :], 0.0).then_inc(dve_zero, 1)
            dve.wait_ge(pool_cst, 2)
            V.tensor_copy(iota_j[:, :], iota_ji[:, :])
            link(V.tensor_copy(node_f[:, :], node_i[:, :]))

            def rows_of_group(g, h):
                for t in range(HALF):
                    wait(dve, sampled, g * HALF + (t - 1))
                    V.tensor_scalar(flags1[(h * HALF + t) % 2], sample_f, node_f[:, bass.ds(g * HALF + t, 1)], None, ALU.is_lt, ALU.add,
                                    accum_out=count1[:, h, t:t + 1]).then_inc(sampled, 1)
                dve.wait_ge(sampled, g * HALF + HALF)
                V.tensor_scalar(row_f[:, h, :], count1[:, h, :], -1.0, 0.0, ALU.add, ALU.max).then_inc(row_ok, 1)
                dve.wait_ge(row_ok, g + 1)
                V.tensor_copy(win_idx[:, h, :], row_f[:, h, :]).then_inc(win_idx_ready, 1)

            def starts_of_group(g, h, rounds):
                dve.wait_ge(win_in[h], rounds * (16 * HALF) + 16 * HALF)
                for t in range(HALF):
                    wait(dve, searched, g * HALF + (t - 1))
                    V.tensor_scalar(flags2[(h * HALF + t) % 2], windows[:, h, t * WINDOW:(t + 1) * WINDOW],
                                    node_f[:, bass.ds(g * HALF + t, 1)], None, ALU.is_lt, ALU.add,
                                    accum_out=below[:, h, t:t + 1]).then_inc(searched, 1)
                dve.wait_ge(searched, g * HALF + HALF)
                V.scalar_tensor_tensor(start_f[:, h, :], row_f[:, h, :], float(WINDOW), below[:, h, :],
                                       ALU.mult, ALU.add).then_inc(start_ok, 1)
                dve.wait_ge(start_ok, g + 1)
                V.tensor_copy(sidx[:, h, :], start_f[:, h, :]).then_inc(sidx_ready, 1)
                V.tensor_copy(starts[:, bass.ds(g * HALF, HALF)], start_f[:, h, :]).then_inc(start_kept, 1)

            def indices_of_group(g, h, rounds):
                dve.wait_ge(swin_in[h], rounds * (16 * HALF) + 16 * HALF)
                V.transpose(src_slots[:, h, :], src_win[:, h, :]).then_inc(src_turned, 1)
                wait_apart(dve, src_turned, g + 1, dve_passed)
                V.tensor_copy(idx_all[:, bass.ds(g * (HALF * DEG), HALF * DEG)], src_slots[:, h, :]
                              ).then_inc(src_kept, 1)

            dve.wait_ge(samples_in, 16)
            rows_of_group(0, 0)
            rows_of_group(1, 1)

            marked = [0]

            def mark(ins):
                marked[0] += 1
                ins.then_inc(prep, 1)
                dve.wait_ge(prep, marked[0])

            dve.wait_ge(w_in, ALL_WEIGHTS)
            dve.wait_ge(pool_cst, 2 + 3 + 2 * QUADS)
            V.tensor_reduce(quad_of[:, :], ident[:, :].rearrange("p (a j) -> p a j", j=DEG), AX_X, ALU.add)
            V.tensor_reduce(tile_of[:, :], ident[:, :].rearrange("p (c t a) -> p t c a", c=QUADS, t=OCT),
                            mybir.AxisListType.XY, ALU.add)
            mark(V.tensor_copy(wtab[0:D, 1:ROW:2], ident[0:D, 0:D]))
            for t in (wo2[:, 0, :], wo2[:, 1, :]):
                V.tensor_copy(t, mats["enc_out"][:, :])
            dve.wait_ge(prep_pe, 7)
            V.tensor_copy(wqT, ps[0:D, 0, 0:D + 1])
            V.tensor_copy(wkT, ps[0:D, 1, 0:D])
            for i in range(2):
                V.tensor_copy(wvT2[:, i, :], ps[0:D, 2, 0:D])
                V.tensor_copy(wkT2[:, i, :], ps[0:D, 3, 0:D])
                V.tensor_copy(wv23[:, i, :], ps[0:D, 5 + i, 0:D])
            link(V.tensor_scalar(c_("qs"), ps[0:D, 4, 0:1], c_("bq2"), D ** -0.5, ALU.add, ALU.mult))
            mark(V.tensor_copy(wide.rearrange("p a b -> p (a b)"), c_("qs").broadcast_to((D, P))))
            dve.wait_ge(prep_pe, 16)
            V.tensor_scalar(wtab[:, 0:ROW:2], ps[0:D + 1, 0, 0:D], D ** -0.5, None, ALU.mult)
            V.tensor_copy(vo_diag[0:D, 0:D], ps[0:D, 1, 0:D])
            V.tensor_copy(vo_diag[D:P, D:P], ps[D:P, 1, 0:D])
            V.tensor_tensor(c_("bo1", P), ps[:, 2, 0:1], c_("bo1", P), ALU.add)
            V.tensor_copy(seed_u[0:D, 6:7], ps[0:D, 3, 0:1])
            V.tensor_copy(seed_u[D:P, 7:8], ps[D:P, 3, 0:1])
            V.tensor_copy(c_("c2", P), ps[:, 4, 0:1])
            V.tensor_tensor(c_("b3"), ps[0:D, 6, 0:1], c_("bo3"), ALU.add)
            link(V.tensor_tensor(c_("b1"), ps[0:D, 5, 0:1], c_("bo2"), ALU.add))
            link(V.tensor_tensor(c_("b1"), c_("b1"), c_("seed"), ALU.add))
            for t, n in ((ff_diag, P), (mats["p_ff"], D), (mats["d_ff"], D)):
                V.tensor_tensor(t[:, :], t[:, :], ident[0:n, 0:n], ALU.add)
            V.tensor_copy(mats["wvo2"][:, :], ps[0:D, 7, 0:D])
            mark(V.tensor_tensor(mats["wvo3"][:, :], ps[0:D, 7, D:2 * D], ident[0:D, 0:D], ALU.add))

            link(V.memset(borrowed, 0.0))

            starts_of_group(0, 0, 0)
            rows_of_group(2, 0)
            starts_of_group(1, 1, 0)
            indices_of_group(0, 0, 0)
            rows_of_group(3, 1)
            with dve.Fori(1, SEARCHES // 2 - 1) as pair:
                for h in range(2):
                    g = pair * 2 + h
                    starts_of_group(g, h, pair)
                    indices_of_group(g - 1, 1 - h, pair - (1 - h))
                    rows_of_group(g + 2, h)
            for h in range(2):
                g = SEARCHES - 2 + h
                starts_of_group(g, h, g // 2)
                indices_of_group(g - 1, 1 - h, (g - 1) // 2)
            V.tensor_copy(idx[:, :, :].rearrange("p s t -> p (s t)"), idx_all[:, 0:RING * OCT]
                          ).then_inc(idx_ready, RING)
            dve.wait_ge(shifted, 1)
            V.tensor_tensor(counts[:, :], ps[:, 0, 0:ITS], starts[:, 0:ITS], ALU.subtract).then_inc(counted, 1)
            dve.wait_ge(counted, 1)
            link(V.tensor_scalar(counts_b[:, :], counts[:, :], float(DEG), None, ALU.min))
            V.transpose(count_slot[:, :].rearrange("p (m b) -> p m b", b=DEG),
                        counts_b[:, :].unsqueeze(2).broadcast_to((P, ITS, DEG)))
            dve.wait_ge(permuted, 1)
            for q in range(QUADS):
                V.tensor_copy(count_seed[:, :, q], ps[:, 1, q * P:q * P + ITS])
            V.tensor_scalar(nonempty[:, :], ps[:, 2, 0:ITS], 0.0, None, ALU.is_gt).then_inc(counts_read, 1)
            dve.wait_ge(counts_read, 1)
            indices_of_group(SEARCHES - 1, 1, SEARCHES // 2 - 1)
            dve.wait_ge(src_kept, SEARCHES)

            def by_slot(ap):
                return ap.rearrange("p (t j) -> p t j", j=DEG)

            iota_slots = iota_j[:, :].unsqueeze(1).broadcast_to((P, 2, DEG))

            def step(s):
                if s.has(L_H2):
                    wait(dve, vo_ps, s.octet(L_H2 - 1))
                    wait(dve, ff_ps, s.octet(L_H2 + 1))
                    V.scalar_tensor_tensor(h2[:, s.slot(L_H2, 2), :], ps[:, B_AV, :], c_("bo1", P),
                                           hT[:, s.slot(L_H2, RING), :], ALU.add, ALU.add).then_inc(h2_sb, 1)
                if s.has_batch(L_SOFTMAX):
                    n = s.batch(L_SOFTMAX)
                    dve.wait_ge(s_ps, s.octet(L_SOFTMAX - 2))
                    dve.wait_ge(mask_ok, n + 1)
                    wait(dve, p_exp, n)
                    V.scalar_tensor_tensor(scores[:, :].rearrange("p (h n) -> p h n", h=2),
                                           empty[:, :].rearrange("p (h n) -> p h n", h=2), MASKED, ps_scores,
                                           ALU.mult, ALU.add).then_inc(s_sb, 1)
                if s.has_iteration(L_Y):
                    y_rows(s)
                if s.has_iteration(L_SEED):
                    m = s.iteration(L_SEED)
                    dve.wait_ge(m2_ok, m + 1)
                    dve.wait_ge(seed_ps, s.octet(L_SEED - 4))
                    wait(dve, seedT_ps, m)
                    V.scalar_tensor_tensor(scores2[:, :], ps_seed, c_("c2", P), empty2[:, :], ALU.add, ALU.add
                                           ).then_inc(s2_sb, 1)
                if s.has_batch(L_SOFTMAX):
                    n = s.batch(L_SOFTMAX)
                    dve.wait_ge(s_sb, n + 1)
                    V.tensor_reduce(top[:, :], by_slot(scores[:, :]), AX_X, ALU.max).then_inc(s_top, 1)
                if s.has_batch(L_NORM):
                    pr = probs[:, s.slot(L_NORM, 4) // 2, :]
                    n = s.batch(L_NORM)
                    dve.wait_ge(p_exp, n + 1)
                    V.tensor_reduce(total[:, :], by_slot(pr), AX_X, ALU.add).then_inc(p_sum, 1)
                if s.has_batch(L_SOFTMAX):
                    dve.wait_ge(s_top, n + 1)
                    V.tensor_tensor(by_slot(scores[:, :]), by_slot(scores[:, :]),
                                    top[:, :].unsqueeze(2).broadcast_to((P, 16, DEG)), ALU.subtract
                                    ).then_inc(s_diff, 1)
                if s.has_batch(L_NORM):
                    dve.wait_ge(p_sum, n + 1)
                    V.reciprocal(share[:, :], total[:, :]).then_inc(p_share, 1)
                if s.has_iteration(L_DEC2):
                    m = s.iteration(L_DEC2)
                    wait(dve, fin_ps, m * 6 + 3)
                    V.scalar_tensor_tensor(pvec[:, :], ps_fin[0:D, :], c_("bff2"), hid1[:, :], ALU.add, ALU.max
                                           ).then_inc(pvec_ok, 1)
                if s.has_iteration(L_OUT):
                    out_rows(s)
                if s.has_iteration(L_WEIGHTS):
                    wait(dve, seedT_ps, s.iteration(L_WEIGHTS) + 1)
                    wait(dve, pool_ps, s.iteration(L_WEIGHTS))
                    V.tensor_tensor(
                        weights2[:, :, :, :],
                        ps_seedT.rearrange("p (c t) -> p c t", c=OCTS_PER_IT)[:, :, 0:OCT].unsqueeze(3).broadcast_to(
                            (P, OCTS_PER_IT, OCT, QUADS)),
                        quad_of[:, :].unsqueeze(1).unsqueeze(1).broadcast_to((P, OCTS_PER_IT, OCT, QUADS)),
                        ALU.mult).then_inc(weights2_ok, 1)
                if s.has_batch(L_NORM):
                    dve.wait_ge(p_share, n + 1)
                    V.tensor_tensor(by_slot(pr), by_slot(pr), share[:, :].unsqueeze(2).broadcast_to((P, 16, DEG)),
                                    ALU.mult).then_inc(p_norm, 1)
                if s.has(L_FF):
                    wait(dve, ff_ps, s.octet(L_FF - 1))
                    wait(dve, pma_ps, s.octet(L_FF + 1))
                    V.scalar_tensor_tensor(xb[:, s.slot(L_FF, 2), :], ps[:, B_FF, :], c_("ff_b", P),
                                           h2[:, s.slot(L_FF, 2), :], ALU.add, ALU.max).then_inc(xb_sb, 1)
                if s.has_batch(L_NORM):
                    dve.wait_ge(p_norm, n + 1)
                    wait(dve, av_ps, s.octet(L_NORM + 2))
                    for q in range(QUADS):
                        lo = DEG * q
                        V.transpose(probs_diag[lo:lo + DEG, s.slot(L_NORM, 4) // 2, :, lo:lo + DEG],
                                    pr[lo:lo + DEG, :].rearrange("p (t j) -> p t j", j=DEG)).then_inc(p_diag, 1)
                if s.has_iteration(L_MASK2):
                    m = s.iteration(L_MASK2)
                    wait(dve, s2_sb, m)
                    V.tensor_tensor(empty2[:, :].rearrange("p (a j) -> p a j", j=DEG),
                                    iota_j[:, :].unsqueeze(1).broadcast_to((P, QUADS, DEG)),
                                    count_seed[:, bass.ds(m, 1), :].rearrange("p m a -> p (m a)").unsqueeze(2)
                                    .broadcast_to((P, QUADS, DEG)), ALU.is_ge).then_inc(m2_cmp, 1)
                    dve.wait_ge(m2_cmp, m + 1)
                    V.tensor_scalar(empty2[:, :], empty2[:, :], MASKED, None, ALU.mult).then_inc(m2_ok, 1)
                if s.has_iteration(L_SEED):
                    m = s.iteration(L_SEED)
                    dve.wait_ge(s2_sb, m + 1)
                    V.tensor_reduce(top2[:, :], by_slot(scores2[:, :]), AX_X, ALU.max).then_inc(s2_top, 1)
                    dve.wait_ge(s2_top, m + 1)
                    V.tensor_tensor(by_slot(scores2[:, :]), by_slot(scores2[:, :]),
                                    top2[:, :].unsqueeze(2).broadcast_to((P, QUADS, DEG)), ALU.subtract
                                    ).then_inc(s2_diff, 1)
                if s.has_iteration(L_SEED_T):
                    m = s.iteration(L_SEED_T)
                    dve.wait_ge(p2_exp, m + 1)
                    V.tensor_reduce(total2[:, :], by_slot(scores2[:, :]), AX_X, ALU.add).then_inc(p2_sum, 1)
                    dve.wait_ge(p2_sum, m + 1)
                    V.reciprocal(share2[:, :], total2[:, :]).then_inc(p2_share, 1)
                    dve.wait_ge(p2_share, m + 1)
                    V.tensor_tensor(by_slot(scores2[:, :]), by_slot(scores2[:, :]),
                                    share2[:, :].unsqueeze(2).broadcast_to((P, QUADS, DEG)), ALU.mult
                                    ).then_inc(p2_norm, 1)
                if s.has_iteration(L_POOL):
                    m = s.iteration(L_POOL)
                    dve.wait_ge(pool_ps, m + 1)
                    V.tensor_tensor(pool_part[:, :].rearrange("p (t d) -> p t d", d=D),
                                    ps[:, B_POOL, :].rearrange("p (t d) -> p t d", d=D),
                                    tile_of[:, :].unsqueeze(2).broadcast_to((P, OCT, D)), ALU.mult
                                    ).then_inc(pool_own, 1)
                    dve.wait_ge(pool_own, m + 1)
                    wait(dve, fin_ps, m * 6 - 5 if s.looped or m > 0 else 0)
                    V.tensor_reduce(pooled[:, :], pool_part[:, :].rearrange("p (t d) -> p d t", d=D), AX_X, ALU.add
                                    ).then_inc(pooled_ok, 1)
                if s.has(0):
                    if s.looped or 1 <= s.at <= OCTETS - RING:
                        dve.wait_ge(g_in[s.slot(1, RING)], s.round(1) * (16 * OCT) + 16 * OCT)
                        V.tensor_copy(idx[:, s.slot(1, RING), :], idx_all[:, bass.ds(s.octet(1 - RING) * OCT, OCT)]
                                      ).then_inc(idx_ready, 1)

                if s.has_batch(L_MASK):
                    n = s.batch(L_MASK)
                    V.tensor_tensor(
                        empty[:, :].rearrange("p (h t j) -> p h t j", h=2, j=DEG),
                        iota_j[:, :].unsqueeze(1).unsqueeze(1).broadcast_to((P, 2, OCT, DEG)),
                        count_slot[:, bass.ds(n * 16, 16)].rearrange("p (t h) -> p h t", h=2).unsqueeze(3).broadcast_to(
                            (P, 2, OCT, DEG)), ALU.is_ge).then_inc(mask_ok, 1)

            def out_rows(s):
                m = s.iteration(L_OUT)
                if s.has_iteration(L_WEIGHTS):
                    dve.wait_ge(seedT_ps, s.iteration(L_WEIGHTS) + 1)
                dve.wait_ge(fin_ps, m * 6 + 5)
                V.scalar_tensor_tensor(dec[:, :], ps_fin[0:D, :], c_("bff3"), hid2[:, :], ALU.add, ALU.max
                                       ).then_inc(dec_ok, 1)
                dve.wait_ge(dec_ok, m + 1)
                V.tensor_scalar(decr[:, :], dec[:, :], 0.0, FLT_MAX, ALU.max, ALU.min).then_inc(decr_ok, 1)

            def y_rows(s):
                m = s.iteration(L_Y)
                dve.wait_ge(fin_ps, m * 6 + 6)
                row = rows[:, bass.ds(m, 1), :].rearrange("p m d -> p (m d)")
                V.scalar_tensor_tensor(row, ps_fin[:, 0:D], nonempty[:, bass.ds(m, 1)], row, ALU.mult, ALU.add
                                       ).then_inc(y_ok, 1)
                dve.wait_ge(y_ok, m + 1)
                V.bn_stats(stats[:, bass.ds(m, 1), :].rearrange("p m n -> p (m n)"), row).then_inc(stats_ok, 1)

            dve.wait_ge(rows_in, ROWS_LOADED)
            steps(dve, step)

            dve.wait_ge(stats_ok, ITS)
            mean, half, var, std, inv = (lnv[:, i, :] for i in range(5))
            V.tensor_tensor(mean, stats[:, :, 1], stats[:, :, 4], ALU.add).then_inc(ln_ok, 1)
            V.tensor_tensor(half, stats[:, :, 1], stats[:, :, 4], ALU.subtract).then_inc(ln_ok, 1)
            V.tensor_tensor(var, stats[:, :, 2], stats[:, :, 5], ALU.add).then_inc(ln_ok, 1)
            dve.wait_ge(ln_ok, 3)
            V.scalar_tensor_tensor(half, half, D / 4.0, half, ALU.mult, ALU.mult).then_inc(ln_ok, 1)
            V.tensor_scalar(mean, mean, 0.5, None, ALU.mult)
            dve.wait_ge(ln_ok, 4)
            link(V.tensor_tensor(var, var, half, ALU.add))
            V.tensor_scalar(var, var, 1.0 / D, None, ALU.mult).then_inc(ln_ok, 1)
            dve.wait_ge(ln_std, 1)
            link(V.reciprocal(inv, std))
            with dve.Fori(0, ITS // 14) as g:
                for k in range(14):
                    m = g * 14 + k
                    row = rows[:, bass.ds(m, 1), :].rearrange("p m d -> p (m d)")
                    ins = V.tensor_scalar(row, row, lnv[:, 0, bass.ds(m, 1)], lnv[:, 4, bass.ds(m, 1)],
                                          ALU.subtract, ALU.mult)
                ins.then_inc(normed, 1)


_OUT = (12500, 64)


def kernel(**inputs):
    import numpy as np
    import concourse.bacc as bacc
    from concourse.bass_utils import run_bass_kernel_spmd

    nc = bacc.Bacc("TRN2", target_bir_lowering=False, num_devices=1)
    arrays, args = {}, {}
    for name, value in inputs.items():
        arr = np.ascontiguousarray(value)
        arrays[f"in_{name}"] = arr
        args[name] = nc.dram_tensor(f"in_{name}", arr.shape, mybir.dt.from_np(arr.dtype), kind="ExternalInput").ap()
    out = nc.dram_tensor("out_rows", _OUT, F32, kind="ExternalOutput").ap()
    gnn_kernel(nc, args, out)
    r = run_bass_kernel_spmd(nc, [arrays], core_ids=[0])
    return r.results[0]["out_rows"]
```

```python
from contextlib import ExitStack

import concourse.bass as bass
from concourse import mybir

ALU = mybir.AluOpType
ACT = mybir.ActivationFunctionType
F32 = mybir.dt.float32
I32 = mybir.dt.int32
BF16 = mybir.dt.bfloat16
AX_X = mybir.AxisListType.X

P = 128
D = 64
DEG = 32
QUADS = P // DEG
OCT = 8
PAIRS = OCT // 2
OCTS_PER_IT = P // (QUADS * OCT)
RING = 8
ROW = 2 * D
MASKED = -3.0e38
FLT_MAX = 3.4028234663852886e38
EPS = 1e-5

SAMPLES = 625
HALF = 7
CHUNK = 7

L_SCORES = 1
L_MASK = 2
L_SOFTMAX = 3
L_NORM = 4
L_ATTEND = 5
L_H2 = 6
L_FF = 6
L_PMA = 7
L_BACK = 8
L_MASK2 = 11
L_SEED = 12
L_SEED_T = 13
L_WEIGHTS = 14
L_POOL = 15
L_DEC1 = 16
L_DEC2 = 17
L_OUT = 18
L_Y = 19


class Step:

    def __init__(self, group, at, octets):
        self.group, self.at, self.looped, self.octets = group, at, not isinstance(group, int), octets

    def octet(self, lag):
        return self.group * 8 + (self.at - lag)

    def batch(self, lag):
        return self.group * 4 + (self.at - lag) // 2

    def iteration(self, lag):
        return self.group * 2 + (self.at - lag) // 4

    def round(self, lag):
        return self.group + (self.at - lag) // RING

    def slot(self, lag, n):
        return (self.at - lag) % n

    def has(self, lag):
        return self.looped or 0 <= self.at - lag < self.octets

    def has_batch(self, lag):
        return (self.at - lag) % 2 == 0 and (self.looped or 0 <= self.at - lag < self.octets)

    def has_iteration(self, lag):
        return (self.at - lag) % 4 == 0 and (self.looped or 0 <= self.at - lag < self.octets)


def wait(eng, sem, count):
    if isinstance(count, int) and count <= 0:
        return
    eng.wait_ge(sem, count)


def wait_apart(eng, sem, count, passed):
    if isinstance(count, int) and count <= 0:
        return
    eng.wait_ge(sem, count)
    if not isinstance(count, int):
        eng.sem_inc(passed, 1)


def gnn_kernel(nc, a, out):
    x, src, dst = a["x"], a["src"], a["dst"]
    w = {k[len("L0_gnn_"):]: v for k, v in a.items() if k.startswith("L0_gnn_")}
    N, E = x.shape[0], src.shape[0]
    ITS = -(-N // P)
    NPAD = ITS * P
    LAST = N - (ITS - 1) * P
    OCTETS = ITS * OCTS_PER_IT
    WINDOW = E // SAMPLES
    CHUNKS = ITS // CHUNK
    assert x.shape[1] == D and SAMPLES * WINDOW == E and ITS % (2 * HALF) == 0 and ITS % (2 * CHUNK) == 0
    SEARCHES = ITS // HALF

    LOOP_FROM = L_Y + 1
    GROUPS = (OCTETS - LOOP_FROM) // RING - 2
    LOOP_TO = LOOP_FROM + RING * GROUPS
    END = OCTETS + L_Y
    EARLY = (LOOP_TO - 1 - L_Y) // OCTS_PER_IT + 1
    NORM_PARTS = 7
    PARTS = [(EARLY * i // NORM_PARTS, EARLY * (i + 1) // NORM_PARTS) for i in range(NORM_PARTS)] + [(EARLY, ITS)]
    assert LOOP_TO + 1 + 2 * NORM_PARTS < END

    with ExitStack() as ctx:
        def sb(name, shape, dt=F32):
            return ctx.enter_context(nc.sbuf_tensor(name, shape, dt))

        def sem(name):
            return ctx.enter_context(nc.semaphore(name))

        table = nc.dram_tensor("node_table", (NPAD, ROW), F32).ap()
        dst_rows = dst.rearrange("(r n) -> r n", n=WINDOW)
        dst_samples = nc.dram_tensor("dst_samples", (1, SAMPLES), I32).ap()
        src_padded = nc.dram_tensor("src_padded", (E + D, 1), I32).ap()

        gathered_all = sb("gathered", [P, max(RING * OCT * ROW, 2 * HALF * WINDOW)])
        gathered = gathered_all[:, 0:RING * OCT * ROW].rearrange("p (s n) -> p s n", s=RING)
        probs_diag = sb("probs_diag", [P, 2, 2 * OCT, P])
        qT = sb("qT", [P, 2, 512])
        avT = sb("avT", [P, 2, 512])
        hT = sb("hT", [P, RING, 512])
        h2 = sb("h2", [P, 2, 512])
        xb = sb("xb", [P, 2, 512])
        xp = sb("xp", [P, 2, 512])
        xp_rows = sb("xp_rows", [P, RING, 512])
        empty = sb("empty", [P, 512])
        scores = sb("scores", [P, 512])
        probs = sb("probs", [P, 2, 512])
        top = sb("top", [P, 16])
        total = sb("total", [P, 16])
        share = sb("share", [P, 16])
        idx = sb("idx", [P, RING, OCT], I32)
        idx_all = sb("idx_all", [P, ITS * DEG], I32)
        count_slot = sb("count_slot", [P, ITS * DEG], BF16)
        rows = sb("rows", [P, ITS, D])
        count_seed = sb("count_seed", [P, ITS, QUADS])
        empty2 = sb("empty2", [P, P])
        scores2 = sb("scores2", [P, P])
        top2 = sb("top2", [P, QUADS])
        total2 = sb("total2", [P, QUADS])
        share2 = sb("share2", [P, QUADS])
        weights2 = sb("weights2", [P, OCTS_PER_IT, OCT, QUADS])
        pool_part = sb("pool_part", [P, 512])
        pooled = sb("pooled", [P, D])
        pooledT = sb("pooledT", [D, P])
        hid1 = sb("hid1", [D, P])
        pvec = sb("pvec", [D, P])
        hid2 = sb("hid2", [D, P])
        dec = sb("dec", [D, P])
        decr = sb("decr", [D, P])
        stats = sb("stats", [P, ITS, 6])
        nonempty = sb("nonempty", [P, ITS])
        lnv = sb("lnv", [P, 5, ITS])

        ident = sb("ident", [P, P])
        shift = scores[:, P:3 * P].rearrange("p (a b) -> p a b", a=2)
        seed_perm = empty[:, :].rearrange("p (a b) -> p a b", a=QUADS)
        pool_perm = scores[:, 0:P]
        quad_of = sb("quad_of", [P, QUADS])
        tile_of = sb("tile_of", [P, OCT])
        iota_j = sb("iota_j", [P, DEG])
        iota_ji = sb("iota_ji", [P, DEG], I32)
        node_i = sb("node_i", [P, ITS], I32)
        node_f = sb("node_f", [P, ITS])
        eps = sb("eps", [P, 1])
        wtab = sb("wtab", [D + 1, ROW])
        wlin = sb("wlin", [D, D])
        ff_diag = sb("ff_diag", [P, P])
        pma_diag = sb("pma_diag", [P, P])
        vo_diag = sb("vo_diag", [P, P])
        seed_u = sb("seed_u", [P, 38])
        mats = {n: sb(n, [D, D]) for n in ("enc_out", "p_out", "p_ff", "d_out", "d_ff", "wvo2", "wvo3")}
        borrowed = probs_diag[:, :, :, :].rearrange("p b t n -> p (b t n)")
        wraw = borrowed[0:D + 1, 0:3 * D]
        p_in = borrowed[0:D, 3 * D:6 * D]
        d_in = borrowed[0:D, 6 * D:9 * D]
        wqT = borrowed[0:D, 9 * D:10 * D + 1]
        wkT = borrowed[0:D, 11 * D:12 * D]
        wvT2, wo2, wkT2, wide, wv23 = (
            borrowed[0:D, i * D:(i + 2) * D].rearrange("p (a b) -> p a b", a=2) for i in range(12, 22, 2))
        cols = sb("cols", [P, 24])
        COLS = ["b_lin", "ff_b", "pma_b", "seed", "bq2", "bk2", "bv2", "bo2", "bff2", "bv3", "bo3", "bff3",
                "qs", "b1", "b3", "c2", "bv1", "bo1"]
        col = {n: i for i, n in enumerate(COLS)}

        def c_(n, rows_=D):
            return cols[0:rows_, col[n]:col[n] + 1]

        count1 = sb("count1", [P, 2, HALF])
        row_f = sb("row_f", [P, 2, HALF])
        below = sb("below", [P, 2, HALF])
        start_f = sb("start_f", [P, 2, HALF])
        counts_b = sb("counts_b", [P, ITS], BF16)
        starts = sb("starts", [P, ITS + 1])
        counts = sb("counts", [P, ITS])
        win_idx = sb("win_idx", [P, 2, HALF], I32)
        sidx = sb("sidx", [P, 2, HALF], I32)

        windows = gathered_all[:, 0:2 * HALF * WINDOW].bitcast(I32).rearrange("p (h n) -> p h n", h=2)
        hflat = hT[:, :, :].rearrange("p s n -> p (s n)")
        trow = hflat[:, 0:2 * CHUNK * ROW].rearrange("p (b n) -> p b n", b=2)
        xflat = xp_rows[:, :, :].rearrange("p s n -> p (s n)")
        src_win = xflat[:, 0:2 * HALF * DEG].bitcast(I32).rearrange("p (h n) -> p h n", h=2)
        src_slots = xflat[:, 2 * HALF * DEG:4 * HALF * DEG].bitcast(I32).rearrange(
            "p (h n) -> p h n", h=2)
        spare = 2 * CHUNK * ROW
        flags2 = [hflat[:, spare + i * WINDOW:spare + (i + 1) * WINDOW] for i in range(2)]
        flags1 = [hflat[:, spare + 2 * WINDOW:spare + 2 * WINDOW + SAMPLES],
                  probs[:, :, :].rearrange("p s n -> p (s n)")[:, 0:SAMPLES]]
        xin = qT[:, :, :].rearrange("p s n -> p (s n)")[:, 0:2 * CHUNK * D].rearrange(
            "p (b t n) -> p b t n", b=2, t=CHUNK)
        xinT = avT[:, :, :].rearrange("p s n -> p (s n)")[0:D, 0:CHUNK * P]
        nodeT = h2[:, :, :].rearrange("p s n -> p (s n)")[0:D + 1, 0:CHUNK * P]
        samples = xb[:, :, :].rearrange("p s n -> p (s n)")[:, 0:SAMPLES].bitcast(I32)

        ps = ctx.enter_context(nc.psum_tensor("ps", [P, 8, 512], F32))
        B_Q, B_HX, B_S, B_AV, B_FF, B_POOL, B_SEED = 0, 1, 2, 4, 5, 6, 7
        ps_scores = ps[:, B_S:B_S + 2, :].rearrange("p h n -> p (h n)").rearrange("p (h n) -> p h n", h=2)[:, :, 0:256]
        ps_seed = ps[:, B_SEED, 0:P]
        ps_seedT = ps[:, B_POOL, P:2 * P]
        ps_fin = ps[:, B_POOL, 2 * P:3 * P]
        psf = ps[:, :, :].rearrange("p b n -> p (b n)")
        ps_xT = psf[0:D, 0:CHUNK * P]
        ps_node = psf[0:D, 1024:1024 + CHUNK * P]
        ps_row = psf[:, 2048:2048 + CHUNK * ROW]

        w_in = sem("w_in")
        samples_out = sem("samples_out")
        samples_in = sem("samples_in")
        pad_out = sem("pad_out")
        x_in = [sem("x_in0"), sem("x_in1")]
        tab_out = [sem("tab_out0"), sem("tab_out1")]
        x_tail = sem("x_tail")
        rows_in = sem("rows_in")
        out_done = sem("out_done")
        pool_cst = sem("pool_cst")
        pool_zero = sem("pool_zero")
        dve_zero = sem("dve_zero")
        dve_chain = sem("dve_chain")
        prep = sem("prep")
        prep_pe = sem("prep_pe")
        t_xT = sem("t_xT")
        t_xTc = sem("t_xTc")
        t_node = sem("t_node")
        t_nodec = sem("t_nodec")
        t_row = sem("t_row")
        t_rowc = sem("t_rowc")
        sampled = sem("sampled")
        row_ok = sem("row_ok")
        win_idx_ready = sem("win_idx_ready")
        win_in = [sem("win_in0"), sem("win_in1")]
        searched = sem("searched")
        start_ok = sem("start_ok")
        sidx_ready = sem("sidx_ready")
        start_kept = sem("start_kept")
        swin_in = [sem("swin_in0"), sem("swin_in1")]
        src_turned = sem("src_turned")
        src_kept = sem("src_kept")
        shifted = sem("shifted")
        counted = sem("counted")
        permuted = sem("permuted")
        counts_read = sem("counts_read")

        g_in = [sem(f"g_in{i}") for i in range(RING)]
        idx_ready = sem("idx_ready")
        q_ps = sem("q_ps")
        q_sb = sem("q_sb")
        h_ps = sem("h_ps")
        h_sb = sem("h_sb")
        s_ps = sem("s_ps")
        av_ps = sem("av_ps")
        av_sb = sem("av_sb")
        vo_ps = sem("vo_ps")
        h2_sb = sem("h2_sb")
        ff_ps = sem("ff_ps")
        xb_sb = sem("xb_sb")
        pma_ps = sem("pma_ps")
        xp_sb = sem("xp_sb")
        back_ps = sem("back_ps")
        back_sb = sem("back_sb")
        seed_ps = sem("seed_ps")
        mask_ok = sem("mask_ok")
        s_sb = sem("s_sb")
        s_top = sem("s_top")
        s_diff = sem("s_diff")
        p_exp = sem("p_exp")
        p_sum = sem("p_sum")
        p_share = sem("p_share")
        p_norm = sem("p_norm")
        p_diag = sem("p_diag")
        m2_cmp = sem("m2_cmp")
        m2_ok = sem("m2_ok")
        s2_sb = sem("s2_sb")
        s2_top = sem("s2_top")
        s2_diff = sem("s2_diff")
        p2_exp = sem("p2_exp")
        p2_sum = sem("p2_sum")
        p2_share = sem("p2_share")
        p2_norm = sem("p2_norm")
        seedT_ps = sem("seedT_ps")
        weights2_ok = sem("weights2_ok")
        pool_ps = sem("pool_ps")
        pool_own = sem("pool_own")
        pooled_ok = sem("pooled_ok")
        fin_ps = sem("fin_ps")
        pooledT_ok = sem("pooledT_ok")
        hid1_ok = sem("hid1_ok")
        pvec_ok = sem("pvec_ok")
        hid2_ok = sem("hid2_ok")
        dec_ok = sem("dec_ok")
        decr_ok = sem("decr_ok")
        y_ok = sem("y_ok")
        stats_ok = sem("stats_ok")
        ln_ok = sem("ln_ok")
        ln_std = sem("ln_std")
        ln_inv = sem("ln_inv")
        ln_shifted = sem("ln_shifted")
        normed = sem("normed")
        pe_passed, pool_passed, dve_passed = sem("pe_passed"), sem("pool_passed"), sem("dve_passed")

        block = ctx.enter_context(nc.Block())

        def steps(eng, body):
            for t in range(LOOP_FROM):
                body(Step(0, t, OCTETS))
            with eng.Fori(0, GROUPS) as group:
                for k in range(RING):
                    body(Step(group, LOOP_FROM + k, OCTETS))
            for t in range(LOOP_TO, END + 1):
                body(Step(0, t, OCTETS))

        WEIGHT_LOADS = []

        def vec(name, lo=0, hi=D):
            return w[name][lo:hi].rearrange("(n o) -> n o", o=1)

        def load(dst_ap, src_ap):
            WEIGHT_LOADS.append((dst_ap, src_ap))

        load(wraw[0:D, :], w["enc_in_w"])
        load(wraw[D:D + 1, :], w["enc_in_b"].rearrange("(o n) -> o n", o=1))
        load(wlin[:, :], w["w_lin"])
        load(mats["enc_out"][:, :], w["enc_out_w"])
        load(p_in[:, :], w["pma_in_w"])
        load(d_in[:, :], w["dec_in_w"])
        load(mats["p_out"][:, :], w["pma_out_w"])
        load(mats["p_ff"][:, :], w["pma_ff_w"])
        load(mats["d_out"][:, :], w["dec_out_w"])
        load(mats["d_ff"][:, :], w["dec_ff_w"])
        load(c_("b_lin"), vec("b_lin"))
        load(c_("bv1"), vec("enc_in_b", 2 * D, 3 * D))
        load(c_("bo1"), vec("enc_out_b"))
        load(cols[D:P, col["bo1"]:col["bo1"] + 1], vec("enc_out_b"))
        load(c_("ff_b"), vec("enc_ff_b"))
        load(cols[D:P, col["ff_b"]:col["ff_b"] + 1], vec("enc_ff_b"))
        load(c_("pma_b"), vec("pma_lin_b"))
        load(cols[D:P, col["pma_b"]:col["pma_b"] + 1], vec("pma_lin_b"))
        load(c_("seed"), w["pma_seed"].rearrange("o n -> n o"))
        load(c_("bq2"), vec("pma_in_b"))
        load(c_("bk2"), vec("pma_in_b", D, 2 * D))
        load(c_("bv2"), vec("pma_in_b", 2 * D, 3 * D))
        load(c_("bo2"), vec("pma_out_b"))
        load(c_("bff2"), vec("pma_ff_b"))
        load(c_("bv3"), vec("dec_in_b", 2 * D, 3 * D))
        load(c_("bo3"), vec("dec_out_b"))
        load(c_("bff3"), vec("dec_ff_b"))
        DIAG_LOADS = [(ff_diag[0:D, 0:D], w["enc_ff_w"]), (ff_diag[D:P, D:P], w["enc_ff_w"]),
                      (pma_diag[0:D, 0:D], w["pma_lin_w"]), (pma_diag[D:P, D:P], w["pma_lin_w"])]
        ALL_WEIGHTS = 16 * (len(WEIGHT_LOADS) + len(DIAG_LOADS))

        ROWS_PER_PART = 14
        ROW_PARTS = ITS // ROWS_PER_PART

        @block.sync
        def _(sp):
            sp.dma_start(dst_samples.rearrange("o n -> n o"), dst_rows[:, 0:1], allow_slow_non_contiguous=True
                         ).then_inc(samples_out, 16)
            sp.dma_start(src_padded[0:E, :].rearrange("(p n) o -> p (n o)", p=P), src.rearrange("(p n) -> p n", p=P)
                         ).then_inc(pad_out, 16)
            sp.dma_start(src_padded[E:E + D, :].rearrange("n o -> o n"), src[0:D].rearrange("(o n) -> o n", o=1)
                         ).then_inc(pad_out, 16)
            early = 2
            for d_, s_ in WEIGHT_LOADS[:early]:
                sp.dma_start(d_, s_).then_inc(w_in, 16)
            sp.wait_ge(samples_out, 16)
            sp.dma_start(samples, dst_samples.broadcast_to((P, SAMPLES))).then_inc(samples_in, 16)
            for d_, s_ in WEIGHT_LOADS[early:]:
                sp.dma_start(d_, s_).then_inc(w_in, 16)
            sp.wait_ge(dve_zero, 1)
            for d_, s_ in DIAG_LOADS:
                sp.dma_start(d_, s_).then_inc(w_in, 16)

            def load_chunk(c, b):
                sp.dma_start(xin[:, b], x[bass.ds(c * (CHUNK * P), CHUNK * P), :].rearrange(
                    "(t p) d -> p t d", p=P)).then_inc(x_in[b], 16)

            def store_chunk(c, b):
                sp.dma_start(table[bass.ds(c * (CHUNK * P), CHUNK * P), :].rearrange("(t p) n -> p t n", p=P),
                             trow[:, b].rearrange("p (t n) -> p t n", t=CHUNK)).then_inc(tab_out[b], 16)

            load_chunk(0, 0)
            load_chunk(1, 1)
            with sp.Fori(0, CHUNKS // 2 - 2) as g:
                for b in range(2):
                    sp.wait_ge(t_rowc, g * 2 + (b + 1))
                    store_chunk(g * 2 + b, b)
                    load_chunk(g * 2 + (b + 2), b)
            sp.wait_ge(t_rowc, CHUNKS - 3)
            store_chunk(CHUNKS - 4, 0)
            load_chunk(CHUNKS - 2, 0)
            sp.wait_ge(t_rowc, CHUNKS - 2)
            store_chunk(CHUNKS - 3, 1)
            base = (CHUNKS - 1) * CHUNK * P
            sp.dma_start(xin[0:LAST, 1, CHUNK - 1], x[N - LAST:N, :]).then_inc(x_tail, 16)
            sp.wait_ge(x_tail, 16)
            sp.dma_start(xin[:, 1, 0:CHUNK - 1], x[base:N - LAST, :].rearrange("(t p) d -> p t d", p=P)
                         ).then_inc(x_in[1], 16)
            for b in range(2):
                sp.wait_ge(t_rowc, CHUNKS - 1 + b)
                store_chunk(CHUNKS - 2 + b, b)
            sp.wait_ge(dve_zero, 2)
            for g in range(ROW_PARTS):
                sp.wait_ge(h_sb, 2 * g + 1)
                lo, hi = ROWS_PER_PART * g, min(ROWS_PER_PART * (g + 1), ITS - 1)
                for q in range(QUADS):
                    sp.dma_start(rows[q::QUADS, lo:hi, :],
                                 x[lo * P:hi * P, :].rearrange("(m a b) d -> a b m d", a=QUADS, b=DEG)[q]
                                 ).then_inc(rows_in, 16)
            for q in range(QUADS):
                n = min(max(LAST - q * DEG, 0), DEG)
                if n:
                    base = (ITS - 1) * P + q * DEG
                    sp.dma_start(rows[q:q + QUADS * (n - 1) + 1:QUADS, ITS - 1, :], x[base:base + n, :]
                                 ).then_inc(rows_in, 16)

            stores = 0
            for part, (lo, end) in enumerate(PARTS):
                sp.wait_ge(normed, part + 1)
                hi = min(end, ITS - 1)
                for q in range(QUADS):
                    sp.dma_start(out[lo * P:hi * P, :].rearrange("(m a b) d -> a b m d", a=QUADS, b=DEG)[q],
                                 rows[q::QUADS, lo:hi, :]).then_inc(out_done, 16)
                    stores += 1
                    n = min(max(LAST - q * DEG, 0), DEG)
                    if end == ITS and n:
                        base = (ITS - 1) * P + q * DEG
                        sp.dma_start(out[base:base + n, :], rows[q:q + QUADS * (n - 1) + 1:QUADS, ITS - 1, :]
                                     ).then_inc(out_done, 16)
                        stores += 1
            sp.wait_ge(out_done, 16 * stores)

        ROWS_LOADED = 16 * (QUADS * ROW_PARTS + sum(1 for q in range(QUADS) if LAST > q * DEG))

        @block.gpsimd
        def _(pool):
            nc.gpsimd.iota(node_i[:, :], [[P, ITS]], 0, 1).then_inc(pool_cst, 1)
            nc.gpsimd.iota(iota_ji[:, :], [[1, DEG]], 0, 0).then_inc(pool_cst, 1)
            for t in (ident[:, :], shift, seed_perm, pool_perm):
                nc.gpsimd.memset(t, 0.0).then_inc(pool_zero, 1)
            pool.wait_ge(pool_zero, 4)

            def one_where_zero(view, pattern, base, mult=1):
                nc.gpsimd.affine_select(out=view, in_=view, compare_op=ALU.not_equal, fill=1.0, base=base,
                                        pattern=pattern, channel_multiplier=mult).then_inc(pool_cst, 1)

            one_where_zero(ident[:, :], [[-1, P]], 0)
            one_where_zero(shift[:, 0, :], [[-1, P]], -1)
            one_where_zero(shift[:, 1, :], [[1, P]], -(P - 1), P)
            for q in range(QUADS):
                one_where_zero(seed_perm[:, q, :].rearrange("p (c r) -> p c r", c=QUADS)[:, :, 0:OCT],
                               [[-OCT, QUADS], [-1, OCT]], -DEG * q)
                one_where_zero(pool_perm.rearrange("p (b a) -> p a b", a=QUADS)[:, q, :],
                               [[-1, DEG]], -DEG * q)

            def gather_windows(table_ap, size, index, target, h, landed):
                for t in range(HALF):
                    pool.indirect_dma_start(
                        out=target[:, h, t * size:(t + 1) * size], out_offset=None, in_=table_ap,
                        in_offset=bass.IndirectOffsetOnAxis(ap=index[:, h, t:t + 1], axis=0),
                    ).then_inc(landed[h], 16)

            for h in range(2):
                pool.wait_ge(win_idx_ready, h + 1)
                gather_windows(dst_rows, WINDOW, win_idx, windows, h, win_in)
            pool.wait_ge(pad_out, 32)
            with pool.Fori(0, SEARCHES // 2 - 1) as g:
                for h in range(2):
                    wait_apart(pool, sidx_ready, g * 2 + (h + 1), pool_passed)
                    gather_windows(src_padded, DEG, sidx, src_win, h, swin_in)
                    wait_apart(pool, win_idx_ready, g * 2 + (h + 3), pool_passed)
                    gather_windows(dst_rows, WINDOW, win_idx, windows, h, win_in)
            for h in range(2):
                pool.wait_ge(sidx_ready, SEARCHES - 1 + h)
                gather_windows(src_padded, DEG, sidx, src_win, h, swin_in)

            pool.wait_ge(idx_ready, RING)
            pool.wait_ge(tab_out[0], 16 * (CHUNKS // 2))
            pool.wait_ge(tab_out[1], 16 * (CHUNKS // 2))

            def step(s):
                if not s.has(0):
                    return
                wait_apart(pool, av_ps, s.octet(RING - 1), pool_passed)
                wait_apart(pool, idx_ready, s.octet(-1), pool_passed)
                for t in range(OCT):
                    pool.indirect_dma_start(
                        out=gathered[:, s.slot(0, RING), t * ROW:(t + 1) * ROW], out_offset=None, in_=table,
                        in_offset=bass.IndirectOffsetOnAxis(ap=idx[:, s.slot(0, RING), t:t + 1], axis=0),
                    ).then_inc(g_in[s.slot(0, RING)], 16)

            steps(pool, step)

        @block.tensor
        def _(pe):
            pe.wait_ge(w_in, ALL_WEIGHTS)
            pe.wait_ge(prep, 1)
            pe.transpose(ps[0:D, 0, 0:D + 1], wraw[:, 0:D], ident[0:D + 1, 0:D + 1]).then_inc(prep_pe, 1)
            pe.transpose(ps[0:D, 1, 0:D], wraw[0:D, D:2 * D], ident[0:D, 0:D]).then_inc(prep_pe, 1)
            pe.transpose(ps[0:D, 2, 0:D], wraw[0:D, 2 * D:3 * D], ident[0:D, 0:D]).then_inc(prep_pe, 1)
            pe.transpose(ps[0:D, 3, 0:D], p_in[:, D:2 * D], ident[0:D, 0:D]).then_inc(prep_pe, 1)
            pe.matmul(ps[0:D, 4, 0:1], p_in[:, 0:D], c_("seed"), start=True, stop=True).then_inc(prep_pe, 1)
            pe.transpose(ps[0:D, 5, 0:D], p_in[:, 2 * D:3 * D], ident[0:D, 0:D]).then_inc(prep_pe, 1)
            pe.transpose(ps[0:D, 6, 0:D], d_in[:, 2 * D:3 * D], ident[0:D, 0:D]).then_inc(prep_pe, 1)
            pe.wait_ge(prep, 2)

            def both(t):
                return t.rearrange("p a b -> p (a b)")

            pe.matmul(ps[0:D + 1, 0, 0:D], wqT, wkT, start=True, stop=True).then_inc(prep_pe, 1)
            pe.matmul(ps[:, 1, 0:D], both(wvT2), mats["enc_out"][:, :], start=True, stop=True).then_inc(prep_pe, 1)
            pe.matmul(ps[:, 2, 0:1], both(wo2), c_("bv1"), start=True, stop=True).then_inc(prep_pe, 1)
            pe.matmul(ps[:, 3, 0:1], both(wkT2), c_("qs"), start=True, stop=True).then_inc(prep_pe, 1)
            pe.matmul(ps[:, 4, 0:1], both(wide), c_("bk2"), start=True, stop=True).then_inc(prep_pe, 1)
            pe.matmul(ps[0:D, 5, 0:1], mats["p_out"][:, :], c_("bv2"), start=True, stop=True).then_inc(prep_pe, 1)
            pe.matmul(ps[0:D, 6, 0:1], mats["d_out"][:, :], c_("bv3"), start=True, stop=True).then_inc(prep_pe, 1)
            pe.matmul(ps[0:D, 7, 0:D], wv23[:, 0, :], mats["p_out"][:, :], start=True, stop=True).then_inc(prep_pe, 1)
            pe.matmul(ps[0:D, 7, D:2 * D], wv23[:, 1, :], mats["d_out"][:, :], start=True, stop=True
                      ).then_inc(prep_pe, 1)
            pe.wait_ge(prep, 3)

            with pe.Fori(0, CHUNKS // 2) as g:
                for b in range(2):
                    n = g * 2 + (b + 1)
                    wait_apart(pe, x_in[b], g * 16 + 16, pe_passed)
                    for t in range(CHUNK):
                        mm = pe.transpose(ps_xT[:, t * P:(t + 1) * P], xin[:, b, t, :], ident[:, :])
                    mm.then_inc(t_xT, 1)
                    wait_apart(pe, t_xTc, n, pe_passed)
                    pe.matmul(ps_node[:, 0:512], wlin[:, :], xinT[:, 0:512], start=True, stop=True)
                    pe.matmul(ps_node[:, 512:CHUNK * P], wlin[:, :], xinT[:, 512:CHUNK * P], start=True, stop=True
                              ).then_inc(t_node, 1)
                    wait_apart(pe, t_nodec, n, pe_passed)
                    for t in range(CHUNK):
                        mm = pe.matmul(ps_row[:, t * ROW:(t + 1) * ROW], nodeT[:, t * P:(t + 1) * P], wtab[:, :],
                                       start=True, stop=True)
                    mm.then_inc(t_row, 1)

            pe.wait_ge(start_kept, SEARCHES)
            pe.wait_ge(t_rowc, CHUNKS)
            pe.matmul(ps[:, 0, 0:ITS], shift[:, 0, :], starts[:, 0:ITS], start=True, stop=False)
            pe.matmul(ps[:, 0, 0:ITS], shift[:, 1, :], starts[:, 1:ITS + 1], start=False, stop=True
                      ).then_inc(shifted, 1)
            pe.wait_ge(counted, 1)
            for q in range(QUADS):
                pe.matmul(ps[:, 1, q * P:q * P + ITS], seed_perm[:, q, :], counts[:, :], start=True, stop=True)
            pe.matmul(ps[:, 2, 0:ITS], pool_perm, counts[:, :], start=True, stop=True).then_inc(permuted, 1)
            pe.wait_ge(counts_read, 1)

            def turn(s, c, bank):
                for p in range(PAIRS):
                    lo = 2 * p * ROW + c
                    mm = pe.transpose(ps[:, bank, p * P:(p + 1) * P],
                                      gathered[:, s.slot(0, RING), lo:lo + 2 * ROW - 1:2], ident[:, :])
                return mm

            def step(s):
                if s.has(0):
                    wait(pe, q_sb, s.octet(0))
                    pe.wait_ge(g_in[s.slot(0, RING)], s.round(0) * (16 * OCT) + 16 * OCT)
                    turn(s, 0, B_Q).then_inc(q_ps, 1)
                    if s.has(L_BACK + 1):
                        wait(pe, back_sb, s.octet(L_BACK))
                    else:
                        wait(pe, h_sb, s.octet(0))
                    turn(s, 1, B_HX).then_inc(h_ps, 1)
                if s.has(L_PMA):
                    wait(pe, xb_sb, s.octet(L_PMA - 1))
                    pe.matmul(ps[:, B_FF, :], pma_diag[:, :], xb[:, s.slot(L_PMA, 2), :], start=True, stop=True
                              ).then_inc(pma_ps, 1)
                if s.has_iteration(L_DEC1):
                    fin_op(s, L_DEC1, pooled_ok, ps_fin[0:D, :], pooled, ident)
                if s.has_iteration(L_DEC2):
                    fin_op(s, L_DEC2, hid1_ok, ps_fin[0:D, :], mats["p_ff"], hid1)
                if s.has_iteration(L_OUT):
                    fin_op(s, L_OUT, hid2_ok, ps_fin[0:D, :], mats["d_ff"], hid2)
                if s.has_iteration(L_WEIGHTS):
                    wait(pe, p2_norm, s.iteration(L_WEIGHTS) + 1)
                    pe.transpose(ps_seedT, scores2[:, :], ident[:, :]).then_inc(seedT_ps, 1)
                if s.has(L_ATTEND):
                    if s.slot(L_ATTEND, 2) == 0:
                        wait(pe, p_diag, s.batch(L_ATTEND) * 4 + 4)
                    wait(pe, h2_sb, s.octet(L_ATTEND))
                    for p in range(PAIRS):
                        for h in range(2):
                            lo = (2 * p + h) * ROW + 1
                            mm = pe.matmul(ps[D * h:D * h + D, B_AV, p * P:(p + 1) * P],
                                           gathered[:, s.slot(L_ATTEND, RING), lo:lo + ROW - 1:2],
                                           probs_diag[:, s.slot(L_ATTEND, 4) // 2,
                                                      OCT * h + PAIRS * s.slot(L_ATTEND, 2) + p, :],
                                           start=True, stop=True)
                    mm.then_inc(av_ps, 1)
                if s.has(L_SCORES):
                    if s.slot(L_SCORES, 2) == 0:
                        wait(pe, s_sb, s.batch(L_SCORES))
                    wait(pe, q_sb, s.octet(L_SCORES - 1))
                    wait_apart(pe, h_sb, s.octet(L_SCORES - 1), pe_passed)
                    par = s.slot(L_SCORES, 2)
                    for p in range(PAIRS):
                        for q in range(QUADS):
                            for h in range(2):
                                lo = p * P + DEG * q
                                hi = D * h
                                mm = pe.matmul(
                                    ps[DEG * q:DEG * q + DEG, B_S + h, (PAIRS * par + p) * DEG:(PAIRS * par + p + 1) * DEG],
                                    qT[hi:hi + D, par, lo:lo + DEG],
                                    hT[hi:hi + D, s.slot(L_SCORES, RING), lo:lo + DEG],
                                    start=True, stop=True)
                    mm.then_inc(s_ps, 1)
                if s.has_iteration(L_POOL):
                    wait(pe, weights2_ok, s.iteration(L_POOL) + 1)
                    wait(pe, y_ok, s.iteration(L_POOL))
                    wait(pe, back_sb, s.octet(L_POOL - OCTS_PER_IT))
                    for c in range(OCTS_PER_IT):
                        mm = pe.matmul(ps[DEG * c:DEG * c + DEG, B_POOL, :],
                                       weights2[:, c].rearrange("p t a -> p (t a)"),
                                       xp_rows[:, (s.slot(L_POOL, RING) + c) % RING, :], start=True, stop=True)
                    mm.then_inc(pool_ps, 1)
                if s.has(L_FF):
                    wait(pe, xp_sb, s.octet(L_FF))
                    wait(pe, h2_sb, s.octet(L_FF - 1))
                    pe.matmul(ps[:, B_FF, :], ff_diag[:, :], h2[:, s.slot(L_FF, 2), :], start=True, stop=True
                              ).then_inc(ff_ps, 1)
                if s.has(L_ATTEND):
                    wait(pe, av_sb, s.octet(L_ATTEND - 1))
                    pe.matmul(ps[:, B_AV, :], vo_diag[:, :], avT[:, s.slot(L_ATTEND, 2), :], start=True, stop=True
                              ).then_inc(vo_ps, 1)
                if s.has_iteration(L_DEC1):
                    fin_op(s, L_DEC1, pooledT_ok, ps_fin[0:D, :], mats["wvo2"], pooledT)
                if s.has_iteration(L_DEC2):
                    fin_op(s, L_DEC2, pvec_ok, ps_fin[0:D, :], mats["wvo3"], pvec)
                if s.has_iteration(L_OUT):
                    if s.has_iteration(L_WEIGHTS):
                        wait(pe, weights2_ok, s.iteration(L_WEIGHTS) + 1)
                    fin_op(s, L_OUT, decr_ok, ps_fin[:, 0:D], decr, ident)
                if s.has(L_BACK):
                    if s.has(0):
                        wait(pe, h_sb, s.octet(-1))
                    else:
                        wait(pe, back_sb, s.octet(L_BACK))
                    wait(pe, xp_sb, s.octet(L_BACK - 1))
                    for p in range(PAIRS):
                        mm = pe.transpose(ps[:, B_HX, p * P:(p + 1) * P],
                                          xp[:, s.slot(L_BACK, 2), p * P:(p + 1) * P], ident[:, :])
                    mm.then_inc(back_ps, 1)
                    c = s.slot(L_BACK, OCTS_PER_IT)
                    if c == 0:
                        wait(pe, s2_sb, s.iteration(L_BACK))
                    for p in range(PAIRS):
                        mm = pe.matmul(ps_seed[DEG * c:DEG * c + DEG, :], seed_u[:, 6 - 2 * p:38 - 2 * p],
                                       xp[:, s.slot(L_BACK, 2), p * P:(p + 1) * P],
                                       start=(p == 0), stop=(p == PAIRS - 1))
                    mm.then_inc(seed_ps, 1)
            def fin_op(s, lag, ready, out_, lhs, rhs):
                wait_apart(pe, ready, s.iteration(lag) + 1, pe_passed)
                if rhs is ident:
                    mm = pe.transpose(out_, lhs[:, :], rhs[0:lhs.shape[0], 0:lhs.shape[0]])
                else:
                    mm = pe.matmul(out_, lhs[:, :], rhs[:, :], start=True, stop=True)
                mm.then_inc(fin_ps, 1)

            steps(pe, step)

        @block.scalar
        def _(act):
            def copy(o, i):
                return nc.scalar.activation(o, i, ACT.Copy)

            act.wait_ge(w_in, ALL_WEIGHTS)
            act.wait_ge(dve_zero, 1)

            def table_chunk(g, b):
                n = g * 2 + (b + 1)
                act.wait_ge(t_xT, n)
                copy(xinT, ps_xT).then_inc(t_xTc, 1)
                act.wait_ge(t_node, n)
                nc.scalar.activation(nodeT[0:D, :], ps_node, ACT.Identity, bias=c_("b_lin")).then_inc(t_nodec, 1)
                act.wait_ge(t_row, n)
                wait(act, tab_out[b], g * 16)
                copy(trow[:, b, :], ps_row).then_inc(t_rowc, 1)

            table_chunk(0, 0)
            table_chunk(0, 1)
            with act.Fori(1, CHUNKS // 2) as g:
                table_chunk(g, 0)
                table_chunk(g, 1)

            def step(s):
                if s.has(0):
                    act.wait_ge(q_ps, s.octet(-1))
                    wait(act, s_ps, s.octet(1))
                    copy(qT[:, s.slot(0, 2), :], ps[:, B_Q, :]).then_inc(q_sb, 1)
                    act.wait_ge(h_ps, s.octet(-1))
                    wait(act, h2_sb, s.octet(RING - 1))
                    copy(hT[:, s.slot(0, RING), :], ps[:, B_HX, :]).then_inc(h_sb, 1)
                if s.has_iteration(L_DEC2):
                    wait(act, fin_ps, s.iteration(L_DEC2) * 6 + 2)
                    nc.scalar.activation(hid1[:, :], ps_fin[0:D, :], ACT.Identity, bias=c_("b1")).then_inc(hid1_ok, 1)
                if s.has_iteration(L_OUT):
                    wait(act, fin_ps, s.iteration(L_OUT) * 6 + 4)
                    nc.scalar.activation(hid2[:, :], ps_fin[0:D, :], ACT.Identity, bias=c_("b3")).then_inc(hid2_ok, 1)
                if s.has_iteration(L_SEED_T):
                    wait(act, s2_diff, s.iteration(L_SEED_T) + 1)
                    nc.scalar.activation(scores2[:, :], scores2[:, :], ACT.Exp).then_inc(p2_exp, 1)
                if s.has(L_PMA):
                    act.wait_ge(pma_ps, s.octet(L_PMA - 1))
                    wait(act, seed_ps, s.octet(L_PMA + 1))
                    nc.scalar.activation(xp[:, s.slot(L_PMA, 2), :], ps[:, B_FF, :], ACT.Relu,
                                         bias=c_("pma_b", P)).then_inc(xp_sb, 1)
                if s.has(L_ATTEND):
                    act.wait_ge(av_ps, s.octet(L_ATTEND - 1))
                    wait(act, vo_ps, s.octet(L_ATTEND + 1))
                    copy(avT[:, s.slot(L_ATTEND, 2), :], ps[:, B_AV, :]).then_inc(av_sb, 1)
                if s.has_batch(L_SOFTMAX):
                    wait(act, s_diff, s.batch(L_SOFTMAX) + 1)
                    wait(act, p_diag, s.batch(L_SOFTMAX + 2) * 4)
                    nc.scalar.activation(probs[:, s.slot(L_SOFTMAX, 4) // 2, :], scores[:, :], ACT.Exp
                                         ).then_inc(p_exp, 1)
                if s.has_iteration(L_DEC1):
                    wait(act, fin_ps, s.iteration(L_DEC1) * 6 + 1)
                    copy(pooledT[:, :], ps_fin[0:D, :]).then_inc(pooledT_ok, 1)
                if s.has(L_BACK):
                    act.wait_ge(back_ps, s.octet(L_BACK - 1))
                    wait(act, pool_ps, s.iteration(L_BACK) - 1)
                    copy(xp_rows[:, s.slot(L_BACK, RING), :], ps[:, B_HX, :]).then_inc(back_sb, 1)
                if not s.looped and s.at == LOOP_TO + 2:
                    deviation(0, EARLY, 1)

            def deviation(lo, hi, n):
                act.wait_ge(ln_ok, 5 * n)
                nc.scalar.activation(lnv[:, 3, lo:hi], lnv[:, 2, lo:hi], ACT.Sqrt, bias=eps[:, 0:1], scale=1.0
                                     ).then_inc(ln_std, 1)

            steps(act, step)
            deviation(EARLY, ITS, 2)

        @block.vector
        def _(dve):
            V = nc.vector
            chained = [0]

            def link(ins):
                chained[0] += 1
                ins.then_inc(dve_chain, 1)
                dve.wait_ge(dve_chain, chained[0])

            V.memset(ff_diag[:, :], 0.0)
            V.memset(pma_diag[:, :], 0.0)
            V.memset(vo_diag[:, :], 0.0)
            V.memset(wtab[:, :], 0.0)
            link(V.memset(nodeT[D:D + 1, :], 1.0))
            V.memset(xin[:, :, :, :], 0.0).then_inc(dve_zero, 1)
            V.memset(seed_u[:, :], 0.0)
            V.memset(starts[:, ITS:ITS + 1], float(E))
            V.memset(eps[:, :], EPS)
            V.memset(rows[:, ITS - 1, :], 0.0).then_inc(dve_zero, 1)
            dve.wait_ge(pool_cst, 2)
            V.tensor_copy(iota_j[:, :], iota_ji[:, :])
            link(V.tensor_copy(node_f[:, :], node_i[:, :]))

            def rows_of_group(g, h):
                for t in range(HALF):
                    wait(dve, sampled, g * HALF + (t - 1))
                    V.tensor_scalar(flags1[(h * HALF + t) % 2], samples, node_f[:, bass.ds(g * HALF + t, 1)], None, ALU.is_lt, ALU.add,
                                    accum_out=count1[:, h, t:t + 1]).then_inc(sampled, 1)
                dve.wait_ge(sampled, g * HALF + HALF)
                V.tensor_scalar(row_f[:, h, :], count1[:, h, :], -1.0, 0.0, ALU.add, ALU.max).then_inc(row_ok, 1)
                dve.wait_ge(row_ok, g + 1)
                V.tensor_copy(win_idx[:, h, :], row_f[:, h, :]).then_inc(win_idx_ready, 1)

            def starts_of_group(g, h, rounds):
                dve.wait_ge(win_in[h], rounds * (16 * HALF) + 16 * HALF)
                for t in range(HALF):
                    wait(dve, searched, g * HALF + (t - 1))
                    V.tensor_scalar(flags2[(h * HALF + t) % 2], windows[:, h, t * WINDOW:(t + 1) * WINDOW],
                                    node_f[:, bass.ds(g * HALF + t, 1)], None, ALU.is_lt, ALU.add,
                                    accum_out=below[:, h, t:t + 1]).then_inc(searched, 1)
                dve.wait_ge(searched, g * HALF + HALF)
                V.scalar_tensor_tensor(start_f[:, h, :], row_f[:, h, :], float(WINDOW), below[:, h, :],
                                       ALU.mult, ALU.add).then_inc(start_ok, 1)
                dve.wait_ge(start_ok, g + 1)
                V.tensor_copy(sidx[:, h, :], start_f[:, h, :]).then_inc(sidx_ready, 1)
                V.tensor_copy(starts[:, bass.ds(g * HALF, HALF)], start_f[:, h, :]).then_inc(start_kept, 1)

            def indices_of_group(g, h, rounds):
                dve.wait_ge(swin_in[h], rounds * (16 * HALF) + 16 * HALF)
                V.transpose(src_slots[:, h, :], src_win[:, h, :]).then_inc(src_turned, 1)
                wait_apart(dve, src_turned, g + 1, dve_passed)
                V.tensor_copy(idx_all[:, bass.ds(g * (HALF * DEG), HALF * DEG)], src_slots[:, h, :]
                              ).then_inc(src_kept, 1)

            dve.wait_ge(samples_in, 16)
            rows_of_group(0, 0)
            rows_of_group(1, 1)

            marked = [0]

            def mark(ins):
                marked[0] += 1
                ins.then_inc(prep, 1)
                dve.wait_ge(prep, marked[0])

            starts_of_group(0, 0, 0)
            rows_of_group(2, 0)
            dve.wait_ge(w_in, ALL_WEIGHTS)
            dve.wait_ge(pool_cst, 2 + 3 + 2 * QUADS)
            V.tensor_reduce(quad_of[:, :], ident[:, :].rearrange("p (a j) -> p a j", j=DEG), AX_X, ALU.add)
            V.tensor_reduce(tile_of[:, :], ident[:, :].rearrange("p (c t a) -> p t c a", c=QUADS, t=OCT),
                            mybir.AxisListType.XY, ALU.add)
            mark(V.tensor_copy(wtab[0:D, 1:ROW:2], ident[0:D, 0:D]))
            for t in (wo2[:, 0, :], wo2[:, 1, :]):
                V.tensor_copy(t, mats["enc_out"][:, :])
            starts_of_group(1, 1, 0)
            indices_of_group(0, 0, 0)
            dve.wait_ge(prep_pe, 7)
            V.tensor_copy(wqT, ps[0:D, 0, 0:D + 1])
            V.tensor_copy(wkT, ps[0:D, 1, 0:D])
            for i in range(2):
                V.tensor_copy(wvT2[:, i, :], ps[0:D, 2, 0:D])
                V.tensor_copy(wkT2[:, i, :], ps[0:D, 3, 0:D])
                V.tensor_copy(wv23[:, i, :], ps[0:D, 5 + i, 0:D])
            link(V.tensor_scalar(c_("qs"), ps[0:D, 4, 0:1], c_("bq2"), D ** -0.5, ALU.add, ALU.mult))
            mark(V.tensor_copy(wide.rearrange("p a b -> p (a b)"), c_("qs").broadcast_to((D, P))))
            rows_of_group(3, 1)
            dve.wait_ge(prep_pe, 16)
            V.tensor_scalar(wtab[:, 0:ROW:2], ps[0:D + 1, 0, 0:D], D ** -0.5, None, ALU.mult)
            V.tensor_copy(vo_diag[0:D, 0:D], ps[0:D, 1, 0:D])
            V.tensor_copy(vo_diag[D:P, D:P], ps[D:P, 1, 0:D])
            V.tensor_tensor(c_("bo1", P), ps[:, 2, 0:1], c_("bo1", P), ALU.add)
            V.tensor_copy(seed_u[0:D, 6:7], ps[0:D, 3, 0:1])
            V.tensor_copy(seed_u[D:P, 7:8], ps[D:P, 3, 0:1])
            V.tensor_copy(c_("c2", P), ps[:, 4, 0:1])
            V.tensor_tensor(c_("b3"), ps[0:D, 6, 0:1], c_("bo3"), ALU.add)
            link(V.tensor_tensor(c_("b1"), ps[0:D, 5, 0:1], c_("bo2"), ALU.add))
            link(V.tensor_tensor(c_("b1"), c_("b1"), c_("seed"), ALU.add))
            for t, n in ((ff_diag, P), (mats["p_ff"], D), (mats["d_ff"], D)):
                V.tensor_tensor(t[:, :], t[:, :], ident[0:n, 0:n], ALU.add)
            V.tensor_copy(mats["wvo2"][:, :], ps[0:D, 7, 0:D])
            mark(V.tensor_tensor(mats["wvo3"][:, :], ps[0:D, 7, D:2 * D], ident[0:D, 0:D], ALU.add))

            V.memset(borrowed, 0.0)

            with dve.Fori(1, SEARCHES // 2 - 1) as pair:
                for h in range(2):
                    g = pair * 2 + h
                    starts_of_group(g, h, pair)
                    indices_of_group(g - 1, 1 - h, pair - (1 - h))
                    rows_of_group(g + 2, h)
            for h in range(2):
                g = SEARCHES - 2 + h
                starts_of_group(g, h, g // 2)
                indices_of_group(g - 1, 1 - h, (g - 1) // 2)
            V.tensor_copy(idx[:, :, :].rearrange("p s t -> p (s t)"), idx_all[:, 0:RING * OCT]
                          ).then_inc(idx_ready, RING)
            dve.wait_ge(shifted, 1)
            V.tensor_tensor(counts[:, :], ps[:, 0, 0:ITS], starts[:, 0:ITS], ALU.subtract).then_inc(counted, 1)
            dve.wait_ge(counted, 1)
            link(V.tensor_scalar(counts_b[:, :], counts[:, :], float(DEG), None, ALU.min))
            V.transpose(count_slot[:, :].rearrange("p (m b) -> p m b", b=DEG),
                        counts_b[:, :].unsqueeze(2).broadcast_to((P, ITS, DEG)))
            dve.wait_ge(permuted, 1)
            for q in range(QUADS):
                V.tensor_copy(count_seed[:, :, q], ps[:, 1, q * P:q * P + ITS])
            V.tensor_scalar(nonempty[:, :], ps[:, 2, 0:ITS], 0.0, None, ALU.is_gt).then_inc(counts_read, 1)
            dve.wait_ge(counts_read, 1)
            indices_of_group(SEARCHES - 1, 1, SEARCHES // 2 - 1)
            dve.wait_ge(src_kept, SEARCHES)

            def by_slot(ap):
                return ap.rearrange("p (t j) -> p t j", j=DEG)

            iota_slots = iota_j[:, :].unsqueeze(1).broadcast_to((P, 2, DEG))

            def step(s):
                if s.has(L_H2):
                    wait(dve, vo_ps, s.octet(L_H2 - 1))
                    wait(dve, ff_ps, s.octet(L_H2 + 1))
                    V.scalar_tensor_tensor(h2[:, s.slot(L_H2, 2), :], ps[:, B_AV, :], c_("bo1", P),
                                           hT[:, s.slot(L_H2, RING), :], ALU.add, ALU.add).then_inc(h2_sb, 1)
                if s.has_batch(L_SOFTMAX):
                    n = s.batch(L_SOFTMAX)
                    dve.wait_ge(s_ps, s.octet(L_SOFTMAX - 2))
                    dve.wait_ge(mask_ok, n + 1)
                    wait(dve, p_exp, n)
                    V.scalar_tensor_tensor(scores[:, :].rearrange("p (h n) -> p h n", h=2),
                                           empty[:, :].rearrange("p (h n) -> p h n", h=2), MASKED, ps_scores,
                                           ALU.mult, ALU.add).then_inc(s_sb, 1)
                if s.has_iteration(L_Y):
                    y_rows(s)
                if s.has_iteration(L_SEED):
                    m = s.iteration(L_SEED)
                    dve.wait_ge(m2_ok, m + 1)
                    dve.wait_ge(seed_ps, s.octet(L_SEED - 4))
                    wait(dve, seedT_ps, m)
                    V.scalar_tensor_tensor(scores2[:, :], ps_seed, c_("c2", P), empty2[:, :], ALU.add, ALU.add
                                           ).then_inc(s2_sb, 1)
                if s.has_batch(L_SOFTMAX):
                    n = s.batch(L_SOFTMAX)
                    dve.wait_ge(s_sb, n + 1)
                    V.tensor_reduce(top[:, :], by_slot(scores[:, :]), AX_X, ALU.max).then_inc(s_top, 1)
                if s.has_batch(L_NORM):
                    pr = probs[:, s.slot(L_NORM, 4) // 2, :]
                    n = s.batch(L_NORM)
                    dve.wait_ge(p_exp, n + 1)
                    V.tensor_reduce(total[:, :], by_slot(pr), AX_X, ALU.add).then_inc(p_sum, 1)
                if s.has_batch(L_SOFTMAX):
                    dve.wait_ge(s_top, n + 1)
                    V.tensor_tensor(by_slot(scores[:, :]), by_slot(scores[:, :]),
                                    top[:, :].unsqueeze(2).broadcast_to((P, 16, DEG)), ALU.subtract
                                    ).then_inc(s_diff, 1)
                if s.has_batch(L_NORM):
                    dve.wait_ge(p_sum, n + 1)
                    V.reciprocal(share[:, :], total[:, :]).then_inc(p_share, 1)
                if s.has_batch(L_NORM):
                    dve.wait_ge(p_share, n + 1)
                    V.tensor_tensor(by_slot(pr), by_slot(pr), share[:, :].unsqueeze(2).broadcast_to((P, 16, DEG)),
                                    ALU.mult).then_inc(p_norm, 1)
                    dve.wait_ge(p_norm, n + 1)
                    wait(dve, av_ps, s.octet(L_NORM + 2))
                    to_diagonal(s, pr, 0, QUADS // 2)
                if s.has_iteration(L_DEC2):
                    m = s.iteration(L_DEC2)
                    wait(dve, fin_ps, m * 6 + 3)
                    V.scalar_tensor_tensor(pvec[:, :], ps_fin[0:D, :], c_("bff2"), hid1[:, :], ALU.add, ALU.max
                                           ).then_inc(pvec_ok, 1)
                if s.has_iteration(L_OUT):
                    out_rows(s)
                if s.has_iteration(L_WEIGHTS):
                    wait(dve, seedT_ps, s.iteration(L_WEIGHTS) + 1)
                    wait(dve, pool_ps, s.iteration(L_WEIGHTS))
                    V.tensor_tensor(
                        weights2[:, :, :, :],
                        ps_seedT.rearrange("p (c t) -> p c t", c=OCTS_PER_IT)[:, :, 0:OCT].unsqueeze(3).broadcast_to(
                            (P, OCTS_PER_IT, OCT, QUADS)),
                        quad_of[:, :].unsqueeze(1).unsqueeze(1).broadcast_to((P, OCTS_PER_IT, OCT, QUADS)),
                        ALU.mult).then_inc(weights2_ok, 1)
                part = -1 if s.looped else s.at - (LOOP_TO + 1)
                if part == 0:
                    moments(0, EARLY, 0)
                part = part // 2 - 1 if part % 2 == 0 and part // 2 <= NORM_PARTS else -1
                if part >= 0:
                    norm_shift(part)
                if s.has(L_FF):
                    wait(dve, ff_ps, s.octet(L_FF - 1))
                    wait(dve, pma_ps, s.octet(L_FF + 1))
                    V.scalar_tensor_tensor(xb[:, s.slot(L_FF, 2), :], ps[:, B_FF, :], c_("ff_b", P),
                                           h2[:, s.slot(L_FF, 2), :], ALU.add, ALU.max).then_inc(xb_sb, 1)
                if part >= 0:
                    norm_scale(part)
                if s.has_batch(L_NORM):
                    to_diagonal(s, pr, QUADS // 2, QUADS)
                if s.has_iteration(L_MASK2):
                    m = s.iteration(L_MASK2)
                    wait(dve, s2_sb, m)
                    V.tensor_tensor(empty2[:, :].rearrange("p (a j) -> p a j", j=DEG),
                                    iota_j[:, :].unsqueeze(1).broadcast_to((P, QUADS, DEG)),
                                    count_seed[:, bass.ds(m, 1), :].rearrange("p m a -> p (m a)").unsqueeze(2)
                                    .broadcast_to((P, QUADS, DEG)), ALU.is_ge).then_inc(m2_cmp, 1)
                    dve.wait_ge(m2_cmp, m + 1)
                    V.tensor_scalar(empty2[:, :], empty2[:, :], MASKED, None, ALU.mult).then_inc(m2_ok, 1)
                if s.has_iteration(L_SEED):
                    m = s.iteration(L_SEED)
                    dve.wait_ge(s2_sb, m + 1)
                    V.tensor_reduce(top2[:, :], by_slot(scores2[:, :]), AX_X, ALU.max).then_inc(s2_top, 1)
                    dve.wait_ge(s2_top, m + 1)
                    V.tensor_tensor(by_slot(scores2[:, :]), by_slot(scores2[:, :]),
                                    top2[:, :].unsqueeze(2).broadcast_to((P, QUADS, DEG)), ALU.subtract
                                    ).then_inc(s2_diff, 1)
                if s.has_iteration(L_SEED_T):
                    m = s.iteration(L_SEED_T)
                    dve.wait_ge(p2_exp, m + 1)
                    V.tensor_reduce(total2[:, :], by_slot(scores2[:, :]), AX_X, ALU.add).then_inc(p2_sum, 1)
                    dve.wait_ge(p2_sum, m + 1)
                    V.reciprocal(share2[:, :], total2[:, :]).then_inc(p2_share, 1)
                    dve.wait_ge(p2_share, m + 1)
                    V.tensor_tensor(by_slot(scores2[:, :]), by_slot(scores2[:, :]),
                                    share2[:, :].unsqueeze(2).broadcast_to((P, QUADS, DEG)), ALU.mult
                                    ).then_inc(p2_norm, 1)
                if s.has_iteration(L_POOL):
                    m = s.iteration(L_POOL)
                    dve.wait_ge(pool_ps, m + 1)
                    V.tensor_tensor(pool_part[:, :].rearrange("p (t d) -> p t d", d=D),
                                    ps[:, B_POOL, :].rearrange("p (t d) -> p t d", d=D),
                                    tile_of[:, :].unsqueeze(2).broadcast_to((P, OCT, D)), ALU.mult
                                    ).then_inc(pool_own, 1)
                    dve.wait_ge(pool_own, m + 1)
                    wait(dve, fin_ps, m * 6 - 5 if s.looped or m > 0 else 0)
                    V.tensor_reduce(pooled[:, :], pool_part[:, :].rearrange("p (t d) -> p d t", d=D), AX_X, ALU.add
                                    ).then_inc(pooled_ok, 1)
                if s.has(0):
                    if s.looped or 1 <= s.at <= OCTETS - RING:
                        dve.wait_ge(g_in[s.slot(1, RING)], s.round(1) * (16 * OCT) + 16 * OCT)
                        V.tensor_copy(idx[:, s.slot(1, RING), :], idx_all[:, bass.ds(s.octet(1 - RING) * OCT, OCT)]
                                      ).then_inc(idx_ready, 1)

                if s.has_batch(L_MASK):
                    n = s.batch(L_MASK)
                    V.tensor_tensor(
                        empty[:, :].rearrange("p (h t j) -> p h t j", h=2, j=DEG),
                        iota_j[:, :].unsqueeze(1).unsqueeze(1).broadcast_to((P, 2, OCT, DEG)),
                        count_slot[:, bass.ds(n * 16, 16)].rearrange("p (t h) -> p h t", h=2).unsqueeze(3).broadcast_to(
                            (P, 2, OCT, DEG)), ALU.is_ge).then_inc(mask_ok, 1)

            def to_diagonal(s, pr, first, last):
                for q in range(first, last):
                    lo = DEG * q
                    V.transpose(probs_diag[lo:lo + DEG, s.slot(L_NORM, 4) // 2, :, lo:lo + DEG],
                                pr[lo:lo + DEG, :].rearrange("p (t j) -> p t j", j=DEG)).then_inc(p_diag, 1)

            def out_rows(s):
                m = s.iteration(L_OUT)
                if s.has_iteration(L_WEIGHTS):
                    dve.wait_ge(seedT_ps, s.iteration(L_WEIGHTS) + 1)
                dve.wait_ge(fin_ps, m * 6 + 5)
                V.scalar_tensor_tensor(dec[:, :], ps_fin[0:D, :], c_("bff3"), hid2[:, :], ALU.add, ALU.max
                                       ).then_inc(dec_ok, 1)
                dve.wait_ge(dec_ok, m + 1)
                V.tensor_scalar(decr[:, :], dec[:, :], 0.0, FLT_MAX, ALU.max, ALU.min).then_inc(decr_ok, 1)

            def y_rows(s):
                if s.at == L_Y:
                    dve.wait_ge(rows_in, ROWS_LOADED)
                m = s.iteration(L_Y)
                dve.wait_ge(fin_ps, m * 6 + 6)
                row = rows[:, bass.ds(m, 1), :].rearrange("p m d -> p (m d)")
                V.scalar_tensor_tensor(row, ps_fin[:, 0:D], nonempty[:, bass.ds(m, 1)], row, ALU.mult, ALU.add
                                       ).then_inc(y_ok, 1)
                dve.wait_ge(y_ok, m + 1)
                V.bn_stats(stats[:, bass.ds(m, 1), :].rearrange("p m n -> p (m n)"), row).then_inc(stats_ok, 1)

            def moments(lo, hi, before):
                dve.wait_ge(stats_ok, hi)
                mean, half, var = (lnv[:, i, lo:hi] for i in range(3))
                done = 5 * before
                V.tensor_tensor(mean, stats[:, lo:hi, 1], stats[:, lo:hi, 4], ALU.add).then_inc(ln_ok, 1)
                V.tensor_tensor(half, stats[:, lo:hi, 1], stats[:, lo:hi, 4], ALU.subtract).then_inc(ln_ok, 1)
                V.tensor_tensor(var, stats[:, lo:hi, 2], stats[:, lo:hi, 5], ALU.add).then_inc(ln_ok, 1)
                dve.wait_ge(ln_ok, done + 3)
                V.scalar_tensor_tensor(half, half, D / 4.0, half, ALU.mult, ALU.mult).then_inc(ln_ok, 1)
                V.tensor_scalar(mean, mean, 0.5, None, ALU.mult)
                dve.wait_ge(ln_ok, done + 4)
                link(V.tensor_tensor(var, var, half, ALU.add))
                V.tensor_scalar(var, var, 1.0 / D, None, ALU.mult).then_inc(ln_ok, 1)

            def by_row(part, i):
                lo, hi = PARTS[part]
                return lnv[:, i, lo:hi].unsqueeze(2).broadcast_to((P, hi - lo, D))

            def norm_shift(part):
                lo, hi = PARTS[part]
                if lo in (0, EARLY):
                    first, last = (0, EARLY) if lo == 0 else (EARLY, ITS)
                    dve.wait_ge(ln_std, 1 if lo == 0 else 2)
                    V.reciprocal(lnv[:, 4, first:last], lnv[:, 3, first:last]).then_inc(ln_inv, 1)
                V.tensor_tensor(rows[:, lo:hi, :], rows[:, lo:hi, :], by_row(part, 0), ALU.subtract
                                ).then_inc(ln_shifted, 1)

            def norm_scale(part):
                lo, hi = PARTS[part]
                dve.wait_ge(ln_inv, 1 if lo < EARLY else 2)
                dve.wait_ge(ln_shifted, part + 1)
                V.tensor_tensor(rows[:, lo:hi, :], rows[:, lo:hi, :], by_row(part, 4), ALU.mult).then_inc(normed, 1)

            steps(dve, step)

            moments(EARLY, ITS, 1)
            norm_shift(NORM_PARTS)
            norm_scale(NORM_PARTS)


_OUT = (12500, 64)


def kernel(**inputs):
    import numpy as np
    import concourse.bacc as bacc
    from concourse.bass_utils import run_bass_kernel_spmd

    nc = bacc.Bacc("TRN2", target_bir_lowering=False, num_devices=1)
    arrays, args = {}, {}
    for name, value in inputs.items():
        arr = np.ascontiguousarray(value)
        arrays[f"in_{name}"] = arr
        args[name] = nc.dram_tensor(f"in_{name}", arr.shape, mybir.dt.from_np(arr.dtype), kind="ExternalInput").ap()
    out = nc.dram_tensor("out_rows", _OUT, F32, kind="ExternalOutput").ap()
    gnn_kernel(nc, args, out)
    r = run_bass_kernel_spmd(nc, [arrays], core_ids=[0])
    return r.results[0]["out_rows"]
```
